# Optimizing a Trainium2 kernel written in Bass

```python
import numpy as np
import jax
import jax.numpy as jnp

def _softmax(x, axis=-1):
    return jax.nn.softmax(x, axis=axis)

def _gelu(x):
    return jax.nn.gelu(x, approximate=True)

def _silu(x):
    return jax.nn.silu(x)

def _sigmoid(x):
    return jax.nn.sigmoid(x)

def _layernorm(x, axis=-1, eps=1e-05):
    m = jnp.mean(x, axis=axis, keepdims=True)
    v = jnp.var(x, axis=axis, keepdims=True)
    return (x - m) / jnp.sqrt(v + eps)

def _scatter_add(tgt, idx, src, axis=0):
    return tgt.at[idx].add(src)

def _segment_sum(src, seg, n):
    return jax.ops.segment_sum(src, seg, n)
kernel_name = 'mk_decoder_postln_d1_seqx_r2_8006dd'

def setup_inputs(seed: int=0):
    np.random.seed(seed)
    _w = jnp.asarray

    def _rec_inputs():
        import jax
        import jax.numpy as jnp
        _rk = jax.random.key(seed)
        x = 7.22e-05 + 1 * jax.random.normal(jax.random.fold_in(_rk, 1), (8, 100, 1024), jnp.float32)
        _lenS = 100 - jax.random.randint(jax.random.fold_in(_rk, 7), (8,), 0, max(1, 100 // 4) + 1, jnp.int32)
        _lenS2 = 722 - jax.random.randint(jax.random.fold_in(_rk, 8), (8,), 0, max(1, 722 // 4) + 1, jnp.int32)
        _ctx_2048P = jax.random.normal(jax.random.fold_in(_rk, 11), (8, 16, 1024), jnp.float32)
        _ctx_2048c = jax.random.dirichlet(jax.random.fold_in(_rk, 511), 0.3 * jnp.ones((16,), jnp.float32), (8, 722))
        _ctx_2048t = jnp.einsum('bsk,bkd->bsd', _ctx_2048c, _ctx_2048P)
        _ctx_2048t = _ctx_2048t * jax.lax.rsqrt(jnp.mean(jnp.square(_ctx_2048t)) + 1e-12) * 0.953939
        ctx_2048 = -0.000514642 + 1.00011 * (_ctx_2048t + 0.3 * jax.random.normal(jax.random.fold_in(_rk, 611), (8, 722, 1024), jnp.float32))
        return (x, ctx_2048)
    x, ctx_2048 = _rec_inputs()

    def _L0_attn_setup():
        import jax, jax.numpy as jnp
        import numpy as np
        H = 8
        DK = 128
        DV = 256
        EPS = 1e-05
        ROPE_BASE = 10000.0

        def _rope(x):
            B, T, h, d = x.shape
            inv_freq = 1.0 / ROPE_BASE ** (jnp.arange(0, d, 2, dtype=jnp.float32) / d)
            t = jnp.arange(T, dtype=jnp.float32)
            freqs = t[:, None] * inv_freq[None, :]
            cos = jnp.cos(freqs)[None, :, None, :]
            sin = jnp.sin(freqs)[None, :, None, :]
            x1, x2 = (x[..., :d // 2], x[..., d // 2:])
            return jnp.concatenate([x1 * cos - x2 * sin, x2 * cos + x1 * sin], axis=-1)
        key = jax.random.key(seed)
        ks = jax.random.split(key, 7)
        hidden = 1024
        B, T = (2, 1024)
        w = 0.02
        return {'hidden_states': jax.random.normal(ks[0], (B, T, hidden), jnp.float32), 'Wq': jax.random.normal(ks[1], (hidden, H * DK), jnp.float32) * w, 'Wk': jax.random.normal(ks[2], (hidden, H * DK), jnp.float32) * w, 'Wv': jax.random.normal(ks[3], (hidden, H * DV), jnp.float32) * w, 'Wg': jax.random.normal(ks[4], (hidden, H * DV), jnp.float32) * w, 'Wo': jax.random.normal(ks[5], (H * DV, hidden), jnp.float32) * w, 'g_norm_weight': jnp.ones((DV,), jnp.float32)}
    _L0_attn_all = _L0_attn_setup()
    _L0_attn_in = {k: v for k, v in _L0_attn_all.items() if k in ('Wq', 'Wk', 'Wv', 'Wg', 'Wo', 'g_norm_weight')}
    del _L0_attn_all

    def _L0_xattn_setup():
        import jax, jax.numpy as jnp
        import numpy as np
        HIDDEN = 1024
        NUM_HEADS = 16
        NUM_KV_HEADS = 4
        HEAD_DIM = 128
        ROPE_THETA = 10000.0
        EPS = 1e-06

        def rms_norm(x, w, eps=EPS):
            var = jnp.mean(jnp.square(x), axis=-1, keepdims=True)
            return x * jax.lax.rsqrt(var + eps) * w

        def rope_cache(L, head_dim, theta, dtype):
            inv_freq = 1.0 / theta ** (jnp.arange(0, head_dim, 2, dtype=jnp.float32) / head_dim)
            t = jnp.arange(L, dtype=jnp.float32)
            freqs = jnp.outer(t, inv_freq)
            emb = jnp.concatenate([freqs, freqs], -1)
            cos = jnp.cos(emb).astype(dtype)[None, :, None, :]
            sin = jnp.sin(emb).astype(dtype)[None, :, None, :]
            return (cos, sin)

        def rotate_half(x):
            x1, x2 = jnp.split(x, 2, axis=-1)
            return jnp.concatenate([-x2, x1], axis=-1)
        key = jax.random.key(seed)
        ks = jax.random.split(key, 10)
        B, L, T = (2, 1024, 256)
        q_out = NUM_HEADS * HEAD_DIM
        kv_out = NUM_KV_HEADS * HEAD_DIM
        s = lambda fan_in: 1.0 / np.sqrt(fan_in)
        return {'x': jax.random.normal(ks[0], (B, L, HIDDEN), jnp.float32), 'h_ctx_kv': jax.random.normal(ks[1], (B, T, HIDDEN), jnp.float32), 'wq': jax.random.normal(ks[2], (HIDDEN, q_out), jnp.float32) * s(HIDDEN), 'wk': jax.random.normal(ks[3], (HIDDEN, kv_out), jnp.float32) * s(HIDDEN), 'wv': jax.random.normal(ks[4], (HIDDEN, kv_out), jnp.float32) * s(HIDDEN), 'wo': jax.random.normal(ks[5], (q_out, HIDDEN), jnp.float32) * s(q_out), 'wk_ctx': jax.random.normal(ks[6], (HIDDEN, kv_out), jnp.float32) * s(HIDDEN), 'wv_ctx': jax.random.normal(ks[7], (HIDDEN, kv_out), jnp.float32) * s(HIDDEN), 'q_norm_w': jnp.ones((HEAD_DIM,), jnp.float32), 'k_norm_w': jnp.ones((HEAD_DIM,), jnp.float32)}
    _L0_xattn_all = _L0_xattn_setup()
    _L0_xattn_in = {k: v for k, v in _L0_xattn_all.items() if k in ('wq', 'wk', 'wv', 'wo', 'wk_ctx', 'wv_ctx', 'q_norm_w', 'k_norm_w')}
    del _L0_xattn_all

    def _L0_ffn_setup():
        import jax, jax.numpy as jnp
        import numpy as np
        DIM_IN = 1024
        DIM_HIDDEN = 4096
        key = jax.random.key(seed)
        k_x, k_g, k_u, k_d = jax.random.split(key, 4)
        s_in = 1.0 / np.sqrt(DIM_IN)
        s_hid = 1.0 / np.sqrt(DIM_HIDDEN)
        x = jax.random.normal(k_x, (4, 1024, DIM_IN), dtype=jnp.float32)
        w_gate = jax.random.uniform(k_g, (DIM_HIDDEN, DIM_IN), jnp.float32, -s_in, s_in)
        w_up = jax.random.uniform(k_u, (DIM_HIDDEN, DIM_IN), jnp.float32, -s_in, s_in)
        w_down = jax.random.uniform(k_d, (DIM_IN, DIM_HIDDEN), jnp.float32, -s_hid, s_hid)
        return {'x': x, 'w_gate': w_gate, 'w_up': w_up, 'w_down': w_down}
    _L0_ffn_all = _L0_ffn_setup()
    _L0_ffn_in = {k: v for k, v in _L0_ffn_all.items() if k in ('w_gate', 'w_up', 'w_down')}
    del _L0_ffn_all
    return {'x': x, 'ctx_2048': ctx_2048, 'L0_attn_Wq': _L0_attn_in['Wq'], 'L0_attn_Wk': _L0_attn_in['Wk'], 'L0_attn_Wv': _L0_attn_in['Wv'], 'L0_attn_Wg': _L0_attn_in['Wg'], 'L0_attn_Wo': _L0_attn_in['Wo'], 'L0_attn_g_norm_weight': _L0_attn_in['g_norm_weight'], 'L0_xattn_wq': _L0_xattn_in['wq'], 'L0_xattn_wk': _L0_xattn_in['wk'], 'L0_xattn_wv': _L0_xattn_in['wv'], 'L0_xattn_wo': _L0_xattn_in['wo'], 'L0_xattn_wk_ctx': _L0_xattn_in['wk_ctx'], 'L0_xattn_wv_ctx': _L0_xattn_in['wv_ctx'], 'L0_xattn_q_norm_w': _L0_xattn_in['q_norm_w'], 'L0_xattn_k_norm_w': _L0_xattn_in['k_norm_w'], 'L0_ffn_w_gate': _L0_ffn_in['w_gate'], 'L0_ffn_w_up': _L0_ffn_in['w_up'], 'L0_ffn_w_down': _L0_ffn_in['w_down']}

def reference(x, ctx_2048, L0_attn_Wq, L0_attn_Wk, L0_attn_Wv, L0_attn_Wg, L0_attn_Wo, L0_attn_g_norm_weight, L0_xattn_wq, L0_xattn_wk, L0_xattn_wv, L0_xattn_wo, L0_xattn_wk_ctx, L0_xattn_wv_ctx, L0_xattn_q_norm_w, L0_xattn_k_norm_w, L0_ffn_w_gate, L0_ffn_w_up, L0_ffn_w_down):
    import jax
    import jax.numpy as jnp

    def _L0_attn_ref(hidden_states, Wq, Wk, Wv, Wg, Wo, g_norm_weight):
        import jax, jax.numpy as jnp
        import numpy as np
        H = 8
        DK = 128
        DV = 256
        EPS = 1e-05
        ROPE_BASE = 10000.0

        def _rope(x):
            B, T, h, d = x.shape
            inv_freq = 1.0 / ROPE_BASE ** (jnp.arange(0, d, 2, dtype=jnp.float32) / d)
            t = jnp.arange(T, dtype=jnp.float32)
            freqs = t[:, None] * inv_freq[None, :]
            cos = jnp.cos(freqs)[None, :, None, :]
            sin = jnp.sin(freqs)[None, :, None, :]
            x1, x2 = (x[..., :d // 2], x[..., d // 2:])
            return jnp.concatenate([x1 * cos - x2 * sin, x2 * cos + x1 * sin], axis=-1)
        B, T, _ = hidden_states.shape
        q = (hidden_states @ Wq).reshape(B, T, H, DK)
        k = (hidden_states @ Wk).reshape(B, T, H, DK)
        v = (hidden_states @ Wv).reshape(B, T, H, DV)
        g = (hidden_states @ Wg).reshape(B, T, H, DV)
        q = _rope(q)
        k = _rope(k)
        gamma = 1.0 - jnp.exp2(-5.0 - jnp.arange(H, dtype=jnp.float32))
        idx = jnp.arange(T)
        diff = idx[:, None] - idx[None, :]
        causal = diff >= 0
        log2g = jnp.log2(gamma)[:, None, None]
        D = jnp.where(causal[None], jnp.exp2(log2g * jnp.where(causal, diff, 0)[None]), 0.0)
        scale = DK ** (-0.5)
        scores = jnp.einsum('bihd,bjhd->bhij', q * scale, k) * D[None]
        o = jnp.einsum('bhij,bjhd->bihd', scores, v)
        rms = jax.lax.rsqrt(jnp.mean(o * o, axis=-1, keepdims=True) + EPS)
        o = o * rms * g_norm_weight
        o = o * (g * jax.nn.sigmoid(g))
        return o.reshape(B, T, H * DV) @ Wo

    def _L0_xattn_ref(x, h_ctx_kv, wq, wk, wv, wo, wk_ctx, wv_ctx, q_norm_w, k_norm_w):
        import jax, jax.numpy as jnp
        import numpy as np
        HIDDEN = 1024
        NUM_HEADS = 16
        NUM_KV_HEADS = 4
        HEAD_DIM = 128
        ROPE_THETA = 10000.0
        EPS = 1e-06

        def rms_norm(x, w, eps=EPS):
            var = jnp.mean(jnp.square(x), axis=-1, keepdims=True)
            return x * jax.lax.rsqrt(var + eps) * w

        def rope_cache(L, head_dim, theta, dtype):
            inv_freq = 1.0 / theta ** (jnp.arange(0, head_dim, 2, dtype=jnp.float32) / head_dim)
            t = jnp.arange(L, dtype=jnp.float32)
            freqs = jnp.outer(t, inv_freq)
            emb = jnp.concatenate([freqs, freqs], -1)
            cos = jnp.cos(emb).astype(dtype)[None, :, None, :]
            sin = jnp.sin(emb).astype(dtype)[None, :, None, :]
            return (cos, sin)

        def rotate_half(x):
            x1, x2 = jnp.split(x, 2, axis=-1)
            return jnp.concatenate([-x2, x1], axis=-1)
        B, L, _ = x.shape
        T = h_ctx_kv.shape[1]
        rep = NUM_HEADS // NUM_KV_HEADS
        q = (x @ wq).reshape(B, L, NUM_HEADS, HEAD_DIM)
        k = (x @ wk).reshape(B, L, NUM_KV_HEADS, HEAD_DIM)
        v = (x @ wv).reshape(B, L, NUM_KV_HEADS, HEAD_DIM)
        q = rms_norm(q, q_norm_w)
        k = rms_norm(k, k_norm_w)
        k_ctx = (h_ctx_kv @ wk_ctx).reshape(B, T, NUM_KV_HEADS, HEAD_DIM)
        v_ctx = (h_ctx_kv @ wv_ctx).reshape(B, T, NUM_KV_HEADS, HEAD_DIM)
        k_ctx = rms_norm(k_ctx, k_norm_w)
        cos, sin = rope_cache(L, HEAD_DIM, ROPE_THETA, x.dtype)
        q = q * cos + rotate_half(q) * sin
        k = k * cos + rotate_half(k) * sin
        k_full = jnp.concatenate([k_ctx, k], axis=1)
        v_full = jnp.concatenate([v_ctx, v], axis=1)
        k_full = jnp.repeat(k_full, rep, axis=2)
        v_full = jnpp_repeat = jnp.repeat(v_full, rep, axis=2)
        i = jnp.arange(L)[:, None]
        j = jnp.arange(L)[None, :]
        causal = jnp.where(j > i, -jnp.inf, 0.0).astype(x.dtype)
        mask = jnp.concatenate([jnp.zeros((L, T), x.dtype), causal], axis=1)
        scale = 1.0 / np.sqrt(HEAD_DIM)
        scores = jnp.einsum('blhd,bmhd->bhlm', q, k_full) * scale + mask
        probs = jax.nn.softmax(scores, axis=-1)
        out = jnp.einsum('bhlm,bmhd->blhd', probs, v_full)
        out = out.reshape(B, L, NUM_HEADS * HEAD_DIM)
        return out @ wo

    def _L0_ffn_ref(x, w_gate, w_up, w_down):
        import jax, jax.numpy as jnp
        import numpy as np
        DIM_IN = 1024
        DIM_HIDDEN = 4096
        gate = jnp.einsum('bsd,hd->bsh', x, w_gate)
        up = jnp.einsum('bsd,hd->bsh', x, w_up)
        gated = jax.nn.silu(gate) * up
        return jnp.einsum('bsh,dh->bsd', gated, w_down)
    x = _layernorm(x + _L0_attn_ref(x, L0_attn_Wq, L0_attn_Wk, L0_attn_Wv, L0_attn_Wg, L0_attn_Wo, L0_attn_g_norm_weight), axis=-1)
    x = _layernorm(x + _L0_xattn_ref(x, ctx_2048, L0_xattn_wq, L0_xattn_wk, L0_xattn_wv, L0_xattn_wo, L0_xattn_wk_ctx, L0_xattn_wv_ctx, L0_xattn_q_norm_w, L0_xattn_k_norm_w), axis=-1)
    x = _layernorm(x + _L0_ffn_ref(x, L0_ffn_w_gate, L0_ffn_w_up, L0_ffn_w_down), axis=-1)
    return x

_drawn_inputs = setup_inputs


def setup_inputs(seed=0):
    import zlib

    import numpy as np

    out = dict(_drawn_inputs(seed))
    spreads = {'L0_attn_g_norm_weight': (1.0, 0.2),
     'L0_xattn_q_norm_w': (1.0, 0.2),
     'L0_xattn_k_norm_w': (1.0, 0.2)}
    factors = {}
    for name, (base, spread) in spreads.items():
        noise = np.random.default_rng([zlib.crc32(name.encode()), seed]).standard_normal(out[name].shape)
        drawn = base * np.exp(spread * noise) if base else spread * noise
        out[name] = jnp.asarray(drawn.astype(out[name].dtype))
    for name, factor in factors.items():
        out[name] = (out[name] * factor).astype(out[name].dtype)
    return out
```

```python
from contextlib import ExitStack

import numpy as np

import concourse.bass as bass
from concourse import mybir

F32 = mybir.dt.float32
F32R = mybir.dt.float32r
ALU = mybir.AluOpType
ACT = mybir.ActivationFunctionType
AX = mybir.AxisListType
ds = bass.ds

P = 128
B, T, D = 8, 100, 1024
NT = B * T
HALF = NT // 2
KT = D // P
RH, RDV = 8, 256
QH_N, KV_N, HD = 16, 4, 128
GRP = QH_N // KV_N
CTX = 722
KEYS = CTX + T
CA = 384
CB = CTX - CA
FF = 4096
CHUNKS = FF // D
UNIT = KT * P
KEY_A = 412
KEY_B = KEYS - KEY_A
KC = -(-KEYS // P)
LASTC = KEYS - (KC - 1) * P
SELF_C = CTX // P
SELF_P = CTX % P

U_CTX, U_RET = 0, 8
U_QK = U_RET + 8 * RH
U_V = U_QK + QH_N + KV_N
U_WO = U_V + 4
U_FFN = U_WO + 16
U_END = U_FFN + 24 * CHUNKS
PAIRS = U_END // 2


class Core:
    pass


def weight_stream(c, sp, first_pair, n):
    with sp.Fori(0, n) as i:
        for s in range(2):
            sp.wait_ge(c.w_lo, 4 * i + (2 * (first_pair + s) - 2))
            sp.dma_start(c.RAW[:, s, :], c.weights[ds(2 * i + (first_pair + s), 1)]
                         .rearrange("a p w -> (a p) w")).then_inc(c.raw[s], 16)


def raw_unit(c, u):
    return c.RAW[:, (u // 2) % 2, (u % 2) * UNIT:(u % 2 + 1) * UNIT]


def split_hi(c, act, u, loop=0, per4=0):
    act.wait_ge(c.raw[(u // 2) % 2], 16 * per4 * loop + 16 * (u // 4 + 1))
    if u >= U_RET + 2:
        act.wait_ge(c.unit_done, 4 * per4 * loop + (u - U_RET - 1))
    act.activation(c.WH[:, u % 2, :], raw_unit(c, u), ACT.Copy).then_inc(c.w_hi, 1)


def split_lo(c, dve, u, loop=0, per4=0):
    dve.wait_ge(c.w_hi, 4 * per4 * loop + (u + 1))
    dve.tensor_tensor(c.WL[:, u % 2, :], raw_unit(c, u), c.WH[:, u % 2, :].bitcast(F32),
                      ALU.subtract).then_inc(c.w_lo, 1)


def halves(ap):
    return ap.rearrange("p (h t) -> p h t", h=2)


def banks2(c, bank, p0=0, p1=P):
    return c.PS[p0:p1, bank:bank + 2, 0:HALF]


def unit_matmuls(c, pe, slot, bank, xh, xl, before_k=None):
    for h in range(2):
        cols = slice(h * HALF, (h + 1) * HALF)
        for k in range(KT):
            if before_k is not None and h == 0:
                before_k(k)
            wh = c.WH[:, slot, k * P:(k + 1) * P]
            wl = c.WL[:, slot, k * P:(k + 1) * P]
            out = c.PS[:, bank + h, 0:HALF]
            pe.matmul(out, wh, xh[:, k, cols], start=(k == 0), stop=False)
            pe.matmul(out, wh, xl[:, k, cols], start=False, stop=False)
            mm = pe.matmul(out, wl, xh[:, k, cols], start=False, stop=(k == KT - 1))
    mm.then_inc(c.unit_done, 1)


def value_matmuls(c, pe, sweep, bank):
    wh = c.WH[:, sweep, :].rearrange("p (k n) -> p k n", n=256)
    wl = c.WL[:, sweep, :].rearrange("p (k n) -> p k n", n=256)
    for b in range(B):
        out = c.PS[0:T, bank + b // 2, (b % 2) * 256:(b % 2 + 1) * 256]
        for k in range(4):
            xh = c.XH[:, 4 * sweep + k, b * T:(b + 1) * T]
            xl = c.XL[:, 4 * sweep + k, b * T:(b + 1) * T]
            first = sweep == 0 and k == 0 and b % 2 == 0
            pe.matmul(out, xh, wh[:, k, :], start=first, stop=False, skip_group_check=True)
            pe.matmul(out, xl, wh[:, k, :], start=False, stop=False, skip_group_check=True)
            mm = pe.matmul(out, xh, wl[:, k, :], start=False, stop=(sweep == 1 and k == 3),
                           skip_group_check=True)
    mm.then_inc(c.unit_done, 1)


def rsqrt_from(c, act, out, stat, eps, ln_done, ln_count):
    act.activation(out, stat, ACT.Ln, bias=eps, scale=1.0).then_inc(ln_done, 1)
    act.wait_ge(ln_done, ln_count)
    return act.activation(out, out, ACT.Exp, scale=-0.5)


def phase_constants(c, nc):
    with nc.Block() as block:
        @block.sync
        def _(sp):
            for s in range(2):
                sp.dma_start(c.RAW[:, s, :], c.weights[s]).then_inc(c.raw[s], 16)
            for tile, src in ((c.COS, c.cos), (c.SIN, c.sin), (c.ID, c.ident),
                              (c.CMASK, c.cmask), (c.NW, c.nw)):
                sp.dma_start(tile[:], src).then_inc(c.const_in, 16)
            sp.wait_ge(c.const_in, 80)

        @block.gpsimd
        def _(pool):
            pool.memset(c.ONES[:], 1.0)
            pool.memset(c.ONES_D[:], 1.0 / D)
            pool.memset(c.ONES_DV[:], 1.0 / RDV)
            pool.memset(c.ONES_HD[:], 1.0 / HD)
            pool.memset(c.EPS5[:], 1e-5)
            pool.memset(c.EPS6[:], 1e-6)


def phase_context(c, nc):
    with ExitStack() as ctx:
        sb = lambda name, shape, dt=F32: ctx.enter_context(nc.sbuf_tensor(name, shape, dt))
        sem = lambda name: ctx.enter_context(nc.semaphore(name))
        CWH = sb("CWH", [P, 8, UNIT], F32R)
        CWL = sb("CWL", [P, 8, UNIT], F32R)
        CR = sb("CR", [P, KT, CA])
        CH = sb("CH", [P, 2, KT, CA], F32R)
        CL = sb("CL", [P, 2, KT, CA], F32R)
        SQ = sb("CSQ", [P, KV_N, CA])
        RS = sb("CRS", [P, 2, CA])
        KS = sb("KS", [P, 2, KV_N, CA])
        VS = sb("VS", [P, 3, KV_N * HD])
        chunk_in, chunk_hi, chunk_lo = sem("chunk_in"), sem("chunk_hi"), sem("chunk_lo")
        k_raw, k_sq, k_var, k_ln, k_rs, k_out = (sem(n) for n in (
            "k_raw", "k_sq", "k_var", "k_ln", "k_rs", "k_out"))
        v_raw, v_out, v_stored = sem("v_raw"), sem("v_out"), sem("v_stored")
        k_stored = [sem("k_stored0"), sem("k_stored1")]
        width, offset = (CA, CB), (0, CA)
        vwh = CWH[:, 4:8, :].rearrange("p u w -> p (u w)").rearrange("p (k n) -> p k n", n=512)
        vwl = CWL[:, 4:8, :].rearrange("p u w -> p (u w)").rearrange("p (k n) -> p k n", n=512)

        with nc.Block() as block:
            @block.gpsimd
            def _(pool):
                pool.sem_inc(k_out, 4)
                pool.sem_inc(k_ln, 2)
                pool.sem_inc(v_out, 2)
                pool.sem_inc(chunk_lo, 1)
                pool.sem_inc(k_stored[0], 16)
                pool.sem_inc(k_stored[1], 16)

            @block.sync
            def _(sp):
                def load(b, e):
                    sp.wait_ge(chunk_lo, 2 * b + e + 1)
                    w = width[e]
                    sp.dma_start(CR[:, :, 0:w], c.context[ds(b, 1), :, :, offset[e]:offset[e] + w]
                                 .rearrange("a p k t -> (a p) k t")).then_inc(chunk_in, 16)

                def store(b, e):
                    w = width[e]
                    sp.wait_ge(k_out, 4 * (2 * b + e) + 4 + 4)
                    dst = c.kscr[ds(b, 1), :, :, offset[e]:offset[e] + w]
                    sp.dma_start(dst.rearrange("a v p t -> p (a v) t"),
                                 KS[:, e, :, 0:w]).then_inc(k_stored[e], 16)
                    sp.wait_ge(v_out, 6 * b + 3 * e + 3 + 2)
                    for t in range(3):
                        rows = min(P, w - t * P)
                        dst = c.vscr[ds(b, 1), :, 0:rows, 3 * e + t, :]
                        sp.dma_start(dst.rearrange("a v p d -> p (a v) d"),
                                     VS[0:rows, t, :].rearrange("p (v d) -> p v d", v=KV_N)
                                     ).then_inc(v_stored, 16)

                load(0, 0)
                for s in range(2):
                    sp.wait_ge(c.w_lo, 2 * (2 + s) - 2)
                    sp.dma_start(c.RAW[:, s, :], c.weights[2 + s]).then_inc(c.raw[s], 16)
                load(0, 1)
                for s in range(2):
                    sp.wait_ge(c.w_lo, 2 * (4 + s) - 2)
                    sp.dma_start(c.RAW[:, s, :], c.weights[4 + s]).then_inc(c.raw[s], 16)
                with sp.Fori(0, B - 1) as b:
                    load(b + 1, 0)
                    store(b, 0)
                    load(b + 1, 1)
                    store(b, 1)
                store(B - 1, 0)
                store(B - 1, 1)
                sp.wait_ge(k_stored[0], 16 * B + 16)
                sp.wait_ge(k_stored[1], 16 * B + 16)
                sp.wait_ge(v_stored, 16 * 6 * B)

            @block.scalar
            def _(act):
                def resident_hi(u):
                    act.wait_ge(c.raw[(u // 2) % 2], 16 * (u // 4 + 1))
                    act.activation(CWH[:, u, :], raw_unit(c, u), ACT.Copy).then_inc(c.w_hi, 1)

                def chunk_split(b, e):
                    w = width[e]
                    act.wait_ge(chunk_in, 32 * b + 16 * (e + 1))
                    act.activation(CH[:, e, :, 0:w], CR[:, :, 0:w], ACT.Copy).then_inc(chunk_hi, 1)

                def body(b, last):
                    for e in range(2):
                        w, n0 = width[e], 4 * e
                        for h in range(KV_N):
                            act.wait_ge(k_raw, 8 * b + (n0 + h + 1))
                            act.activation(SQ[:, h, 0:w], c.PS[:, h, 0:w],
                                           ACT.Square).then_inc(k_sq, 1)
                        if e == 0:
                            chunk_split(b, 1)
                        elif not last:
                            chunk_split(b + 1, 0)
                        for h in range(KV_N):
                            act.wait_ge(k_var, 8 * b + (n0 + h + 1))
                            act.wait_ge(k_out, 8 * b + (n0 + h + 3))
                            rsqrt_from(c, act, RS[:, h % 2, 0:w], c.PS[:, 6 + h % 2, 0:w],
                                       c.EPS6[:], k_ln, 8 * b + (n0 + h + 3)).then_inc(k_rs, 1)

                act.preload_act_table_set("natural_log_exp_and_others")
                for u in range(2):
                    resident_hi(u)
                chunk_split(0, 0)
                for u in range(2, 8):
                    resident_hi(u)
                split_hi(c, act, 8)
                split_hi(c, act, 9)
                with act.Fori(0, B - 1) as b:
                    body(b, False)
                body(B - 1, True)

            @block.vector
            def _(dve):
                def resident_lo(u):
                    dve.wait_ge(c.w_hi, u + 1)
                    dve.tensor_tensor(CWL[:, u, :], raw_unit(c, u), CWH[:, u, :].bitcast(F32),
                                      ALU.subtract).then_inc(c.w_lo, 1)

                def chunk_split(b, e):
                    w = width[e]
                    dve.wait_ge(chunk_hi, 2 * b + (e + 1))
                    dve.tensor_tensor(CL[:, e, :, 0:w], CR[:, :, 0:w],
                                      CH[:, e, :, 0:w].bitcast(F32),
                                      ALU.subtract).then_inc(chunk_lo, 1)

                def body(b, last):
                    for e in range(2):
                        w = width[e]
                        if e == 0:
                            chunk_split(b, 1)
                        elif not last:
                            chunk_split(b + 1, 0)

                        def value_out(t):
                            rows = min(P, w - t * P)
                            n = 3 * e + t
                            dve.wait_ge(v_raw, 6 * b + (n + 1))
                            if t == 0 and not (e == 0 and isinstance(b, int) and b == 0):
                                dve.wait_ge(v_stored, 96 * b + 48 * e)
                            dve.tensor_copy(VS[0:rows, t, :],
                                            c.PS[0:rows, 4 + n % 2, :]).then_inc(v_out, 1)

                        def key_out(h):
                            dve.wait_ge(k_rs, 8 * b + (4 * e + h + 1))
                            if h == 0:
                                dve.wait_ge(k_stored[e], 16 * b + 16)
                            dve.scalar_tensor_tensor(
                                out=KS[:, e, h, 0:w], in0=c.PS[:, h, 0:w],
                                scalar=c.NW[:, QH_N:QH_N + 1], in1=RS[:, h % 2, 0:w],
                                op0=ALU.mult, op1=ALU.mult).then_inc(k_out, 1)

                        value_out(0)
                        key_out(0)
                        key_out(1)
                        value_out(1)
                        key_out(2)
                        key_out(3)
                        value_out(2)

                for u in range(2):
                    resident_lo(u)
                chunk_split(0, 0)
                for u in range(2, 8):
                    resident_lo(u)
                split_lo(c, dve, 8)
                split_lo(c, dve, 9)
                body(0, False)
                with dve.Fori(1, B - 1) as b:
                    body(b, False)
                body(B - 1, True)

            @block.tensor
            def _(pe):
                def keys(b, e, h):
                    w = width[e]
                    pe.wait_ge(k_out, 8 * b + (4 * e + h + 1))
                    out = c.PS[:, h, 0:w]
                    for k in range(KT):
                        wh, wl = CWH[:, h, k * P:(k + 1) * P], CWL[:, h, k * P:(k + 1) * P]
                        pe.matmul(out, wh, CH[:, e, k, 0:w], start=(k == 0), stop=False)
                        pe.matmul(out, wh, CL[:, e, k, 0:w], start=False, stop=False)
                        mm = pe.matmul(out, wl, CH[:, e, k, 0:w], start=False, stop=(k == KT - 1))
                    mm.then_inc(k_raw, 1)

                def key_variance(b, e, h):
                    pe.wait_ge(k_sq, 8 * b + (4 * e + h + 1))
                    pe.wait_ge(k_ln, 8 * b + (4 * e + h + 1))
                    pe.matmul(c.PS[:, 6 + h % 2, 0:width[e]], c.ONES_HD[:], SQ[:, h, 0:width[e]],
                              start=True, stop=True).then_inc(k_var, 1)

                def values(b, e, t):
                    rows = min(P, width[e] - t * P)
                    n = 3 * e + t
                    pe.wait_ge(v_out, 6 * b + (n + 1))
                    out = c.PS[0:rows, 4 + n % 2, :]
                    for k in range(KT):
                        ch = CH[:, e, k, t * P:t * P + rows]
                        cl = CL[:, e, k, t * P:t * P + rows]
                        pe.matmul(out, ch, vwh[:, k, :], start=(k == 0), stop=False)
                        pe.matmul(out, cl, vwh[:, k, :], start=False, stop=False)
                        mm = pe.matmul(out, ch, vwl[:, k, :], start=False, stop=(k == KT - 1))
                    mm.then_inc(v_raw, 1)

                pe.wait_ge(c.w_lo, 8)
                with pe.Fori(0, B) as b:
                    for e in range(2):
                        pe.wait_ge(chunk_lo, 2 * b + (e + 2))
                        for h in range(KV_N):
                            keys(b, e, h)
                        values(b, e, 0)
                        key_variance(b, e, 0)
                        key_variance(b, e, 1)
                        values(b, e, 1)
                        key_variance(b, e, 2)
                        key_variance(b, e, 3)
                        values(b, e, 2)


def phase_retention(c, nc):
    with ExitStack() as ctx:
        sb = lambda name, shape, dt=F32: ctx.enter_context(nc.sbuf_tensor(name, shape, dt))
        sem = lambda name: ctx.enter_context(nc.semaphore(name))
        DECAY = sb("DECAY", [T, RH, T])
        GNW = sb("GNW", [P, 2])
        T1, T2 = sb("T1", [P, NT]), sb("T2", [P, NT])
        QK = [[sb(f"{n}{part}", [P, NT], F32R) for part in "HL"] for n in "QK"]
        VH, VL = sb("VH", [T, B, RDV], F32R), sb("VL", [T, B, RDV], F32R)
        G = sb("G", [P, 2, NT])
        SM = sb("SM", [T, NT])
        SH, SL = sb("SH", [T, NT], F32R), sb("SL", [T, NT], F32R)
        SQ = sb("SQ", [P, 2, NT])
        RS = sb("RS", [P, NT])
        OR = sb("OR", [P, 2, NT])
        OH, OL = sb("OH", [P, 2, NT], F32R), sb("OL", [P, 2, NT], F32R)
        names = ("x_in", "x_hi", "x_lo", "turned", "roped", "qk_hi", "qk_lo", "v_hi", "v_lo",
                 "s_raw", "s_masked", "s_hi", "s_lo", "gated", "o_raw", "o_sq", "o_var", "o_ln",
                 "o_rs", "o_gated", "o_normed", "o_hi", "o_lo", "wo_raw", "r_added")
        (x_in, x_hi, x_lo, turned, roped, qk_hi, qk_lo, v_hi, v_lo, s_raw, s_masked, s_hi, s_lo,
         gated, o_raw, o_sq, o_var, o_ln, o_rs, o_gated, o_normed, o_hi, o_lo, wo_raw,
         r_added) = (sem("r_" + n) for n in names)
        R, XH, XL = c.R, c.XH, c.XL
        batches = lambda ap: ap.rearrange("p (b t) -> p b t", t=T)
        bank_tokens = lambda p0, p1: c.PS[p0:p1, 0:2, 0:HALF].rearrange(
            "p h (b t) -> p h b t", t=T)

        with nc.Block() as block:
            @block.sync
            def _(sp):
                for k in range(KT):
                    sp.dma_start(R[:, k, :], c.x[:, k, :]).then_inc(x_in, 16)
                sp.dma_start(DECAY[:], c.decay).then_inc(c.const_in, 16)
                sp.dma_start(GNW[:], c.gnw).then_inc(c.const_in, 16)
                weight_stream(c, sp, U_RET // 2 + 2, 2 * RH)

            @block.scalar
            def _(act):
                act.wait_ge(x_in, 16 * KT)
                for k in range(KT):
                    act.activation(XH[:, k, :], R[:, k, :], ACT.Copy).then_inc(x_hi, 1)
                with act.Fori(0, RH) as i:
                    for n in range(2):
                        split_hi(c, act, U_RET + n + 2, i, 2)
                        act.wait_ge(roped, 2 * i + (n + 1))
                        act.activation(QK[n][0][:], T1[:], ACT.Copy).then_inc(qk_hi, 1)
                    split_hi(c, act, U_RET + 4, i, 2)
                    split_hi(c, act, U_RET + 5, i, 2)
                    act.activation(VH[:].rearrange("p (g b) n -> p g (b n)", b=2),
                                   c.PS[0:T, 4:8, :], ACT.Copy).then_inc(v_hi, 1)
                    act.wait_ge(s_masked, i + 1)
                    act.activation(SH[:], SM[:], ACT.Copy).then_inc(s_hi, 1)
                    split_hi(c, act, U_RET + 6, i, 2)
                    act.activation(halves(G[:, 0, :]), banks2(c, 2), ACT.Silu).then_inc(gated, 1)
                    act.wait_ge(o_raw, i + 1)
                    act.activation(SQ[:].rearrange("p t (h n) -> p (t h) n", h=2),
                                   c.PS[:, 4:8, 0:HALF], ACT.Square).then_inc(o_sq, 1)
                    split_hi(c, act, U_RET + 7, i, 2)
                    act.activation(halves(G[:, 1, :]), banks2(c, 0), ACT.Silu).then_inc(gated, 1)
                    act.preload_act_table_set("natural_log_exp_and_others")
                    act.wait_ge(o_var, i + 1)
                    rsqrt_from(c, act, halves(RS[:]), banks2(c, 2), c.EPS5[:], o_ln,
                               i + 1).then_inc(o_rs, 1)
                    for t in range(2):
                        act.wait_ge(o_normed, 2 * i + (t + 1))
                        act.activation(OH[:, t, :], OR[:, t, :], ACT.Copy).then_inc(o_hi, 1)
                    split_hi(c, act, U_RET + 8, i, 2)
                    split_hi(c, act, U_RET + 9, i, 2)

            @block.vector
            def _(dve):
                for k in range(KT):
                    dve.wait_ge(x_hi, k + 1)
                    dve.tensor_tensor(XL[:, k, :], R[:, k, :], XH[:, k, :].bitcast(F32),
                                      ALU.subtract).then_inc(x_lo, 1)
                dve.wait_ge(c.const_in, 112)
                cos = c.COS[:].unsqueeze(1).broadcast_to([P, 4, T])

                def rope(n, i):
                    dve.wait_ge(c.unit_done, 8 * i + (n + 1))
                    for h in range(2):
                        bank = c.PS[:, 2 * n + h, 0:HALF].rearrange("p (b t) -> p b t", t=T)
                        cols = slice(h * HALF, (h + 1) * HALF)
                        t1, t2 = batches(T1[:, cols]), batches(T2[:, cols])
                        dve.tensor_tensor(t1, bank, cos, ALU.mult)
                        for lo in (0, 64):
                            hi = 64 - lo
                            ins = dve.tensor_tensor(
                                t2[lo:lo + 64], bank[hi:hi + 64],
                                c.SIN[lo:lo + 64].unsqueeze(1).broadcast_to([64, 4, T]), ALU.mult)
                    ins.then_inc(turned, 1)
                    dve.wait_ge(turned, 2 * i + (n + 1))
                    dve.tensor_tensor(T1[:], T1[:], T2[:], ALU.add).then_inc(roped, 1)
                    dve.wait_ge(qk_hi, 2 * i + (n + 1))
                    dve.tensor_tensor(QK[n][1][:], T1[:], QK[n][0][:].bitcast(F32),
                                      ALU.subtract).then_inc(qk_lo, 1)
                    dve.wait_ge(qk_lo, 2 * i + (n + 1))

                with dve.Fori(0, RH) as i:
                    for n in range(2):
                        split_lo(c, dve, U_RET + n + 2, i, 2)
                        rope(n, i)
                    split_lo(c, dve, U_RET + 4, i, 2)
                    split_lo(c, dve, U_RET + 5, i, 2)
                    dve.wait_ge(v_hi, i + 1)
                    dve.tensor_tensor(VL[:].rearrange("p (g b) n -> p g (b n)", b=2),
                                      c.PS[0:T, 4:8, :],
                                      VH[:].bitcast(F32).rearrange("p (g b) n -> p g (b n)", b=2),
                                      ALU.subtract).then_inc(v_lo, 1)
                    dve.wait_ge(s_raw, i + 1)
                    for h in range(2):
                        decay = DECAY[:, ds(i, 1), :].broadcast_to([T, 4, T])
                        ins = dve.tensor_tensor(
                            batches(SM[:, h * HALF:(h + 1) * HALF]),
                            c.PS[0:T, h, 0:HALF].rearrange("p (b t) -> p b t", t=T), decay,
                            ALU.mult)
                    ins.then_inc(s_masked, 1)
                    dve.wait_ge(s_hi, i + 1)
                    dve.tensor_tensor(SL[:], SM[:], SH[:].bitcast(F32),
                                      ALU.subtract).then_inc(s_lo, 1)
                    split_lo(c, dve, U_RET + 6, i, 2)
                    split_lo(c, dve, U_RET + 7, i, 2)
                    dve.wait_ge(o_sq, i + 1)
                    dve.wait_ge(gated, 2 * i + 2)
                    dve.tensor_tensor(OR[:].rearrange("p t (h n) -> p (t h) n", h=2),
                                      c.PS[:, 4:8, 0:HALF],
                                      G[:].rearrange("p t (h n) -> p (t h) n", h=2),
                                      ALU.mult).then_inc(o_gated, 1)
                    dve.wait_ge(o_gated, i + 1)
                    dve.wait_ge(o_rs, i + 1)
                    for t in range(2):
                        dve.scalar_tensor_tensor(out=OR[:, t, :], in0=OR[:, t, :],
                                                 scalar=GNW[:, t:t + 1], in1=RS[:], op0=ALU.mult,
                                                 op1=ALU.mult).then_inc(o_normed, 1)
                    for t in range(2):
                        dve.wait_ge(o_hi, 2 * i + (t + 1))
                        dve.tensor_tensor(OL[:, t, :], OR[:, t, :], OH[:, t, :].bitcast(F32),
                                          ALU.subtract).then_inc(o_lo, 1)
                    for n in range(KT):
                        if n % 4 == 3:
                            dve.wait_ge(c.unit_done, 8 * i + (7 + n // 4))
                        else:
                            dve.wait_ge(wo_raw, 6 * i + (n + 1 - n // 4))
                        dve.tensor_tensor(halves(R[:, n, :]), halves(R[:, n, :]),
                                          banks2(c, 2 * (n % 4)), ALU.add).then_inc(r_added, 1)
                        if n % 4 == 3:
                            split_lo(c, dve, U_RET + 8 + n // 4, i, 2)

            @block.tensor
            def _(pe):
                def weights(j, i):
                    pe.wait_ge(c.w_lo, 8 * i + (U_RET + j + 1))

                with pe.Fori(0, RH) as i:
                    weights(0, i)
                    unit_matmuls(c, pe, 0, 0, XH, XL, lambda k: pe.wait_ge(x_lo, k + 1))
                    weights(1, i)
                    unit_matmuls(c, pe, 1, 2, XH, XL)
                    pe.wait_ge(roped, 2 * i + 1)
                    for s in range(2):
                        weights(2 + s, i)
                        value_matmuls(c, pe, s, 4)
                    pe.wait_ge(qk_lo, 2 * i + 2)
                    for b in range(B):
                        out = c.PS[0:T, b // 4, (b % 4) * T:(b % 4 + 1) * T]
                        cols = slice(b * T, (b + 1) * T)
                        (qh, ql), (kh, kl) = QK
                        pe.matmul(out, kh[:, cols], qh[:, cols], start=True, stop=False)
                        pe.matmul(out, kh[:, cols], ql[:, cols], start=False, stop=False)
                        mm = pe.matmul(out, kl[:, cols], qh[:, cols], start=False, stop=True)
                    mm.then_inc(s_raw, 1)
                    weights(4, i)
                    unit_matmuls(c, pe, 0, 2, XH, XL)
                    pe.wait_ge(v_lo, i + 1)
                    pe.wait_ge(s_lo, i + 1)
                    for t in range(2):
                        for b in range(B):
                            out = c.PS[:, 4 + 2 * t + b // 4, (b % 4) * T:(b % 4 + 1) * T]
                            cols = slice(b * T, (b + 1) * T)
                            vh, vl = VH[:, b, t * P:(t + 1) * P], VL[:, b, t * P:(t + 1) * P]
                            pe.matmul(out, vh, SH[:, cols], start=True, stop=False)
                            pe.matmul(out, vh, SL[:, cols], start=False, stop=False)
                            mm = pe.matmul(out, vl, SH[:, cols], start=False, stop=True)
                    mm.then_inc(o_raw, 1)
                    weights(5, i)
                    unit_matmuls(c, pe, 1, 0, XH, XL)
                    pe.wait_ge(o_sq, i + 1)
                    pe.wait_ge(gated, 2 * i + 1)
                    for h in range(2):
                        for t in range(2):
                            mm = pe.matmul(c.PS[:, 2 + h, 0:HALF], c.ONES_DV[:],
                                           SQ[:, t, h * HALF:(h + 1) * HALF], start=(t == 0),
                                           stop=(t == 1))
                    mm.then_inc(o_var, 1)
                    for n in range(KT):
                        if n % 4 == 0:
                            weights(6 + n // 4, i)
                        if n == 0:
                            pe.wait_ge(o_lo, 2 * i + 2)
                            pe.wait_ge(gated, 2 * i + 2)
                        if n == 1:
                            pe.wait_ge(o_rs, i + 1)
                        if n == 2:
                            pe.wait_ge(o_gated, i + 1)
                        if n >= 4:
                            pe.wait_ge(r_added, 8 * i + (n - 3))
                        for h in range(2):
                            cols = slice(h * HALF, (h + 1) * HALF)
                            out = c.PS[:, 2 * (n % 4) + h, 0:HALF]
                            for t in range(2):
                                w = slice(((n % 4) * 2 + t) * P, ((n % 4) * 2 + t + 1) * P)
                                wh, wl = c.WH[:, n // 4, w], c.WL[:, n // 4, w]
                                pe.matmul(out, wh, OH[:, t, cols], start=(t == 0), stop=False)
                                pe.matmul(out, wh, OL[:, t, cols], start=False, stop=False)
                                mm = pe.matmul(out, wl, OH[:, t, cols], start=False,
                                               stop=(t == 1))
                        mm.then_inc(c.unit_done if n % 4 == 3 else wo_raw, 1)
                    pe.wait_ge(r_added, 8 * i + 6)


def phase_layernorm(c, nc, name, out_dram=None):
    with ExitStack() as ctx:
        sb = lambda n, shape, dt=F32: ctx.enter_context(nc.sbuf_tensor(name + n, shape, dt))
        sem = lambda n: ctx.enter_context(nc.semaphore(name + n))
        SQ = sb("SQ", [P, KT, NT])
        Y, Z = sb("Y", [P, NT]), sb("Z", [P, NT])
        (mean, centred, squared, var, ln, rs, newton, normed, hi, lo, stored) = (
            sem(n) for n in ("mean", "centred", "squared", "var", "ln", "rs", "newton", "normed",
                             "hi", "lo", "stored"))
        R = c.R
        with nc.Block() as block:
            @block.tensor
            def _(pe):
                for h in range(2):
                    for k in range(KT):
                        mm = pe.matmul(c.PS[:, h, 0:HALF], c.ONES_D[:],
                                       R[:, k, h * HALF:(h + 1) * HALF], start=(k == 0),
                                       stop=(k == KT - 1))
                mm.then_inc(mean, 1)
                for k in range(KT):
                    pe.wait_ge(squared, k + 1)
                    for h in range(2):
                        mm = pe.matmul(c.PS[:, 2 + h, 0:HALF], c.ONES_D[:],
                                       SQ[:, k, h * HALF:(h + 1) * HALF], start=(k == 0),
                                       stop=(k == KT - 1))
                mm.then_inc(var, 1)

            @block.scalar
            def _(act):
                act.preload_act_table_set("natural_log_exp_and_others")
                for k in range(KT):
                    act.wait_ge(centred, k + 1)
                    act.activation(SQ[:, k, :], R[:, k, :], ACT.Square).then_inc(squared, 1)
                act.wait_ge(var, 1)
                rsqrt_from(c, act, halves(Y[:]), banks2(c, 2), c.EPS5[:], ln, 1).then_inc(rs, 1)
                if out_dram is None:
                    for k in range(KT):
                        act.wait_ge(normed, k + 1)
                        act.activation(c.XH[:, k, :], R[:, k, :], ACT.Copy).then_inc(hi, 1)

            @block.vector
            def _(dve):
                dve.wait_ge(mean, 1)
                for k in range(KT):
                    dve.tensor_tensor(halves(R[:, k, :]), halves(R[:, k, :]), banks2(c, 0),
                                      ALU.subtract).then_inc(centred, 1)
                dve.wait_ge(rs, 1)
                dve.scalar_tensor_tensor(out=halves(Z[:]), in0=banks2(c, 2), scalar=c.EPS5[:],
                                         in1=halves(Y[:]), op0=ALU.add,
                                         op1=ALU.mult).then_inc(newton, 1)
                dve.wait_ge(newton, 1)
                dve.tensor_tensor(Z[:], Z[:], Y[:], ALU.mult).then_inc(newton, 1)
                dve.wait_ge(newton, 2)
                dve.tensor_scalar(Z[:], Z[:], -0.5, 1.5, ALU.mult, ALU.add).then_inc(newton, 1)
                dve.wait_ge(newton, 3)
                dve.tensor_tensor(Y[:], Y[:], Z[:], ALU.mult).then_inc(newton, 1)
                dve.wait_ge(newton, 4)
                for k in range(KT):
                    dve.tensor_tensor(R[:, k, :], R[:, k, :], Y[:], ALU.mult).then_inc(normed, 1)
                    if out_dram is None:
                        dve.wait_ge(hi, k + 1)
                        dve.tensor_tensor(c.XL[:, k, :], R[:, k, :],
                                          c.XH[:, k, :].bitcast(F32), ALU.subtract)

            @block.sync
            def _(sp):
                if out_dram is not None:
                    for k in range(KT):
                        sp.wait_ge(normed, k + 1)
                        sp.dma_start(out_dram[:, k, :], R[:, k, :]).then_inc(stored, 16)
                    sp.wait_ge(stored, 16 * KT)


def phase_heads(c, nc):
    HEADS = QH_N + KV_N
    with ExitStack() as ctx:
        sb = lambda n, shape, dt=F32: ctx.enter_context(nc.sbuf_tensor("h_" + n, shape, dt))
        sem = lambda n: ctx.enter_context(nc.semaphore("h_" + n))
        T1, T2 = sb("T1", [P, 2, NT]), sb("T2", [P, NT])
        SQ, RS = sb("SQ", [P, 2, NT]), sb("RS", [P, 2, NT])
        squared, taken, var, ln, rs, roped, out = (sem(n) for n in (
            "squared", "taken", "var", "ln", "rs", "roped", "out"))
        with nc.Block() as block:
            @block.gpsimd
            def _(pool):
                pool.sem_inc(taken, 2)
                pool.sem_inc(ln, 2)
                pool.sem_inc(out, 2)

            @block.sync
            def _(sp):
                weight_stream(c, sp, U_QK // 2 + 2, HEADS // 4)

            @block.tensor
            def _(pe):
                def variance(j, i):
                    pe.wait_ge(squared, 4 * i + (j + 1))
                    pe.wait_ge(ln, 4 * i + (j + 1))
                    for h in range(2):
                        mm = pe.matmul(c.PS[:, 4 + 2 * (j % 2) + h, 0:HALF], c.ONES_HD[:],
                                       SQ[:, j % 2, h * HALF:(h + 1) * HALF], start=True,
                                       stop=True)
                    mm.then_inc(var, 1)

                with pe.Fori(0, HEADS // 4) as i:
                    for j in range(4):
                        pe.wait_ge(taken, 4 * i + (j + 1))
                        pe.wait_ge(c.w_lo, 4 * i + (U_QK + j + 1))
                        unit_matmuls(c, pe, j % 2, 2 * (j % 2), c.XH, c.XL)
                        if j > 0:
                            variance(j - 1, i)
                    variance(3, i)

            @block.scalar
            def _(act):
                def root(j, i):
                    act.wait_ge(var, 4 * i + (j + 1))
                    act.wait_ge(out, 4 * i + (j + 1))
                    rsqrt_from(c, act, halves(RS[:, j % 2, :]), banks2(c, 4 + 2 * (j % 2)),
                               c.EPS6[:], ln, 4 * i + (j + 3)).then_inc(rs, 1)

                act.preload_act_table_set("natural_log_exp_and_others")
                with act.Fori(0, HEADS // 4) as i:
                    for j in range(4):
                        split_hi(c, act, U_QK + j + 2, i, 1)
                        act.activation(halves(SQ[:, j % 2, :]), banks2(c, 2 * (j % 2)),
                                       ACT.Square).then_inc(squared, 1)
                        if j > 0:
                            root(j - 1, i)
                    root(3, i)

            @block.vector
            def _(dve):
                def finish(j, i):
                    dve.wait_ge(roped, 4 * i + (j + 1))
                    dve.wait_ge(rs, 4 * i + (j + 1))
                    dve.tensor_tensor(c.QX[:, ds(4 * NT * i + j * NT, NT)], T1[:, j % 2, :],
                                      RS[:, j % 2, :], ALU.mult).then_inc(out, 1)

                with dve.Fori(0, HEADS // 4) as i:
                    for j in range(4):
                        split_lo(c, dve, U_QK + j + 2, i, 1)
                        dve.wait_ge(squared, 4 * i + (j + 1))
                        for h in range(2):
                            bank = c.PS[:, 2 * (j % 2) + h, 0:HALF].rearrange(
                                "p (b t) -> p b t", t=T)
                            cols = slice(h * HALF, (h + 1) * HALF)
                            t1 = T1[:, j % 2, cols].rearrange("p (b t) -> p b t", t=T)
                            t2 = T2[:, cols].rearrange("p (b t) -> p b t", t=T)
                            dve.scalar_tensor_tensor(
                                out=t1, in0=bank, scalar=c.NW[:, ds(4 * i + j, 1)],
                                in1=c.COS[:].unsqueeze(1).broadcast_to([P, 4, T]), op0=ALU.mult,
                                op1=ALU.mult)
                            for lo in (0, 64):
                                hi = 64 - lo
                                ins = dve.scalar_tensor_tensor(
                                    out=t2[lo:lo + 64], in0=bank[hi:hi + 64],
                                    scalar=c.NW[lo:lo + 64, ds(4 * i + (HEADS + j), 1)],
                                    in1=c.SIN[lo:lo + 64].unsqueeze(1).broadcast_to([64, 4, T]),
                                    op0=ALU.mult, op1=ALU.mult)
                        ins.then_inc(taken, 1)
                        dve.wait_ge(taken, 4 * i + (j + 3))
                        dve.tensor_tensor(T1[:, j % 2, :], T1[:, j % 2, :], T2[:],
                                          ALU.add).then_inc(roped, 1)
                        if j > 0:
                            finish(j - 1, i)
                        if j == 0:
                            dve.wait_ge(roped, 4 * i + 1)
                        else:
                            dve.wait_ge(out, 4 * i + (j + 2))
                    finish(3, i)
                    dve.wait_ge(out, 4 * i + 6)


def phase_self_kv(c, nc):
    with ExitStack() as ctx:
        sem = lambda n: ctx.enter_context(nc.semaphore("s_" + n))
        VT = ctx.enter_context(nc.sbuf_tensor("VT", [T, 2, B, 2 * HD], F32))
        copied, stored = sem("copied"), sem("stored")
        with nc.Block() as block:
            @block.sync
            def _(sp):
                for v in range(KV_N):
                    sp.dma_start(c.kscr[:, v, :, CTX:KEYS].rearrange("b p t -> p b t"),
                                 c.QX[:, (QH_N + v) * NT:(QH_N + v + 1) * NT]
                                 .rearrange("p (b t) -> p b t", t=T)).then_inc(stored, 16)
                weight_stream(c, sp, U_V // 2 + 2, 1)
                for m in range(2):
                    sp.wait_ge(copied, m + 1)
                    for v in range(2):
                        for lo, hi, chunk, row in ((0, P - SELF_P, SELF_C, SELF_P),
                                                   (P - SELF_P, T, SELF_C + 1, 0)):
                            sp.dma_start(
                                c.vscr[:, 2 * m + v, row:row + hi - lo, chunk, :]
                                .rearrange("b p d -> p b d"),
                                VT[lo:hi, m, :, v * HD:(v + 1) * HD]).then_inc(stored, 16)
                sp.wait_ge(stored, 16 * (KV_N + 8))

            @block.tensor
            def _(pe):
                for m in range(2):
                    for s in range(2):
                        pe.wait_ge(c.w_lo, U_V + 2 * m + s + 1)
                        value_matmuls(c, pe, s, 4 * m)

            @block.scalar
            def _(act):
                for j in range(4):
                    split_hi(c, act, U_V + j + 2)

            @block.vector
            def _(dve):
                for m in range(2):
                    split_lo(c, dve, U_V + 2 * m + 2)
                    split_lo(c, dve, U_V + 2 * m + 3)
                    dve.wait_ge(c.unit_done, U_V + 2 * m + 2 - U_RET)
                    dve.tensor_copy(VT[:, m].rearrange("p (g b) n -> p g (b n)", b=2),
                                    c.PS[0:T, 4 * m:4 * m + 4, :]).then_inc(copied, 1)


def phase_attention(c, nc):
    with ExitStack() as ctx:
        sb = lambda n, shape, dt=F32: ctx.enter_context(nc.sbuf_tensor("a_" + n, shape, dt))
        sem = lambda n: ctx.enter_context(nc.semaphore("a_" + n))
        KRAW, VRAW = sb("KRAW", [P, KEYS]), sb("VRAW", [P, KC, HD])
        at = [0]

        def room(*shape):
            n = int(np.prod(shape))
            dims = "abc"[:len(shape)]
            views = [x[:].rearrange("p k t -> p (k t)")[:, at[0]:at[0] + n].rearrange(
                f"p ({' '.join(dims)}) -> p {' '.join(dims)}",
                **dict(zip(dims, shape))) for x in (c.XH, c.XL)]
            at[0] += n
            return views

        KHL = room(2, KEYS)
        VHL = room(2, KC * HD)
        PTH, PTL = room(KC, GRP, T)
        QHL = [sb("QH", [P, 2, GRP * T], F32R), sb("QL", [P, 2, GRP * T], F32R)]
        PR = sb("PR", [T, 2, KC * P])
        MX, NB, SU, RR = (sb("MX", [T, 2, 2]), sb("NB", [T, 2]), sb("SU", [T, 2, 2]),
                          sb("RR", [T, 2]))
        DG, IV = sb("DG", [T, 2, T]), sb("IV", [P, GRP * T])
        (kv_in, kv_hi, kv_lo, q_hi, q_lo, s_raw, masked, maxed, bias, exped, summed, recip,
         diag, inv_raw, inv_out, turned, p_hi, p_lo, o_raw, o_out, zeroed) = (sem(n) for n in (
             "kv_in", "kv_hi", "kv_lo", "q_hi", "q_lo", "s_raw", "masked", "maxed", "bias",
             "exped", "summed", "recip", "diag", "inv_raw", "inv_out", "turned", "p_hi", "p_lo",
             "o_raw", "o_out", "zeroed"))
        SCALE = float(HD) ** -0.5
        qx = c.QX[:].rearrange("p (h n) -> p h n", n=NT)

        def query_view(b, v):
            return qx[:, GRP * v:GRP * (v + 1), ds(b * T, T)]

        def heads(ap):
            return ap.rearrange("p (h t) -> p h t", h=GRP)

        def ahead(b, m, n, last):
            if m + n < QH_N:
                return b, m + n
            return None if last else (b + 1, m + n - QH_N)

        def every_batch(eng, body):
            with eng.Fori(0, B - 1) as b:
                body(b, False)
            body(B - 1, True)

        with nc.Block() as block:
            @block.gpsimd
            def _(pool):
                pool.memset(VRAW[:], 0.0).then_inc(zeroed, 1)
                pool.memset(PR[:], 0.0).then_inc(zeroed, 1)
                pool.sem_inc(kv_lo, 1)
                pool.sem_inc(exped, 2)
                pool.sem_inc(p_lo, 2)
                pool.sem_inc(o_out, 1)
                pool.sem_inc(inv_out, 1)
                pool.sem_inc(inv_raw, 2)
                with pool.Fori(0, B) as b:
                    for m in range(QH_N):
                        pool.wait_ge(inv_raw, 16 * b + (m + 1))
                        pool.wait_ge(recip, 16 * b + (m + 1))
                        pool.tensor_tensor(DG[:, m % 2, :], c.ID[0:T, 0:T],
                                           RR[:, m % 2:m % 2 + 1].broadcast_to([T, T]),
                                           ALU.mult).then_inc(diag, 1)

            @block.sync
            def _(sp):
                sp.wait_ge(zeroed, 1)
                with sp.Fori(0, B) as b:
                    for v in range(KV_N):
                        sp.wait_ge(kv_lo, 4 * b + (v + 1))
                        sp.dma_start(KRAW[:], c.kscr[ds(b, 1), v].rearrange("a p t -> (a p) t")
                                     ).then_inc(kv_in, 16)
                        sp.dma_start(VRAW[:, 0:KC - 1, :], c.vscr[ds(b, 1), v, :, 0:KC - 1, :]
                                     .rearrange("a p k d -> (a p) k d")).then_inc(kv_in, 16)
                        sp.dma_start(VRAW[0:LASTC, KC - 1, :],
                                     c.vscr[ds(b, 1), v, 0:LASTC, KC - 1, :]
                                     .rearrange("a p d -> (a p) d")).then_inc(kv_in, 16)

            @block.tensor
            def _(pe):
                def scores(b, m):
                    v, j, s = m // GRP, m % GRP, 2 * (m % 2)
                    pe.wait_ge(exped, 16 * b + (m + 1))
                    if j == 0:
                        pe.wait_ge(q_lo, 4 * b + (v + 1))
                    q = [x[:, v % 2, j * T:(j + 1) * T] for x in QHL]
                    for bank, k0, k1 in ((s, 0, KEY_A), (s + 1, KEY_A, KEYS)):
                        out = c.PS[0:T, bank, 0:k1 - k0]
                        k = [x[:, v % 2, k0:k1] for x in KHL]
                        pe.matmul(out, q[0], k[0], start=True, stop=False)
                        pe.matmul(out, q[0], k[1], start=False, stop=False)
                        mm = pe.matmul(out, q[1], k[0], start=False, stop=True)
                    mm.then_inc(s_raw, 1)

                def turn(b, m):
                    pe.wait_ge(exped, 16 * b + (m + 3))
                    for bank, chunks in ((4, range(0, 4)), (5, range(4, KC))):
                        pe.wait_ge(p_lo, 32 * b + (2 * m + bank - 3))
                        for n, k in enumerate(chunks):
                            mm = pe.transpose(c.PS[:, bank, n * T:(n + 1) * T],
                                              PR[:, m % 2, k * P:(k + 1) * P], c.ID[0:T, 0:T])
                        mm.then_inc(turned, 1)

                def inverse(b, m):
                    pe.wait_ge(diag, 16 * b + (m + 1))
                    if m % GRP == 0:
                        pe.wait_ge(inv_out, 4 * b + (m // GRP + 1))
                    pe.matmul(c.PS[:, 7, (m % GRP) * T:(m % GRP + 1) * T], c.ONES[0:T, :],
                              DG[:, m % 2, :], start=True, stop=True).then_inc(inv_raw, 1)

                def weigh(b, v):
                    pe.wait_ge(p_lo, 32 * b + (8 * v + 8 + 2))
                    pe.wait_ge(o_out, 4 * b + (v + 1))
                    out = c.PS[:, 6, 0:GRP * T]
                    for k in range(KC):
                        vh, vl = (x[:, v % 2, k * HD:(k + 1) * HD] for x in VHL)
                        ph = PTH[:, k].rearrange("p h t -> p (h t)")
                        pl = PTL[:, k].rearrange("p h t -> p (h t)")
                        pe.matmul(out, vh, ph, start=(k == 0), stop=False)
                        pe.matmul(out, vh, pl, start=False, stop=False)
                        mm = pe.matmul(out, vl, ph, start=False, stop=(k == KC - 1))
                    mm.then_inc(o_raw, 1)

                def body(b, last):
                    for m in range(QH_N):
                        if (nxt := ahead(b, m, 2, last)) is not None:
                            scores(*nxt)
                        if m % GRP == 0 and m > 0:
                            weigh(b, m // GRP - 1)
                        turn(b, m)
                        if m > 0:
                            inverse(b, m - 1)
                    inverse(b, QH_N - 1)
                    weigh(b, KV_N - 1)

                scores(0, 0)
                scores(0, 1)
                every_batch(pe, body)

            @block.scalar
            def _(act):
                def split_group(b, v):
                    act.wait_ge(kv_in, 192 * b + 48 * (v + 1))
                    act.activation(KHL[0][:, v % 2, :], KRAW[:], ACT.Copy)
                    act.activation(VHL[0][:, v % 2, :], VRAW[:].rearrange("p k d -> p (k d)"),
                                   ACT.Copy).then_inc(kv_hi, 1)
                    act.activation(heads(QHL[0][:, v % 2, :]), query_view(b, v),
                                   ACT.Copy).then_inc(q_hi, 1)

                def exponentials(b, m):
                    act.wait_ge(bias, 16 * b + (m + 1))
                    s = m % 2
                    for e, k0, k1 in ((0, 0, KEY_A), (1, KEY_A, KEYS)):
                        ins = act.activation(PR[:, s, k0:k1], c.PS[0:T, 2 * s + e, 0:k1 - k0],
                                             ACT.Exp, bias=NB[:, s:s + 1], scale=SCALE,
                                             accum_out=SU[:, s, e:e + 1])
                    ins.then_inc(exped, 1)

                def turned_hi(b, m):
                    for n, (bank, k0, k1) in enumerate(((4, 0, 4), (5, 4, KC))):
                        act.wait_ge(turned, 32 * b + (2 * m + n + 1))
                        act.activation(PTH[:, k0:k1, m % GRP, :],
                                       c.PS[:, bank, 0:(k1 - k0) * T].rearrange(
                                           "p (k t) -> p k t", t=T), ACT.Copy).then_inc(p_hi, 1)

                def inverse_out(b, v):
                    act.wait_ge(o_out, 4 * b + (v + 1))
                    act.wait_ge(inv_raw, 16 * b + (4 * v + 4 + 2))
                    act.activation(IV[:], c.PS[:, 7, 0:GRP * T], ACT.Copy).then_inc(inv_out, 1)

                def body(b, last):
                    for m in range(QH_N):
                        if (nxt := ahead(b, m, 1, last)) is not None:
                            exponentials(*nxt)
                        turned_hi(b, m)
                        if m % GRP == 0:
                            if m > 0:
                                inverse_out(b, m // GRP - 1)
                            if (nxt := ahead(b, m, GRP, last)) is not None:
                                split_group(nxt[0], nxt[1] // GRP)
                    inverse_out(b, KV_N - 1)

                act.preload_act_table_set("natural_log_exp_and_others")
                act.wait_ge(zeroed, 2)
                split_group(0, 0)
                exponentials(0, 0)
                every_batch(act, body)

            @block.vector
            def _(dve):
                def split_group(b, v):
                    dve.wait_ge(kv_hi, 4 * b + (v + 1))
                    dve.tensor_tensor(KHL[1][:, v % 2, :], KRAW[:],
                                      KHL[0][:, v % 2, :].bitcast(F32), ALU.subtract)
                    dve.tensor_tensor(VHL[1][:, v % 2, :], VRAW[:].rearrange("p k d -> p (k d)"),
                                      VHL[0][:, v % 2, :].bitcast(F32),
                                      ALU.subtract).then_inc(kv_lo, 1)
                    dve.wait_ge(q_hi, 4 * b + (v + 1))
                    dve.tensor_tensor(heads(QHL[1][:, v % 2, :]), query_view(b, v),
                                      heads(QHL[0][:, v % 2, :].bitcast(F32)),
                                      ALU.subtract).then_inc(q_lo, 1)

                def maxima(b, m):
                    s = m % 2
                    dve.wait_ge(s_raw, 16 * b + (m + 1))
                    own = c.PS[0:T, 2 * s + 1, KEY_B - T:KEY_B]
                    dve.tensor_tensor(own, own, c.CMASK[:], ALU.add).then_inc(masked, 1)
                    dve.tensor_reduce(MX[:, s, 0:1], c.PS[0:T, 2 * s, 0:KEY_A], AX.X, ALU.max)
                    dve.wait_ge(masked, 16 * b + (m + 1))
                    dve.tensor_reduce(MX[:, s, 1:2], c.PS[0:T, 2 * s + 1, 0:KEY_B], AX.X,
                                      ALU.max).then_inc(maxed, 1)
                    dve.wait_ge(maxed, 16 * b + (m + 1))
                    dve.tensor_scalar(NB[:, s:s + 1], MX[:, s, 0:1], MX[:, s, 1:2], -SCALE,
                                      ALU.max, ALU.mult).then_inc(bias, 1)

                def reciprocals(b, m):
                    s = m % 2
                    dve.wait_ge(exped, 16 * b + (m + 3))
                    dve.wait_ge(inv_raw, 16 * b + (m + 1))
                    dve.tensor_tensor(RR[:, s:s + 1], SU[:, s, 0:1], SU[:, s, 1:2],
                                      ALU.add).then_inc(summed, 1)
                    dve.wait_ge(summed, 16 * b + (m + 1))
                    dve.reciprocal(RR[:, s:s + 1], RR[:, s:s + 1]).then_inc(recip, 1)

                def turned_lo(b, m):
                    for n, (bank, k0, k1) in enumerate(((4, 0, 4), (5, 4, KC))):
                        dve.wait_ge(p_hi, 32 * b + (2 * m + n + 1))
                        dve.tensor_tensor(PTL[:, k0:k1, m % GRP, :],
                                          c.PS[:, bank, 0:(k1 - k0) * T].rearrange(
                                              "p (k t) -> p k t", t=T),
                                          PTH[:, k0:k1, m % GRP, :].bitcast(F32),
                                          ALU.subtract).then_inc(p_lo, 1)

                def output(b, v):
                    dve.wait_ge(inv_out, 4 * b + (v + 2))
                    dve.wait_ge(o_raw, 4 * b + (v + 1))
                    dve.tensor_tensor(query_view(b, v), heads(c.PS[:, 6, 0:GRP * T]),
                                      heads(IV[:]), ALU.mult).then_inc(o_out, 1)

                def body(b, last):
                    for m in range(QH_N):
                        reciprocals(b, m)
                        if (nxt := ahead(b, m, 2, last)) is not None:
                            maxima(*nxt)
                        turned_lo(b, m)
                        if m % GRP == 0:
                            if m > 0:
                                output(b, m // GRP - 1)
                            if (nxt := ahead(b, m, GRP, last)) is not None:
                                split_group(nxt[0], nxt[1] // GRP)
                    output(b, KV_N - 1)

                split_group(0, 0)
                maxima(0, 0)
                maxima(0, 1)
                every_batch(dve, body)


def phase_attention_out(c, nc):
    with ExitStack() as ctx:
        sem = lambda n: ctx.enter_context(nc.semaphore("w_" + n))
        x_hi, x_lo, added = sem("x_hi"), sem("x_lo"), sem("added")
        qx = c.QX[:].rearrange("p (h n) -> p h n", n=NT)
        with nc.Block() as block:
            @block.gpsimd
            def _(pool):
                pool.sem_inc(added, 4)

            @block.sync
            def _(sp):
                weight_stream(c, sp, U_WO // 2 + 2, 4)

            @block.tensor
            def _(pe):
                for g in range(2):
                    with pe.Fori(0, 2) as q:
                        for j in range(4):
                            pe.wait_ge(added, 4 * q + (8 * g + j + 1))
                            pe.wait_ge(c.w_lo, 4 * q + (U_WO + 8 * g + j + 1))
                            unit_matmuls(c, pe, j % 2, 2 * j, c.XH, c.XL,
                                         (lambda k: pe.wait_ge(x_lo, 8 * g + k + 1))
                                         if j == 0 else None)

            @block.scalar
            def _(act):
                for g in range(2):
                    if g == 1:
                        act.wait_ge(c.unit_done, U_WO + 8 - U_RET)
                    for k in range(KT):
                        act.activation(c.XH[:, k, :], qx[:, 8 * g + k, :],
                                       ACT.Copy).then_inc(x_hi, 1)
                    with act.Fori(0, 2) as q:
                        for j in range(4):
                            split_hi(c, act, U_WO + 8 * g + j + 2, q, 1)

            @block.vector
            def _(dve):
                for g in range(2):
                    for k in range(KT):
                        dve.wait_ge(x_hi, 8 * g + k + 1)
                        dve.tensor_tensor(c.XL[:, k, :], qx[:, 8 * g + k, :],
                                          c.XH[:, k, :].bitcast(F32),
                                          ALU.subtract).then_inc(x_lo, 1)
                    with dve.Fori(0, 2) as q:
                        for j in range(4):
                            split_lo(c, dve, U_WO + 8 * g + j + 2, q, 1)
                            dve.wait_ge(c.unit_done, 4 * q + (U_WO + 8 * g + j + 1 - U_RET))
                            r = c.R[:, ds(4 * q + j, 1), :].rearrange(
                                "p a (h t) -> p (a h) t", h=2)
                            dve.tensor_tensor(r, r, banks2(c, 2 * j),
                                              ALU.add).then_inc(added, 1)


def phase_ffn(c, nc):
    PER = 24
    with ExitStack() as ctx:
        sb = lambda n, shape, dt=F32: ctx.enter_context(nc.sbuf_tensor("f_" + n, shape, dt))
        sem = lambda n: ctx.enter_context(nc.semaphore("f_" + n))
        HH, HL = sb("HH", [P, KT, NT], F32R), sb("HL", [P, KT, NT], F32R)
        G, HF = sb("G", [P, NT]), sb("HF", [P, NT])
        gated, freed, h_hi, h_lo = (sem(n) for n in ("gated", "freed", "h_hi", "h_lo"))
        with nc.Block() as block:
            @block.gpsimd
            def _(pool):
                pool.sem_inc(freed, 4)

            @block.sync
            def _(sp):
                weight_stream(c, sp, U_FFN // 2 + 2, (PAIRS - U_FFN // 2 - 2) // 2)
                sp.wait_ge(c.w_lo, 2 * PAIRS - 2)
                sp.dma_start(c.RAW[:, 0, :], c.weights[PAIRS - 1]).then_inc(c.raw[0], 16)

            @block.tensor
            def _(pe):
                def unit(t, m, j, off, xh, xl, before_k=None):
                    pe.wait_ge(freed, PER * t + 4 * m + (off + j + 1))
                    pe.wait_ge(c.w_lo, PER * t + 4 * m + (U_FFN + off + j + 1))
                    unit_matmuls(c, pe, j % 2, 2 * j, xh, xl, before_k)

                with pe.Fori(0, CHUNKS) as t:
                    with pe.Fori(0, 4) as m:
                        for j in range(4):
                            unit(t, m, j, 0, c.XH, c.XL)
                    with pe.Fori(0, 2) as m:
                        for j in range(4):
                            unit(t, m, j, 16, HH, HL,
                                 (lambda k: pe.wait_ge(h_lo, 8 * t + (k + 1)))
                                 if j == 0 else None)

            @block.scalar
            def _(act):
                with act.Fori(0, CHUNKS) as t:
                    for m in range(4):
                        for e in range(2):
                            split_ahead_hi(c, act, 2 * e, t, m, 0)
                            act.activation(halves(G[:]), banks2(c, 4 * e),
                                           ACT.Silu).then_inc(gated, 1)
                            split_ahead_hi(c, act, 2 * e + 1, t, m, 0)
                            act.wait_ge(freed, PER * t + 4 * m + (2 * e + 2 + 4))
                            act.activation(HH[:, 2 * m + e, :], HF[:],
                                           ACT.Copy).then_inc(h_hi, 1)
                    with act.Fori(0, 2) as m:
                        for j in range(4):
                            split_ahead_hi(c, act, j, t, m, 16)

            @block.vector
            def _(dve):
                with dve.Fori(0, CHUNKS) as t:
                    with dve.Fori(0, 4) as m:
                        for e in range(2):
                            split_ahead_lo(c, dve, 2 * e, t, m, 0)
                            split_ahead_lo(c, dve, 2 * e + 1, t, m, 0)
                            dve.wait_ge(gated, 8 * t + 2 * m + (e + 1))
                            dve.wait_ge(c.unit_done,
                                        PER * t + 4 * m + (U_FFN + 2 * e + 2 - U_RET))
                            dve.tensor_tensor(halves(HF[:]), banks2(c, 4 * e + 2),
                                              halves(G[:]), ALU.mult).then_inc(freed, 2)
                            dve.wait_ge(h_hi, 8 * t + 2 * m + (e + 1))
                            dve.tensor_tensor(
                                HL[:, ds(2 * m + e, 1), :].rearrange("p a t -> p (a t)"), HF[:],
                                HH[:, ds(2 * m + e, 1), :].rearrange("p a t -> p (a t)")
                                .bitcast(F32), ALU.subtract).then_inc(h_lo, 1)
                            dve.wait_ge(h_lo, 8 * t + 2 * m + (e + 1))
                    with dve.Fori(0, 2) as m:
                        for j in range(4):
                            split_ahead_lo(c, dve, j, t, m, 16)
                            dve.wait_ge(c.unit_done,
                                        PER * t + 4 * m + (U_FFN + 16 + j + 1 - U_RET))
                            r = c.R[:, ds(4 * m + j, 1), :].rearrange(
                                "p a (h t) -> p (a h) t", h=2)
                            dve.tensor_tensor(r, r, banks2(c, 2 * j),
                                              ALU.add).then_inc(freed, 1)


def split_ahead_hi(c, act, j, t, m, off):
    u = U_FFN + off + j + 2
    act.wait_ge(c.raw[(u // 2) % 2], 96 * t + 16 * m + 16 * (u // 4 + 1))
    act.wait_ge(c.unit_done, 24 * t + 4 * m + (u - U_RET - 1))
    act.activation(c.WH[:, u % 2, :], raw_unit(c, u), ACT.Copy).then_inc(c.w_hi, 1)


def split_ahead_lo(c, dve, j, t, m, off):
    u = U_FFN + off + j + 2
    dve.wait_ge(c.w_hi, 24 * t + 4 * m + (u + 1))
    dve.tensor_tensor(c.WL[:, u % 2, :], raw_unit(c, u), c.WH[:, u % 2, :].bitcast(F32),
                      ALU.subtract).then_inc(c.w_lo, 1)


def decoder_layer(nc, c):
    with ExitStack() as ctx:
        sb = lambda n, shape, dt=F32: ctx.enter_context(nc.sbuf_tensor(n, shape, dt))
        sem = lambda n: ctx.enter_context(nc.semaphore(n))
        c.PS = ctx.enter_context(nc.psum_tensor("PS", [P, 8, 512], F32))
        c.RAW = sb("RAW", [P, 2, 2 * UNIT])
        c.WH, c.WL = sb("WH", [P, 2, UNIT], F32R), sb("WL", [P, 2, UNIT], F32R)
        c.COS, c.SIN = sb("COS", [P, T]), sb("SIN", [P, T])
        c.ID = sb("ID", [P, P])
        c.CMASK = sb("CMASK", [T, T])
        c.NW = sb("NW", [P, 2 * (QH_N + KV_N)])
        c.ONES_D, c.ONES_DV, c.ONES_HD = (sb(n, [P, P]) for n in ("ONES_D", "ONES_DV", "ONES_HD"))
        c.ONES = sb("ONES", [P, P])
        c.EPS5, c.EPS6 = sb("EPS5", [P, 1]), sb("EPS6", [P, 1])
        c.raw = [sem("raw0"), sem("raw1")]
        c.w_hi, c.w_lo, c.unit_done = sem("w_hi"), sem("w_lo"), sem("unit_done")
        c.const_in = sem("const_in")
        phase_constants(c, nc)
        phase_context(c, nc)
        c.R = sb("R", [P, KT, NT])
        c.XH, c.XL = sb("XH", [P, KT, NT], F32R), sb("XL", [P, KT, NT], F32R)
        phase_retention(c, nc)
        phase_layernorm(c, nc, "n1_")
        with ExitStack() as attention:
            c.QX = attention.enter_context(nc.sbuf_tensor("QX", [P, (QH_N + KV_N) * NT], F32))
            phase_heads(c, nc)
            phase_self_kv(c, nc)
            phase_attention(c, nc)
            phase_attention_out(c, nc)
        phase_layernorm(c, nc, "n2_")
        phase_ffn(c, nc)
        phase_layernorm(c, nc, "n3_", c.out)


def _tables():
    inv = np.float32(1.0) / np.float32(10000.0) ** (np.arange(0, HD, 2, dtype=np.float32)
                                                    / np.float32(HD))
    angle = np.arange(T, dtype=np.float32)[:, None] * inv[None, :]
    cos, sin = np.cos(angle).T, np.sin(angle).T
    gamma = np.float32(1.0) - np.exp2(-5.0 - np.arange(RH, dtype=np.float32)).astype(np.float32)
    diff = np.arange(T)[None, :] - np.arange(T)[:, None]
    power = np.exp2(np.log2(gamma.astype(np.float64))[None, :, None]
                    * np.maximum(diff, 0)[:, None, :])
    decay = np.where(diff[:, None, :] >= 0, power * float(HD) ** -0.5, 0.0)
    future = np.arange(T)[None, :] > np.arange(T)[:, None]
    f = lambda a: np.ascontiguousarray(a, dtype=np.float32)
    return {"cos": f(np.concatenate([cos, cos])), "sin": f(np.concatenate([-sin, sin])),
            "decay": f(decay), "cmask": f(np.where(future, -1e30, 0.0)), "ident": f(np.eye(P))}


def _unit(w, n0):
    return w[:, n0:n0 + P].reshape(KT, P, P).transpose(1, 0, 2).reshape(P, UNIT)


def _values(w, n0, n):
    return w[:, n0:n0 + n].reshape(KT, P, n).transpose(1, 0, 2).reshape(P, KT * n)


def _pack_weights(a):
    out = np.empty((PAIRS, P, 2 * UNIT), np.float32)
    at = [0]

    def put(*parts):
        for x in parts:
            for m in range(0, x.shape[1], UNIT):
                out[at[0] // 2, :, (at[0] % 2) * UNIT:(at[0] % 2 + 1) * UNIT] = x[:, m:m + UNIT]
                at[0] += 1

    put(*(_unit(a["L0_xattn_wk_ctx"], v * HD) for v in range(KV_N)))
    put(_values(a["L0_xattn_wv_ctx"], 0, KV_N * HD))
    for h in range(RH):
        put(_unit(a["L0_attn_Wq"], h * P), _unit(a["L0_attn_Wk"], h * P))
        put(_values(a["L0_attn_Wv"], h * RDV, RDV))
        put(_unit(a["L0_attn_Wg"], h * RDV), _unit(a["L0_attn_Wg"], h * RDV + P))
        put(a["L0_attn_Wo"][h * RDV:(h + 1) * RDV].reshape(2, P, KT, P).transpose(1, 2, 0, 3)
            .reshape(P, 2 * UNIT))
    put(*(_unit(a["L0_xattn_wq"], h * HD) for h in range(QH_N)))
    put(*(_unit(a["L0_xattn_wk"], v * HD) for v in range(KV_N)))
    put(*(_values(a["L0_xattn_wv"], m * 2 * HD, 2 * HD) for m in range(2)))
    for g in range(2):
        put(*(_unit(a["L0_xattn_wo"][g * D:(g + 1) * D], n * P) for n in range(KT)))
    gate, up, down = (a[f"L0_ffn_w_{n}"].T for n in ("gate", "up", "down"))
    for t in range(CHUNKS):
        for k in range(KT):
            put(_unit(gate, t * D + k * P), _unit(up, t * D + k * P))
        put(*(_unit(down[t * D:(t + 1) * D], n * P) for n in range(KT)))
    return out


def kernel(**inputs):
    import concourse.bacc as bacc
    from concourse.bass_utils import run_bass_kernel_spmd

    a = {k: np.asarray(v) for k, v in inputs.items()}
    qw, kw = a["L0_xattn_q_norm_w"], a["L0_xattn_k_norm_w"]
    turn = lambda w: np.concatenate([w[HD // 2:], w[:HD // 2]])
    arrays = {
        "weights": _pack_weights(a),
        "x": np.ascontiguousarray(a["x"].reshape(NT, KT, P).transpose(2, 1, 0)),
        "context": np.ascontiguousarray(
            a["ctx_2048"].reshape(B, CTX, KT, P).transpose(0, 3, 2, 1)),
        "gnw": np.ascontiguousarray(a["L0_attn_g_norm_weight"].reshape(2, P).T),
        "nw": np.stack([qw] * QH_N + [kw] * KV_N + [turn(qw)] * QH_N + [turn(kw)] * KV_N, 1),
        **_tables(),
    }
    nc = bacc.Bacc("TRN2", target_bir_lowering=False, num_devices=1)
    c = Core()
    for name, array in arrays.items():
        handle = nc.dram_tensor(name + "_dram", array.shape, F32, kind="ExternalInput")
        c.__dict__[name] = handle.ap()
    c.out = nc.dram_tensor("out_dram", (P, KT, NT), F32, kind="ExternalOutput").ap()
    c.kscr = nc.dram_tensor("keys_scratch", (B, KV_N, P, KEYS), F32, kind="Internal").ap()
    c.vscr = nc.dram_tensor("values_scratch", (B, KV_N, P, KC, HD), F32, kind="Internal").ap()
    decoder_layer(nc, c)
    r = run_bass_kernel_spmd(nc, [{k + "_dram": v for k, v in arrays.items()}], core_ids=[0])
    return r.results[0]["out_dram"].transpose(2, 1, 0).reshape(B, T, D)
```

```python
from contextlib import ExitStack

import numpy as np

import concourse.bass as bass
from concourse import mybir

F32 = mybir.dt.float32
F32R = mybir.dt.float32r
ALU = mybir.AluOpType
ACT = mybir.ActivationFunctionType
AX = mybir.AxisListType
ds = bass.ds

P = 128
B, T, D = 8, 100, 1024
NT = B * T
HALF = NT // 2
KT = D // P
RH, RDV = 8, 256
QH_N, KV_N, HD = 16, 4, 128
GRP = QH_N // KV_N
CTX = 722
KEYS = CTX + T
CA = 384
CB = CTX - CA
FF = 4096
CHUNKS = FF // D
UNIT = KT * P
KEY_A = 412
RING = 4
KC = -(-KEYS // P)
LASTC = KEYS - (KC - 1) * P
SELF_C = CTX // P
SELF_P = CTX % P

U_CTX, U_RET = 0, 8
U_QK = U_RET + 8 * RH
U_V = U_QK + QH_N + KV_N
U_WO = U_V + 4
U_FFN = U_WO + 16
U_END = U_FFN + 24 * CHUNKS
PAIRS = U_END // 2


class Core:
    pass


def weight_stream(c, sp, first_pair, n):
    with sp.Fori(0, n) as i:
        for s in range(2):
            sp.wait_ge(c.w_lo, 4 * i + (2 * (first_pair + s) - 2))
            sp.dma_start(c.RAW[:, s, :], c.weights[ds(2 * i + (first_pair + s), 1)]
                         .rearrange("a p w -> (a p) w")).then_inc(c.raw[s], 16)


def raw_unit(c, u):
    return c.RAW[:, (u // 2) % 2, (u % 2) * UNIT:(u % 2 + 1) * UNIT]


def split_hi(c, act, u, loop=0, per4=0):
    act.wait_ge(c.raw[(u // 2) % 2], 16 * per4 * loop + 16 * (u // 4 + 1))
    if u >= U_RET + 2:
        act.wait_ge(c.unit_done, 4 * per4 * loop + (u - U_RET - 1))
    act.activation(c.WH[:, u % 2, :], raw_unit(c, u), ACT.Copy).then_inc(c.w_hi, 1)


def split_lo(c, dve, u, loop=0, per4=0):
    dve.wait_ge(c.w_hi, 4 * per4 * loop + (u + 1))
    dve.tensor_tensor(c.WL[:, u % 2, :], raw_unit(c, u), c.WH[:, u % 2, :].bitcast(F32),
                      ALU.subtract).then_inc(c.w_lo, 1)


def halves(ap):
    return ap.rearrange("p (h t) -> p h t", h=2)


def banks2(c, bank, p0=0, p1=P):
    return c.PS[p0:p1, bank:bank + 2, 0:HALF]


def unit_matmuls(c, pe, slot, bank, xh, xl, before_k=None):
    for h in range(2):
        cols = slice(h * HALF, (h + 1) * HALF)
        for k in range(KT):
            if before_k is not None and h == 0:
                before_k(k)
            wh = c.WH[:, slot, k * P:(k + 1) * P]
            wl = c.WL[:, slot, k * P:(k + 1) * P]
            out = c.PS[:, bank + h, 0:HALF]
            pe.matmul(out, wh, xh[:, k, cols], start=(k == 0), stop=False)
            pe.matmul(out, wh, xl[:, k, cols], start=False, stop=False)
            mm = pe.matmul(out, wl, xh[:, k, cols], start=False, stop=(k == KT - 1))
    mm.then_inc(c.unit_done, 1)


def value_matmuls(c, pe, sweep, bank):
    wh = c.WH[:, sweep, :].rearrange("p (k n) -> p k n", n=256)
    wl = c.WL[:, sweep, :].rearrange("p (k n) -> p k n", n=256)
    for b in range(B):
        out = c.PS[0:T, bank + b // 2, (b % 2) * 256:(b % 2 + 1) * 256]
        for k in range(4):
            xh = c.XH[:, 4 * sweep + k, b * T:(b + 1) * T]
            xl = c.XL[:, 4 * sweep + k, b * T:(b + 1) * T]
            first = sweep == 0 and k == 0 and b % 2 == 0
            pe.matmul(out, xh, wh[:, k, :], start=first, stop=False, skip_group_check=True)
            pe.matmul(out, xl, wh[:, k, :], start=False, stop=False, skip_group_check=True)
            mm = pe.matmul(out, xh, wl[:, k, :], start=False, stop=(sweep == 1 and k == 3),
                           skip_group_check=True)
    mm.then_inc(c.unit_done, 1)


def rsqrt_from(c, act, out, stat, eps, ln_done, ln_count):
    act.activation(out, stat, ACT.Ln, bias=eps, scale=1.0).then_inc(ln_done, 1)
    act.wait_ge(ln_done, ln_count)
    return act.activation(out, out, ACT.Exp, scale=-0.5)


def phase_constants(c, nc):
    with nc.Block() as block:
        @block.sync
        def _(sp):
            for s in range(2):
                sp.dma_start(c.RAW[:, s, :], c.weights[s]).then_inc(c.raw[s], 16)
            for tile, src in ((c.COS, c.cos), (c.SIN, c.sin), (c.ID, c.ident),
                              (c.CMASK, c.cmask), (c.NW, c.nw)):
                sp.dma_start(tile[:], src).then_inc(c.const_in, 16)
            sp.wait_ge(c.const_in, 80)

        @block.gpsimd
        def _(pool):
            pool.memset(c.ONES[:], 1.0)
            pool.memset(c.ONES_D[:], 1.0 / D)
            pool.memset(c.ONES_DV[:], 1.0 / RDV)
            pool.memset(c.ONES_HD[:], 1.0 / HD)
            pool.memset(c.EPS5[:], 1e-5)
            pool.memset(c.EPS6[:], 1e-6)


def phase_context(c, nc):
    with ExitStack() as ctx:
        sb = lambda name, shape, dt=F32: ctx.enter_context(nc.sbuf_tensor(name, shape, dt))
        sem = lambda name: ctx.enter_context(nc.semaphore(name))
        CWH = sb("CWH", [P, 8, UNIT], F32R)
        CWL = sb("CWL", [P, 8, UNIT], F32R)
        CR = sb("CR", [P, KT, CA])
        CH = sb("CH", [P, 2, KT, CA], F32R)
        CL = sb("CL", [P, 2, KT, CA], F32R)
        SQ = sb("CSQ", [P, KV_N, CA])
        RS = sb("CRS", [P, 2, CA])
        KS = sb("KS", [P, 2, KV_N, CA])
        VS = sb("VS", [P, 3, KV_N * HD])
        chunk_in, chunk_hi, chunk_lo = sem("chunk_in"), sem("chunk_hi"), sem("chunk_lo")
        k_raw, k_sq, k_var, k_ln, k_rs, k_out = (sem(n) for n in (
            "k_raw", "k_sq", "k_var", "k_ln", "k_rs", "k_out"))
        v_raw, v_out, v_stored = sem("v_raw"), sem("v_out"), sem("v_stored")
        k_stored = [sem("k_stored0"), sem("k_stored1")]
        width, offset = (CA, CB), (0, CA)
        vwh = CWH[:, 4:8, :].rearrange("p u w -> p (u w)").rearrange("p (k n) -> p k n", n=512)
        vwl = CWL[:, 4:8, :].rearrange("p u w -> p (u w)").rearrange("p (k n) -> p k n", n=512)

        with nc.Block() as block:
            @block.gpsimd
            def _(pool):
                pool.sem_inc(k_out, 4)
                pool.sem_inc(k_ln, 2)
                pool.sem_inc(v_out, 2)
                pool.sem_inc(chunk_lo, 1)
                pool.sem_inc(k_stored[0], 16)
                pool.sem_inc(k_stored[1], 16)

            @block.sync
            def _(sp):
                def load(b, e):
                    sp.wait_ge(chunk_lo, 2 * b + e + 1)
                    w = width[e]
                    sp.dma_start(CR[:, :, 0:w], c.context[ds(b, 1), :, :, offset[e]:offset[e] + w]
                                 .rearrange("a p k t -> (a p) k t")).then_inc(chunk_in, 16)

                def store(b, e):
                    w = width[e]
                    sp.wait_ge(k_out, 4 * (2 * b + e) + 4 + 4)
                    dst = c.kscr[ds(b, 1), :, :, offset[e]:offset[e] + w]
                    sp.dma_start(dst.rearrange("a v p t -> p (a v) t"),
                                 KS[:, e, :, 0:w]).then_inc(k_stored[e], 16)
                    sp.wait_ge(v_out, 6 * b + 3 * e + 3 + 2)
                    for t in range(3):
                        rows = min(P, w - t * P)
                        dst = c.vscr[ds(b, 1), :, 0:rows, 3 * e + t, :]
                        sp.dma_start(dst.rearrange("a v p d -> p (a v) d"),
                                     VS[0:rows, t, :].rearrange("p (v d) -> p v d", v=KV_N)
                                     ).then_inc(v_stored, 16)

                load(0, 0)
                for s in range(2):
                    sp.wait_ge(c.w_lo, 2 * (2 + s) - 2)
                    sp.dma_start(c.RAW[:, s, :], c.weights[2 + s]).then_inc(c.raw[s], 16)
                load(0, 1)
                for s in range(2):
                    sp.wait_ge(c.w_lo, 2 * (4 + s) - 2)
                    sp.dma_start(c.RAW[:, s, :], c.weights[4 + s]).then_inc(c.raw[s], 16)
                with sp.Fori(0, B - 1) as b:
                    load(b + 1, 0)
                    store(b, 0)
                    load(b + 1, 1)
                    store(b, 1)
                store(B - 1, 0)
                store(B - 1, 1)
                sp.wait_ge(k_stored[0], 16 * B + 16)
                sp.wait_ge(k_stored[1], 16 * B + 16)
                sp.wait_ge(v_stored, 16 * 6 * B)

            @block.scalar
            def _(act):
                def resident_hi(u):
                    act.wait_ge(c.raw[(u // 2) % 2], 16 * (u // 4 + 1))
                    act.activation(CWH[:, u, :], raw_unit(c, u), ACT.Copy).then_inc(c.w_hi, 1)

                def chunk_split(b, e):
                    w = width[e]
                    act.wait_ge(chunk_in, 32 * b + 16 * (e + 1))
                    act.activation(CH[:, e, :, 0:w], CR[:, :, 0:w], ACT.Copy).then_inc(chunk_hi, 1)

                def body(b, last):
                    for e in range(2):
                        w, n0 = width[e], 4 * e
                        for h in range(KV_N):
                            act.wait_ge(k_raw, 8 * b + (n0 + h + 1))
                            act.activation(SQ[:, h, 0:w], c.PS[:, h, 0:w],
                                           ACT.Square).then_inc(k_sq, 1)
                        if e == 0:
                            chunk_split(b, 1)
                        elif not last:
                            chunk_split(b + 1, 0)
                        for h in range(KV_N):
                            act.wait_ge(k_var, 8 * b + (n0 + h + 1))
                            act.wait_ge(k_out, 8 * b + (n0 + h + 3))
                            rsqrt_from(c, act, RS[:, h % 2, 0:w], c.PS[:, 6 + h % 2, 0:w],
                                       c.EPS6[:], k_ln, 8 * b + (n0 + h + 3)).then_inc(k_rs, 1)

                act.preload_act_table_set("natural_log_exp_and_others")
                for u in range(2):
                    resident_hi(u)
                chunk_split(0, 0)
                for u in range(2, 8):
                    resident_hi(u)
                split_hi(c, act, 8)
                split_hi(c, act, 9)
                with act.Fori(0, B - 1) as b:
                    body(b, False)
                body(B - 1, True)

            @block.vector
            def _(dve):
                def resident_lo(u):
                    dve.wait_ge(c.w_hi, u + 1)
                    dve.tensor_tensor(CWL[:, u, :], raw_unit(c, u), CWH[:, u, :].bitcast(F32),
                                      ALU.subtract).then_inc(c.w_lo, 1)

                def chunk_split(b, e):
                    w = width[e]
                    dve.wait_ge(chunk_hi, 2 * b + (e + 1))
                    dve.tensor_tensor(CL[:, e, :, 0:w], CR[:, :, 0:w],
                                      CH[:, e, :, 0:w].bitcast(F32),
                                      ALU.subtract).then_inc(chunk_lo, 1)

                def body(b, last):
                    for e in range(2):
                        w = width[e]
                        if e == 0:
                            chunk_split(b, 1)
                        elif not last:
                            chunk_split(b + 1, 0)

                        def value_out(t):
                            rows = min(P, w - t * P)
                            n = 3 * e + t
                            dve.wait_ge(v_raw, 6 * b + (n + 1))
                            if t == 0 and not (e == 0 and isinstance(b, int) and b == 0):
                                dve.wait_ge(v_stored, 96 * b + 48 * e)
                            dve.tensor_copy(VS[0:rows, t, :],
                                            c.PS[0:rows, 4 + n % 2, :]).then_inc(v_out, 1)

                        def key_out(h):
                            dve.wait_ge(k_rs, 8 * b + (4 * e + h + 1))
                            if h == 0:
                                dve.wait_ge(k_stored[e], 16 * b + 16)
                            dve.scalar_tensor_tensor(
                                out=KS[:, e, h, 0:w], in0=c.PS[:, h, 0:w],
                                scalar=c.NW[:, QH_N:QH_N + 1], in1=RS[:, h % 2, 0:w],
                                op0=ALU.mult, op1=ALU.mult).then_inc(k_out, 1)

                        value_out(0)
                        key_out(0)
                        key_out(1)
                        value_out(1)
                        key_out(2)
                        key_out(3)
                        value_out(2)

                for u in range(2):
                    resident_lo(u)
                chunk_split(0, 0)
                for u in range(2, 8):
                    resident_lo(u)
                split_lo(c, dve, 8)
                split_lo(c, dve, 9)
                body(0, False)
                with dve.Fori(1, B - 1) as b:
                    body(b, False)
                body(B - 1, True)

            @block.tensor
            def _(pe):
                def keys(b, e, h):
                    w = width[e]
                    pe.wait_ge(k_out, 8 * b + (4 * e + h + 1))
                    out = c.PS[:, h, 0:w]
                    for k in range(KT):
                        wh, wl = CWH[:, h, k * P:(k + 1) * P], CWL[:, h, k * P:(k + 1) * P]
                        pe.matmul(out, wh, CH[:, e, k, 0:w], start=(k == 0), stop=False)
                        pe.matmul(out, wh, CL[:, e, k, 0:w], start=False, stop=False)
                        mm = pe.matmul(out, wl, CH[:, e, k, 0:w], start=False, stop=(k == KT - 1))
                    mm.then_inc(k_raw, 1)

                def key_variance(b, e, h):
                    pe.wait_ge(k_sq, 8 * b + (4 * e + h + 1))
                    pe.wait_ge(k_ln, 8 * b + (4 * e + h + 1))
                    pe.matmul(c.PS[:, 6 + h % 2, 0:width[e]], c.ONES_HD[:], SQ[:, h, 0:width[e]],
                              start=True, stop=True).then_inc(k_var, 1)

                def values(b, e, t):
                    rows = min(P, width[e] - t * P)
                    n = 3 * e + t
                    pe.wait_ge(v_out, 6 * b + (n + 1))
                    out = c.PS[0:rows, 4 + n % 2, :]
                    for k in range(KT):
                        ch = CH[:, e, k, t * P:t * P + rows]
                        cl = CL[:, e, k, t * P:t * P + rows]
                        pe.matmul(out, ch, vwh[:, k, :], start=(k == 0), stop=False)
                        pe.matmul(out, cl, vwh[:, k, :], start=False, stop=False)
                        mm = pe.matmul(out, ch, vwl[:, k, :], start=False, stop=(k == KT - 1))
                    mm.then_inc(v_raw, 1)

                pe.wait_ge(c.w_lo, 8)
                with pe.Fori(0, B) as b:
                    for e in range(2):
                        pe.wait_ge(chunk_lo, 2 * b + (e + 2))
                        for h in range(KV_N):
                            keys(b, e, h)
                        values(b, e, 0)
                        key_variance(b, e, 0)
                        key_variance(b, e, 1)
                        values(b, e, 1)
                        key_variance(b, e, 2)
                        key_variance(b, e, 3)
                        values(b, e, 2)


def phase_retention(c, nc):
    with ExitStack() as ctx:
        sb = lambda name, shape, dt=F32: ctx.enter_context(nc.sbuf_tensor(name, shape, dt))
        sem = lambda name: ctx.enter_context(nc.semaphore(name))
        DECAY = sb("DECAY", [T, RH, T])
        GNW = sb("GNW", [P, 2])
        T1, T2 = sb("T1", [P, NT]), sb("T2", [P, NT])
        QK = [[sb(f"{n}{part}", [P, NT], F32R) for part in "HL"] for n in "QK"]
        VH, VL = sb("VH", [T, B, RDV], F32R), sb("VL", [T, B, RDV], F32R)
        G = sb("G", [P, 2, NT])
        SM = sb("SM", [T, NT])
        SH, SL = sb("SH", [T, NT], F32R), sb("SL", [T, NT], F32R)
        SQ = sb("SQ", [P, 2, NT])
        RS = sb("RS", [P, NT])
        OR = sb("OR", [P, 2, NT])
        OH, OL = sb("OH", [P, 2, NT], F32R), sb("OL", [P, 2, NT], F32R)
        names = ("x_in", "x_hi", "x_lo", "turned", "roped", "qk_hi", "qk_lo", "v_hi", "v_lo",
                 "s_raw", "s_masked", "s_hi", "s_lo", "gated", "o_raw", "o_sq", "o_var", "o_ln",
                 "o_rs", "o_gated", "o_normed", "o_hi", "o_lo", "wo_raw", "r_added")
        (x_in, x_hi, x_lo, turned, roped, qk_hi, qk_lo, v_hi, v_lo, s_raw, s_masked, s_hi, s_lo,
         gated, o_raw, o_sq, o_var, o_ln, o_rs, o_gated, o_normed, o_hi, o_lo, wo_raw,
         r_added) = (sem("r_" + n) for n in names)
        R, XH, XL = c.R, c.XH, c.XL
        batches = lambda ap: ap.rearrange("p (b t) -> p b t", t=T)
        bank_tokens = lambda p0, p1: c.PS[p0:p1, 0:2, 0:HALF].rearrange(
            "p h (b t) -> p h b t", t=T)

        with nc.Block() as block:
            @block.sync
            def _(sp):
                for k in range(KT):
                    sp.dma_start(R[:, k, :], c.x[:, k, :]).then_inc(x_in, 16)
                sp.dma_start(DECAY[:], c.decay).then_inc(c.const_in, 16)
                sp.dma_start(GNW[:], c.gnw).then_inc(c.const_in, 16)
                weight_stream(c, sp, U_RET // 2 + 2, 2 * RH)

            @block.scalar
            def _(act):
                act.wait_ge(x_in, 16 * KT)
                for k in range(KT):
                    act.activation(XH[:, k, :], R[:, k, :], ACT.Copy).then_inc(x_hi, 1)
                with act.Fori(0, RH) as i:
                    for n in range(2):
                        split_hi(c, act, U_RET + n + 2, i, 2)
                        act.wait_ge(roped, 2 * i + (n + 1))
                        act.activation(QK[n][0][:], T1[:], ACT.Copy).then_inc(qk_hi, 1)
                    split_hi(c, act, U_RET + 4, i, 2)
                    split_hi(c, act, U_RET + 5, i, 2)
                    act.activation(VH[:].rearrange("p (g b) n -> p g (b n)", b=2),
                                   c.PS[0:T, 4:8, :], ACT.Copy).then_inc(v_hi, 1)
                    act.wait_ge(s_masked, i + 1)
                    act.activation(SH[:], SM[:], ACT.Copy).then_inc(s_hi, 1)
                    split_hi(c, act, U_RET + 6, i, 2)
                    act.activation(halves(G[:, 0, :]), banks2(c, 2), ACT.Silu).then_inc(gated, 1)
                    act.wait_ge(o_raw, i + 1)
                    act.activation(SQ[:].rearrange("p t (h n) -> p (t h) n", h=2),
                                   c.PS[:, 4:8, 0:HALF], ACT.Square).then_inc(o_sq, 1)
                    split_hi(c, act, U_RET + 7, i, 2)
                    act.activation(halves(G[:, 1, :]), banks2(c, 0), ACT.Silu).then_inc(gated, 1)
                    act.preload_act_table_set("natural_log_exp_and_others")
                    act.wait_ge(o_var, i + 1)
                    rsqrt_from(c, act, halves(RS[:]), banks2(c, 2), c.EPS5[:], o_ln,
                               i + 1).then_inc(o_rs, 1)
                    for t in range(2):
                        act.wait_ge(o_normed, 2 * i + (t + 1))
                        act.activation(OH[:, t, :], OR[:, t, :], ACT.Copy).then_inc(o_hi, 1)
                    split_hi(c, act, U_RET + 8, i, 2)
                    split_hi(c, act, U_RET + 9, i, 2)

            @block.vector
            def _(dve):
                for k in range(KT):
                    dve.wait_ge(x_hi, k + 1)
                    dve.tensor_tensor(XL[:, k, :], R[:, k, :], XH[:, k, :].bitcast(F32),
                                      ALU.subtract).then_inc(x_lo, 1)
                dve.wait_ge(c.const_in, 112)
                cos = c.COS[:].unsqueeze(1).broadcast_to([P, 4, T])

                def rope(n, i):
                    dve.wait_ge(c.unit_done, 8 * i + (n + 1))
                    for h in range(2):
                        bank = c.PS[:, 2 * n + h, 0:HALF].rearrange("p (b t) -> p b t", t=T)
                        cols = slice(h * HALF, (h + 1) * HALF)
                        t1, t2 = batches(T1[:, cols]), batches(T2[:, cols])
                        dve.tensor_tensor(t1, bank, cos, ALU.mult)
                        for lo in (0, 64):
                            hi = 64 - lo
                            ins = dve.tensor_tensor(
                                t2[lo:lo + 64], bank[hi:hi + 64],
                                c.SIN[lo:lo + 64].unsqueeze(1).broadcast_to([64, 4, T]), ALU.mult)
                    ins.then_inc(turned, 1)
                    dve.wait_ge(turned, 2 * i + (n + 1))
                    dve.tensor_tensor(T1[:], T1[:], T2[:], ALU.add).then_inc(roped, 1)
                    dve.wait_ge(qk_hi, 2 * i + (n + 1))
                    dve.tensor_tensor(QK[n][1][:], T1[:], QK[n][0][:].bitcast(F32),
                                      ALU.subtract).then_inc(qk_lo, 1)
                    dve.wait_ge(qk_lo, 2 * i + (n + 1))

                with dve.Fori(0, RH) as i:
                    for n in range(2):
                        split_lo(c, dve, U_RET + n + 2, i, 2)
                        rope(n, i)
                    split_lo(c, dve, U_RET + 4, i, 2)
                    split_lo(c, dve, U_RET + 5, i, 2)
                    dve.wait_ge(v_hi, i + 1)
                    dve.tensor_tensor(VL[:].rearrange("p (g b) n -> p g (b n)", b=2),
                                      c.PS[0:T, 4:8, :],
                                      VH[:].bitcast(F32).rearrange("p (g b) n -> p g (b n)", b=2),
                                      ALU.subtract).then_inc(v_lo, 1)
                    dve.wait_ge(s_raw, i + 1)
                    for h in range(2):
                        decay = DECAY[:, ds(i, 1), :].broadcast_to([T, 4, T])
                        ins = dve.tensor_tensor(
                            batches(SM[:, h * HALF:(h + 1) * HALF]),
                            c.PS[0:T, h, 0:HALF].rearrange("p (b t) -> p b t", t=T), decay,
                            ALU.mult)
                    ins.then_inc(s_masked, 1)
                    dve.wait_ge(s_hi, i + 1)
                    dve.tensor_tensor(SL[:], SM[:], SH[:].bitcast(F32),
                                      ALU.subtract).then_inc(s_lo, 1)
                    split_lo(c, dve, U_RET + 6, i, 2)
                    split_lo(c, dve, U_RET + 7, i, 2)
                    dve.wait_ge(o_sq, i + 1)
                    dve.wait_ge(gated, 2 * i + 2)
                    dve.tensor_tensor(OR[:].rearrange("p t (h n) -> p (t h) n", h=2),
                                      c.PS[:, 4:8, 0:HALF],
                                      G[:].rearrange("p t (h n) -> p (t h) n", h=2),
                                      ALU.mult).then_inc(o_gated, 1)
                    dve.wait_ge(o_gated, i + 1)
                    dve.wait_ge(o_rs, i + 1)
                    for t in range(2):
                        dve.scalar_tensor_tensor(out=OR[:, t, :], in0=OR[:, t, :],
                                                 scalar=GNW[:, t:t + 1], in1=RS[:], op0=ALU.mult,
                                                 op1=ALU.mult).then_inc(o_normed, 1)
                    for t in range(2):
                        dve.wait_ge(o_hi, 2 * i + (t + 1))
                        dve.tensor_tensor(OL[:, t, :], OR[:, t, :], OH[:, t, :].bitcast(F32),
                                          ALU.subtract).then_inc(o_lo, 1)
                    for n in range(KT):
                        if n % 4 == 3:
                            dve.wait_ge(c.unit_done, 8 * i + (7 + n // 4))
                        else:
                            dve.wait_ge(wo_raw, 6 * i + (n + 1 - n // 4))
                        dve.tensor_tensor(halves(R[:, n, :]), halves(R[:, n, :]),
                                          banks2(c, 2 * (n % 4)), ALU.add).then_inc(r_added, 1)
                        if n % 4 == 3:
                            split_lo(c, dve, U_RET + 8 + n // 4, i, 2)

            @block.tensor
            def _(pe):
                def weights(j, i):
                    pe.wait_ge(c.w_lo, 8 * i + (U_RET + j + 1))

                with pe.Fori(0, RH) as i:
                    weights(0, i)
                    unit_matmuls(c, pe, 0, 0, XH, XL, lambda k: pe.wait_ge(x_lo, k + 1))
                    weights(1, i)
                    unit_matmuls(c, pe, 1, 2, XH, XL)
                    pe.wait_ge(roped, 2 * i + 1)
                    for s in range(2):
                        weights(2 + s, i)
                        value_matmuls(c, pe, s, 4)
                    pe.wait_ge(qk_lo, 2 * i + 2)
                    for b in range(B):
                        out = c.PS[0:T, b // 4, (b % 4) * T:(b % 4 + 1) * T]
                        cols = slice(b * T, (b + 1) * T)
                        (qh, ql), (kh, kl) = QK
                        pe.matmul(out, kh[:, cols], qh[:, cols], start=True, stop=False)
                        pe.matmul(out, kh[:, cols], ql[:, cols], start=False, stop=False)
                        mm = pe.matmul(out, kl[:, cols], qh[:, cols], start=False, stop=True)
                    mm.then_inc(s_raw, 1)
                    weights(4, i)
                    unit_matmuls(c, pe, 0, 2, XH, XL)
                    pe.wait_ge(v_lo, i + 1)
                    pe.wait_ge(s_lo, i + 1)
                    for t in range(2):
                        for b in range(B):
                            out = c.PS[:, 4 + 2 * t + b // 4, (b % 4) * T:(b % 4 + 1) * T]
                            cols = slice(b * T, (b + 1) * T)
                            vh, vl = VH[:, b, t * P:(t + 1) * P], VL[:, b, t * P:(t + 1) * P]
                            pe.matmul(out, vh, SH[:, cols], start=True, stop=False)
                            pe.matmul(out, vh, SL[:, cols], start=False, stop=False)
                            mm = pe.matmul(out, vl, SH[:, cols], start=False, stop=True)
                    mm.then_inc(o_raw, 1)
                    weights(5, i)
                    unit_matmuls(c, pe, 1, 0, XH, XL)
                    pe.wait_ge(o_sq, i + 1)
                    pe.wait_ge(gated, 2 * i + 1)
                    for h in range(2):
                        for t in range(2):
                            mm = pe.matmul(c.PS[:, 2 + h, 0:HALF], c.ONES_DV[:],
                                           SQ[:, t, h * HALF:(h + 1) * HALF], start=(t == 0),
                                           stop=(t == 1))
                    mm.then_inc(o_var, 1)
                    for n in range(KT):
                        if n % 4 == 0:
                            weights(6 + n // 4, i)
                        if n == 0:
                            pe.wait_ge(o_lo, 2 * i + 2)
                            pe.wait_ge(gated, 2 * i + 2)
                        if n == 1:
                            pe.wait_ge(o_rs, i + 1)
                        if n == 2:
                            pe.wait_ge(o_gated, i + 1)
                        if n >= 4:
                            pe.wait_ge(r_added, 8 * i + (n - 3))
                        for h in range(2):
                            cols = slice(h * HALF, (h + 1) * HALF)
                            out = c.PS[:, 2 * (n % 4) + h, 0:HALF]
                            for t in range(2):
                                w = slice(((n % 4) * 2 + t) * P, ((n % 4) * 2 + t + 1) * P)
                                wh, wl = c.WH[:, n // 4, w], c.WL[:, n // 4, w]
                                pe.matmul(out, wh, OH[:, t, cols], start=(t == 0), stop=False)
                                pe.matmul(out, wh, OL[:, t, cols], start=False, stop=False)
                                mm = pe.matmul(out, wl, OH[:, t, cols], start=False,
                                               stop=(t == 1))
                        mm.then_inc(c.unit_done if n % 4 == 3 else wo_raw, 1)
                    pe.wait_ge(r_added, 8 * i + 6)


def phase_layernorm(c, nc, name, out_dram=None):
    with ExitStack() as ctx:
        sb = lambda n, shape, dt=F32: ctx.enter_context(nc.sbuf_tensor(name + n, shape, dt))
        sem = lambda n: ctx.enter_context(nc.semaphore(name + n))
        SQ = sb("SQ", [P, KT, NT])
        Y, Z = sb("Y", [P, NT]), sb("Z", [P, NT])
        (mean, centred, squared, var, ln, rs, newton, normed, hi, lo, stored) = (
            sem(n) for n in ("mean", "centred", "squared", "var", "ln", "rs", "newton", "normed",
                             "hi", "lo", "stored"))
        R = c.R
        with nc.Block() as block:
            @block.tensor
            def _(pe):
                for h in range(2):
                    for k in range(KT):
                        mm = pe.matmul(c.PS[:, h, 0:HALF], c.ONES_D[:],
                                       R[:, k, h * HALF:(h + 1) * HALF], start=(k == 0),
                                       stop=(k == KT - 1))
                mm.then_inc(mean, 1)
                for k in range(KT):
                    pe.wait_ge(squared, k + 1)
                    for h in range(2):
                        mm = pe.matmul(c.PS[:, 2 + h, 0:HALF], c.ONES_D[:],
                                       SQ[:, k, h * HALF:(h + 1) * HALF], start=(k == 0),
                                       stop=(k == KT - 1))
                mm.then_inc(var, 1)

            @block.scalar
            def _(act):
                act.preload_act_table_set("natural_log_exp_and_others")
                for k in range(KT):
                    act.wait_ge(centred, k + 1)
                    act.activation(SQ[:, k, :], R[:, k, :], ACT.Square).then_inc(squared, 1)
                act.wait_ge(var, 1)
                rsqrt_from(c, act, halves(Y[:]), banks2(c, 2), c.EPS5[:], ln, 1).then_inc(rs, 1)
                if out_dram is None:
                    for k in range(KT):
                        act.wait_ge(normed, k + 1)
                        act.activation(c.XH[:, k, :], R[:, k, :], ACT.Copy).then_inc(hi, 1)

            @block.vector
            def _(dve):
                dve.wait_ge(mean, 1)
                for k in range(KT):
                    dve.tensor_tensor(halves(R[:, k, :]), halves(R[:, k, :]), banks2(c, 0),
                                      ALU.subtract).then_inc(centred, 1)
                dve.wait_ge(rs, 1)
                dve.scalar_tensor_tensor(out=halves(Z[:]), in0=banks2(c, 2), scalar=c.EPS5[:],
                                         in1=halves(Y[:]), op0=ALU.add,
                                         op1=ALU.mult).then_inc(newton, 1)
                dve.wait_ge(newton, 1)
                dve.tensor_tensor(Z[:], Z[:], Y[:], ALU.mult).then_inc(newton, 1)
                dve.wait_ge(newton, 2)
                dve.tensor_scalar(Z[:], Z[:], -0.5, 1.5, ALU.mult, ALU.add).then_inc(newton, 1)
                dve.wait_ge(newton, 3)
                dve.tensor_tensor(Y[:], Y[:], Z[:], ALU.mult).then_inc(newton, 1)
                dve.wait_ge(newton, 4)
                for k in range(KT):
                    dve.tensor_tensor(R[:, k, :], R[:, k, :], Y[:], ALU.mult).then_inc(normed, 1)
                    if out_dram is None:
                        dve.wait_ge(hi, k + 1)
                        dve.tensor_tensor(c.XL[:, k, :], R[:, k, :],
                                          c.XH[:, k, :].bitcast(F32), ALU.subtract)

            @block.sync
            def _(sp):
                if out_dram is not None:
                    for k in range(KT):
                        sp.wait_ge(normed, k + 1)
                        sp.dma_start(out_dram[:, k, :], R[:, k, :]).then_inc(stored, 16)
                    sp.wait_ge(stored, 16 * KT)


def phase_heads(c, nc):
    HEADS = QH_N + KV_N
    with ExitStack() as ctx:
        sb = lambda n, shape, dt=F32: ctx.enter_context(nc.sbuf_tensor("h_" + n, shape, dt))
        sem = lambda n: ctx.enter_context(nc.semaphore("h_" + n))
        T1, T2 = sb("T1", [P, 2, NT]), sb("T2", [P, NT])
        SQ, RS = sb("SQ", [P, 2, NT]), sb("RS", [P, 2, NT])
        squared, taken, var, ln, rs, roped, out = (sem(n) for n in (
            "squared", "taken", "var", "ln", "rs", "roped", "out"))
        with nc.Block() as block:
            @block.gpsimd
            def _(pool):
                pool.sem_inc(taken, 2)
                pool.sem_inc(ln, 2)
                pool.sem_inc(out, 2)

            @block.sync
            def _(sp):
                weight_stream(c, sp, U_QK // 2 + 2, HEADS // 4)

            @block.tensor
            def _(pe):
                def variance(j, i):
                    pe.wait_ge(squared, 4 * i + (j + 1))
                    pe.wait_ge(ln, 4 * i + (j + 1))
                    for h in range(2):
                        mm = pe.matmul(c.PS[:, 4 + 2 * (j % 2) + h, 0:HALF], c.ONES_HD[:],
                                       SQ[:, j % 2, h * HALF:(h + 1) * HALF], start=True,
                                       stop=True)
                    mm.then_inc(var, 1)

                with pe.Fori(0, HEADS // 4) as i:
                    for j in range(4):
                        pe.wait_ge(taken, 4 * i + (j + 1))
                        pe.wait_ge(c.w_lo, 4 * i + (U_QK + j + 1))
                        unit_matmuls(c, pe, j % 2, 2 * (j % 2), c.XH, c.XL)
                        if j > 0:
                            variance(j - 1, i)
                    variance(3, i)

            @block.scalar
            def _(act):
                def root(j, i):
                    act.wait_ge(var, 4 * i + (j + 1))
                    act.wait_ge(out, 4 * i + (j + 1))
                    rsqrt_from(c, act, halves(RS[:, j % 2, :]), banks2(c, 4 + 2 * (j % 2)),
                               c.EPS6[:], ln, 4 * i + (j + 3)).then_inc(rs, 1)

                act.preload_act_table_set("natural_log_exp_and_others")
                with act.Fori(0, HEADS // 4) as i:
                    for j in range(4):
                        split_hi(c, act, U_QK + j + 2, i, 1)
                        act.activation(halves(SQ[:, j % 2, :]), banks2(c, 2 * (j % 2)),
                                       ACT.Square).then_inc(squared, 1)
                        if j > 0:
                            root(j - 1, i)
                    root(3, i)

            @block.vector
            def _(dve):
                def finish(j, i):
                    dve.wait_ge(roped, 4 * i + (j + 1))
                    dve.wait_ge(rs, 4 * i + (j + 1))
                    dve.tensor_tensor(c.QX[:, ds(4 * NT * i + j * NT, NT)], T1[:, j % 2, :],
                                      RS[:, j % 2, :], ALU.mult).then_inc(out, 1)

                with dve.Fori(0, HEADS // 4) as i:
                    for j in range(4):
                        split_lo(c, dve, U_QK + j + 2, i, 1)
                        dve.wait_ge(squared, 4 * i + (j + 1))
                        for h in range(2):
                            bank = c.PS[:, 2 * (j % 2) + h, 0:HALF].rearrange(
                                "p (b t) -> p b t", t=T)
                            cols = slice(h * HALF, (h + 1) * HALF)
                            t1 = T1[:, j % 2, cols].rearrange("p (b t) -> p b t", t=T)
                            t2 = T2[:, cols].rearrange("p (b t) -> p b t", t=T)
                            dve.scalar_tensor_tensor(
                                out=t1, in0=bank, scalar=c.NW[:, ds(4 * i + j, 1)],
                                in1=c.COS[:].unsqueeze(1).broadcast_to([P, 4, T]), op0=ALU.mult,
                                op1=ALU.mult)
                            for lo in (0, 64):
                                hi = 64 - lo
                                ins = dve.scalar_tensor_tensor(
                                    out=t2[lo:lo + 64], in0=bank[hi:hi + 64],
                                    scalar=c.NW[lo:lo + 64, ds(4 * i + (HEADS + j), 1)],
                                    in1=c.SIN[lo:lo + 64].unsqueeze(1).broadcast_to([64, 4, T]),
                                    op0=ALU.mult, op1=ALU.mult)
                        ins.then_inc(taken, 1)
                        dve.wait_ge(taken, 4 * i + (j + 3))
                        dve.tensor_tensor(T1[:, j % 2, :], T1[:, j % 2, :], T2[:],
                                          ALU.add).then_inc(roped, 1)
                        if j > 0:
                            finish(j - 1, i)
                        if j == 0:
                            dve.wait_ge(roped, 4 * i + 1)
                        else:
                            dve.wait_ge(out, 4 * i + (j + 2))
                    finish(3, i)
                    dve.wait_ge(out, 4 * i + 6)


def phase_self_kv(c, nc):
    with ExitStack() as ctx:
        sem = lambda n: ctx.enter_context(nc.semaphore("s_" + n))
        VT = ctx.enter_context(nc.sbuf_tensor("VT", [T, 2, B, 2 * HD], F32))
        copied, stored = sem("copied"), sem("stored")
        with nc.Block() as block:
            @block.sync
            def _(sp):
                for v in range(KV_N):
                    sp.dma_start(c.kscr[:, v, :, CTX:KEYS].rearrange("b p t -> p b t"),
                                 c.QX[:, (QH_N + v) * NT:(QH_N + v + 1) * NT]
                                 .rearrange("p (b t) -> p b t", t=T)).then_inc(stored, 16)
                weight_stream(c, sp, U_V // 2 + 2, 1)
                for m in range(2):
                    sp.wait_ge(copied, m + 1)
                    for v in range(2):
                        for lo, hi, chunk, row in ((0, P - SELF_P, SELF_C, SELF_P),
                                                   (P - SELF_P, T, SELF_C + 1, 0)):
                            sp.dma_start(
                                c.vscr[:, 2 * m + v, row:row + hi - lo, chunk, :]
                                .rearrange("b p d -> p b d"),
                                VT[lo:hi, m, :, v * HD:(v + 1) * HD]).then_inc(stored, 16)
                sp.wait_ge(stored, 16 * (KV_N + 8))

            @block.tensor
            def _(pe):
                for m in range(2):
                    for s in range(2):
                        pe.wait_ge(c.w_lo, U_V + 2 * m + s + 1)
                        value_matmuls(c, pe, s, 4 * m)

            @block.scalar
            def _(act):
                for j in range(4):
                    split_hi(c, act, U_V + j + 2)

            @block.vector
            def _(dve):
                for m in range(2):
                    split_lo(c, dve, U_V + 2 * m + 2)
                    split_lo(c, dve, U_V + 2 * m + 3)
                    dve.wait_ge(c.unit_done, U_V + 2 * m + 2 - U_RET)
                    dve.tensor_copy(VT[:, m].rearrange("p (g b) n -> p g (b n)", b=2),
                                    c.PS[0:T, 4 * m:4 * m + 4, :]).then_inc(copied, 1)


def phase_attention(c, nc):
    with ExitStack() as ctx:
        sb = lambda n, shape, dt=F32: ctx.enter_context(nc.sbuf_tensor("a_" + n, shape, dt))
        sem = lambda n: ctx.enter_context(nc.semaphore("a_" + n))
        GT = GRP * T
        KRAW, VRAW = sb("KRAW", [P, KEYS]), sb("VRAW", [P, KC, HD])
        at = [0]

        def room(*shape):
            n = int(np.prod(shape))
            dims = "abc"[:len(shape)]
            views = [x[:].rearrange("p k t -> p (k t)")[:, at[0]:at[0] + n].rearrange(
                f"p ({' '.join(dims)}) -> p {' '.join(dims)}",
                **dict(zip(dims, shape))) for x in (c.XH, c.XL)]
            at[0] += n
            return views

        KHL = room(2, KEYS)
        VHL = room(2, KC * HD)
        EHL = room(KC, GT)
        QHL = [sb("QH", [P, 2, GT], F32R), sb("QL", [P, 2, GT], F32R)]
        E = sb("E", [P, RING, GT])
        MX = sb("MX", [T, 2])
        DG = sb("DG", [T, 2, GT], F32R)
        IV, CV = sb("IV", [P, GT]), sb("CV", [P, GT])
        MASK, ID4 = sb("MASK", [T, SELF_P + T], F32R), sb("ID4", [T, GT], F32R)
        NEG, ONE = sb("NEG", [T, P], F32R), sb("ONE", [P, P], F32R)
        (k_in, v_in, tables, k_hi, k_lo, v_hi, v_lo, q_hi, q_lo, m_raw, maxed, diag, s_raw,
         exped, e_hi, e_lo, weighed, ln, inverted, newton, o_out, zeroed) = (sem(n) for n in (
             "k_in", "v_in", "tables", "k_hi", "k_lo", "v_hi", "v_lo", "q_hi", "q_lo", "m_raw",
             "maxed", "diag", "s_raw", "exped", "e_hi", "e_lo", "weighed", "ln", "inverted",
             "newton", "o_out", "zeroed"))
        SCALE = float(HD) ** -0.5
        qx = c.QX[:].rearrange("p (h n) -> p h n", n=NT)
        rows = [P] * (KC - 1) + [LASTC]
        MAXIMA_AT = (1, 2, 4, 5)
        KEYS_AT, VALUES_AT = 4, 4
        OUTPUT_AT = 2

        def query_view(b, v):
            return qx[:, GRP * v:GRP * (v + 1), ds(b * T, T)]

        def heads(ap):
            return ap.rearrange("p (h t) -> p h t", h=GRP)

        def after(b, v, last):
            if v + 1 < KV_N:
                return b, v + 1
            return None if last else (b + 1, 0)

        def before(b, v, first):
            if v > 0:
                return b, v - 1
            return None if first else (b - 1, KV_N - 1)

        def chunk_no(b, v, k):
            return KV_N * KC * b, KC * v + k

        def every_batch(eng, body):
            body(0, True, False)
            with eng.Fori(1, B - 1) as b:
                body(b, False, False)
            body(B - 1, False, True)

        with nc.Block() as block:
            @block.gpsimd
            def _(pool):
                pool.memset(VRAW[:], 0.0).then_inc(zeroed, 1)
                pool.sem_inc(k_lo, 1)
                pool.sem_inc(v_lo, 1)
                pool.sem_inc(maxed, 2)
                pool.sem_inc(diag, 2)
                pool.sem_inc(exped, RING)
                pool.sem_inc(e_lo, RING)
                pool.sem_inc(weighed, KC)
                pool.sem_inc(o_out, 1)

                def values_lo(b, v):
                    pool.wait_ge(v_hi, 4 * b + (v + 1))
                    pool.tensor_tensor(VHL[1][:, v % 2, :], VRAW[:].rearrange("p k d -> p (k d)"),
                                       VHL[0][:, v % 2, :].bitcast(F32),
                                       ALU.subtract).then_inc(v_lo, 1)

                def diagonal(b, v, j):
                    pool.wait_ge(maxed, 16 * b + (4 * v + j + 3))
                    pool.tensor_tensor(DG[:, v % 2, j * T:(j + 1) * T], c.ID[0:T, 0:T],
                                       MX[:, j % 2:j % 2 + 1].broadcast_to([T, T]),
                                       ALU.mult).then_inc(diag, 1)

                def body(b, first, last):
                    for v in range(KV_N):
                        if (nxt := after(b, v, last)) is not None:
                            for j in range(GRP):
                                diagonal(*nxt, j)
                            values_lo(*nxt)

                for j in range(GRP):
                    diagonal(0, 0, j)
                values_lo(0, 0)
                every_batch(pool, body)

            @block.sync
            def _(sp):
                sp.wait_ge(zeroed, 1)
                with sp.Fori(0, B) as b:
                    for v in range(KV_N):
                        sp.wait_ge(k_lo, 4 * b + (v + 1))
                        sp.dma_start(KRAW[:], c.kscr[ds(b, 1), v].rearrange("a p t -> (a p) t")
                                     ).then_inc(k_in, 16)
                        sp.wait_ge(v_lo, 4 * b + (v + 1))
                        sp.dma_start(VRAW[:, 0:KC - 1, :], c.vscr[ds(b, 1), v, :, 0:KC - 1, :]
                                     .rearrange("a p k d -> (a p) k d")).then_inc(v_in, 16)
                        sp.dma_start(VRAW[0:LASTC, KC - 1, :],
                                     c.vscr[ds(b, 1), v, 0:LASTC, KC - 1, :]
                                     .rearrange("a p d -> (a p) d")).then_inc(v_in, 16)

            @block.tensor
            def _(pe):
                def maxima_scores(b, v, j):
                    if j == 0:
                        pe.wait_ge(q_hi, 4 * b + (v + 1))
                    pe.wait_ge(maxed, 16 * b + (4 * v + j + 1))
                    q, s = QHL[0][:, v % 2, j * T:(j + 1) * T], 2 * (j % 2)
                    pe.matmul(c.PS[0:T, s, 0:KEY_A], q, KHL[0][:, v % 2, 0:KEY_A], start=True,
                              stop=True)
                    pe.matmul(c.PS[0:T, s + 1, 0:KEY_A], q, KHL[0][:, v % 2, KEYS - KEY_A:KEYS],
                              start=True, stop=False, skip_group_check=True)
                    pe.matmul(c.PS[0:T, s + 1, KEY_A - T:KEY_A], ID4[:, 0:T],
                              MASK[:, SELF_P:SELF_P + T], start=False, stop=True,
                              skip_group_check=True).then_inc(m_raw, 1)

                def scores(b, v, k):
                    n, at = chunk_no(b, v, k)
                    out = c.PS[0:rows[k], 4 + at % 2, 0:GT]
                    kh, kl = (x[:, v % 2, k * P:k * P + rows[k]] for x in KHL)
                    qh, ql = (x[:, v % 2, :] for x in QHL)
                    pe.wait_ge(exped, n + (at + 1 + RING - 2))
                    if k == 0:
                        pe.wait_ge(q_lo, 4 * b + (v + 1))
                    pe.matmul(out, kh, qh, start=True, stop=False)
                    pe.matmul(out, kh, ql, start=False, stop=False)
                    pe.matmul(out, kl, qh, start=False, stop=False)
                    if k >= SELF_C:
                        m0 = (k - SELF_C) * P
                        pe.matmul(out, MASK[:, m0:m0 + rows[k]], ID4[:], start=False, stop=False)
                    if k == 0:
                        pe.wait_ge(diag, 16 * b + (4 * v + 4 + 2))
                    pe.matmul(out, NEG[:, 0:rows[k]], DG[:, v % 2, :], start=False,
                              stop=True).then_inc(s_raw, 1)

                def weigh(b, v, k):
                    n, at = chunk_no(b, v, k)
                    pe.wait_ge(e_lo, n + (at + 1 + RING))
                    if k == 0:
                        pe.wait_ge(v_lo, 4 * b + (v + 2))
                        pe.wait_ge(o_out, 4 * b + (v + 1))
                    r = rows[k]
                    vh, vl = (x[0:r, v % 2, k * HD:(k + 1) * HD] for x in VHL)
                    eh, el = (x[0:r, k, :] for x in EHL)
                    out, total = c.PS[:, 6, 0:GT], c.PS[:, 7, 0:GT]
                    pe.matmul(out, vh, eh, start=(k == 0), stop=False)
                    pe.matmul(out, vh, el, start=False, stop=False)
                    pe.matmul(out, vl, eh, start=False, stop=(k == KC - 1))
                    pe.matmul(total, ONE[0:r, :], eh, start=(k == 0), stop=False)
                    pe.matmul(total, ONE[0:r, :], el, start=False,
                              stop=(k == KC - 1)).then_inc(weighed, 1)

                WEIGHED_OF_LAST = {0: (3, 4), 1: (5,), 2: (6,)}
                WEIGHED_OF_OWN = {5: (0, 1), 6: (2,)}

                def body(b, first, last):
                    for v in range(KV_N):
                        nxt, prev = after(b, v, last), before(b, v, first)
                        for k in range(KC):
                            scores(b, v, k)
                            for w in WEIGHED_OF_LAST.get(k, ()) if prev is not None else ():
                                weigh(*prev, w)
                            for w in WEIGHED_OF_OWN.get(k, ()):
                                weigh(b, v, w)
                            if k in MAXIMA_AT and nxt is not None:
                                maxima_scores(*nxt, MAXIMA_AT.index(k))

                pe.wait_ge(tables, 4)
                for j in range(GRP):
                    maxima_scores(0, 0, j)
                every_batch(pe, body)
                for k in range(3, KC):
                    weigh(B - 1, KV_N - 1, k)

            @block.scalar
            def _(act):
                def keys_hi(b, v):
                    act.wait_ge(k_in, 64 * b + 16 * (v + 1))
                    act.activation(KHL[0][:, v % 2, :], KRAW[:], ACT.Copy).then_inc(k_hi, 1)
                    act.activation(heads(QHL[0][:, v % 2, :]), query_view(b, v),
                                   ACT.Copy).then_inc(q_hi, 1)

                def values_hi(b, v):
                    act.wait_ge(v_in, 128 * b + 32 * (v + 1))
                    act.activation(VHL[0][:, v % 2, :], VRAW[:].rearrange("p k d -> p (k d)"),
                                   ACT.Copy).then_inc(v_hi, 1)

                def exponentials(b, v, k):
                    n, at = chunk_no(b, v, k)
                    r = rows[k]
                    act.wait_ge(s_raw, n + (at + 1))
                    act.wait_ge(e_lo, n + (at + 1))
                    act.activation(E[0:r, at % RING, :], c.PS[0:r, 4 + at % 2, 0:GT], ACT.Exp,
                                   scale=SCALE).then_inc(exped, 1)
                    act.wait_ge(exped, n + (at + 1 + RING))
                    act.wait_ge(weighed, n + (at + 1))
                    act.activation(EHL[0][0:r, k, :], E[0:r, at % RING, :],
                                   ACT.Copy).then_inc(e_hi, 1)

                def inverse(b, v):
                    act.wait_ge(weighed, 28 * b + (KC * v + 2 * KC))
                    act.wait_ge(o_out, 4 * b + (v + 1))
                    act.activation(IV[:], c.PS[:, 7, 0:GT], ACT.Ln).then_inc(ln, 1)
                    act.wait_ge(ln, 4 * b + (v + 1))
                    act.activation(IV[:], IV[:], ACT.Exp, scale=-1.0).then_inc(inverted, 1)

                def body(b, first, last):
                    for v in range(KV_N):
                        nxt, prev = after(b, v, last), before(b, v, first)
                        for k in range(KC):
                            exponentials(b, v, k)
                            if k == 0 and nxt is not None:
                                keys_hi(*nxt)
                            if k == 2 and prev is not None:
                                inverse(*prev)
                            if k == VALUES_AT and nxt is not None:
                                values_hi(*nxt)

                act.preload_act_table_set("natural_log_exp_and_others")
                act.activation(MASK[:], c.CMASK[:], ACT.Copy).then_inc(tables, 1)
                act.activation(heads(ID4[:]), c.ID[0:T, 0:T].unsqueeze(1)
                               .broadcast_to([T, GRP, T]), ACT.Copy).then_inc(tables, 1)
                act.activation(NEG[:], c.ONES[0:T, :], ACT.Copy, scale=-1.0).then_inc(tables, 1)
                act.activation(ONE[:], c.ONES[:], ACT.Copy).then_inc(tables, 1)
                keys_hi(0, 0)
                values_hi(0, 0)
                every_batch(act, body)
                inverse(B - 1, KV_N - 1)

            @block.vector
            def _(dve):
                def keys_lo(b, v):
                    dve.wait_ge(k_hi, 4 * b + (v + 1))
                    dve.tensor_tensor(KHL[1][:, v % 2, :], KRAW[:],
                                      KHL[0][:, v % 2, :].bitcast(F32),
                                      ALU.subtract).then_inc(k_lo, 1)
                    dve.wait_ge(q_hi, 4 * b + (v + 1))
                    dve.tensor_tensor(heads(QHL[1][:, v % 2, :]), query_view(b, v),
                                      heads(QHL[0][:, v % 2, :].bitcast(F32)),
                                      ALU.subtract).then_inc(q_lo, 1)

                def maximum(b, v, j):
                    dve.wait_ge(m_raw, 16 * b + (4 * v + j + 1))
                    dve.wait_ge(diag, 16 * b + (4 * v + j + 1))
                    dve.tensor_reduce(MX[:, j % 2:j % 2 + 1], c.PS[0:T, 2 * (j % 2):2 * (j % 2) + 2, 0:KEY_A], AX.XY,
                                      ALU.max).then_inc(maxed, 1)

                def exponentials_lo(b, v, k):
                    n, at = chunk_no(b, v, k)
                    r = rows[k]
                    dve.wait_ge(e_hi, n + (at + 1))
                    dve.tensor_tensor(EHL[1][0:r, k, :], E[0:r, at % RING, :],
                                      EHL[0][0:r, k, :].bitcast(F32),
                                      ALU.subtract).then_inc(e_lo, 1)

                def output(b, v):
                    dve.wait_ge(inverted, 4 * b + (v + 1))
                    dve.tensor_tensor(CV[:], c.PS[:, 7, 0:GT], IV[:], ALU.mult).then_inc(newton, 1)
                    dve.wait_ge(newton, 8 * b + (2 * v + 1))
                    dve.scalar_tensor_tensor(out=CV[:], in0=CV[:], scalar=2.0, in1=IV[:],
                                             op0=ALU.subtract, op1=ALU.mult).then_inc(newton, 1)
                    dve.wait_ge(newton, 8 * b + (2 * v + 2))
                    dve.scalar_tensor_tensor(out=query_view(b, v), in0=heads(c.PS[:, 6, 0:GT]),
                                             scalar=-1.0, in1=heads(CV[:]), op0=ALU.mult,
                                             op1=ALU.mult).then_inc(o_out, 1)

                def body(b, first, last):
                    for v in range(KV_N):
                        nxt, prev = after(b, v, last), before(b, v, first)
                        for k in range(KC):
                            if k in MAXIMA_AT and nxt is not None:
                                maximum(*nxt, MAXIMA_AT.index(k))
                            if k == OUTPUT_AT and prev is not None:
                                output(*prev)
                            exponentials_lo(b, v, k)
                            if k == KEYS_AT and nxt is not None:
                                keys_lo(*nxt)

                keys_lo(0, 0)
                for j in range(GRP):
                    maximum(0, 0, j)
                every_batch(dve, body)
                output(B - 1, KV_N - 1)


def phase_attention_out(c, nc):
    with ExitStack() as ctx:
        sem = lambda n: ctx.enter_context(nc.semaphore("w_" + n))
        x_hi, x_lo, added = sem("x_hi"), sem("x_lo"), sem("added")
        qx = c.QX[:].rearrange("p (h n) -> p h n", n=NT)
        with nc.Block() as block:
            @block.gpsimd
            def _(pool):
                pool.sem_inc(added, 4)

            @block.sync
            def _(sp):
                weight_stream(c, sp, U_WO // 2 + 2, 4)

            @block.tensor
            def _(pe):
                for g in range(2):
                    with pe.Fori(0, 2) as q:
                        for j in range(4):
                            pe.wait_ge(added, 4 * q + (8 * g + j + 1))
                            pe.wait_ge(c.w_lo, 4 * q + (U_WO + 8 * g + j + 1))
                            unit_matmuls(c, pe, j % 2, 2 * j, c.XH, c.XL,
                                         (lambda k: pe.wait_ge(x_lo, 8 * g + k + 1))
                                         if j == 0 else None)

            @block.scalar
            def _(act):
                for g in range(2):
                    if g == 1:
                        act.wait_ge(c.unit_done, U_WO + 8 - U_RET)
                    for k in range(KT):
                        act.activation(c.XH[:, k, :], qx[:, 8 * g + k, :],
                                       ACT.Copy).then_inc(x_hi, 1)
                    with act.Fori(0, 2) as q:
                        for j in range(4):
                            split_hi(c, act, U_WO + 8 * g + j + 2, q, 1)

            @block.vector
            def _(dve):
                for g in range(2):
                    for k in range(KT):
                        dve.wait_ge(x_hi, 8 * g + k + 1)
                        dve.tensor_tensor(c.XL[:, k, :], qx[:, 8 * g + k, :],
                                          c.XH[:, k, :].bitcast(F32),
                                          ALU.subtract).then_inc(x_lo, 1)
                    with dve.Fori(0, 2) as q:
                        for j in range(4):
                            split_lo(c, dve, U_WO + 8 * g + j + 2, q, 1)
                            dve.wait_ge(c.unit_done, 4 * q + (U_WO + 8 * g + j + 1 - U_RET))
                            r = c.R[:, ds(4 * q + j, 1), :].rearrange(
                                "p a (h t) -> p (a h) t", h=2)
                            dve.tensor_tensor(r, r, banks2(c, 2 * j),
                                              ALU.add).then_inc(added, 1)


def phase_ffn(c, nc):
    PER = 24
    with ExitStack() as ctx:
        sb = lambda n, shape, dt=F32: ctx.enter_context(nc.sbuf_tensor("f_" + n, shape, dt))
        sem = lambda n: ctx.enter_context(nc.semaphore("f_" + n))
        HH, HL = sb("HH", [P, KT, NT], F32R), sb("HL", [P, KT, NT], F32R)
        G, HF = sb("G", [P, NT]), sb("HF", [P, NT])
        gated, freed, h_hi, h_lo = (sem(n) for n in ("gated", "freed", "h_hi", "h_lo"))
        with nc.Block() as block:
            @block.gpsimd
            def _(pool):
                pool.sem_inc(freed, 4)

            @block.sync
            def _(sp):
                weight_stream(c, sp, U_FFN // 2 + 2, (PAIRS - U_FFN // 2 - 2) // 2)
                sp.wait_ge(c.w_lo, 2 * PAIRS - 2)
                sp.dma_start(c.RAW[:, 0, :], c.weights[PAIRS - 1]).then_inc(c.raw[0], 16)

            @block.tensor
            def _(pe):
                def unit(t, m, j, off, xh, xl, before_k=None):
                    pe.wait_ge(freed, PER * t + 4 * m + (off + j + 1))
                    pe.wait_ge(c.w_lo, PER * t + 4 * m + (U_FFN + off + j + 1))
                    unit_matmuls(c, pe, j % 2, 2 * j, xh, xl, before_k)

                with pe.Fori(0, CHUNKS) as t:
                    with pe.Fori(0, 4) as m:
                        for j in range(4):
                            unit(t, m, j, 0, c.XH, c.XL)
                    with pe.Fori(0, 2) as m:
                        for j in range(4):
                            unit(t, m, j, 16, HH, HL,
                                 (lambda k: pe.wait_ge(h_lo, 8 * t + (k + 1)))
                                 if j == 0 else None)

            @block.scalar
            def _(act):
                with act.Fori(0, CHUNKS) as t:
                    for m in range(4):
                        for e in range(2):
                            split_ahead_hi(c, act, 2 * e, t, m, 0)
                            act.activation(halves(G[:]), banks2(c, 4 * e),
                                           ACT.Silu).then_inc(gated, 1)
                            split_ahead_hi(c, act, 2 * e + 1, t, m, 0)
                            act.wait_ge(freed, PER * t + 4 * m + (2 * e + 2 + 4))
                            act.activation(HH[:, 2 * m + e, :], HF[:],
                                           ACT.Copy).then_inc(h_hi, 1)
                    with act.Fori(0, 2) as m:
                        for j in range(4):
                            split_ahead_hi(c, act, j, t, m, 16)

            @block.vector
            def _(dve):
                with dve.Fori(0, CHUNKS) as t:
                    with dve.Fori(0, 4) as m:
                        for e in range(2):
                            split_ahead_lo(c, dve, 2 * e, t, m, 0)
                            split_ahead_lo(c, dve, 2 * e + 1, t, m, 0)
                            dve.wait_ge(gated, 8 * t + 2 * m + (e + 1))
                            dve.wait_ge(c.unit_done,
                                        PER * t + 4 * m + (U_FFN + 2 * e + 2 - U_RET))
                            dve.tensor_tensor(halves(HF[:]), banks2(c, 4 * e + 2),
                                              halves(G[:]), ALU.mult).then_inc(freed, 2)
                            dve.wait_ge(h_hi, 8 * t + 2 * m + (e + 1))
                            dve.tensor_tensor(
                                HL[:, ds(2 * m + e, 1), :].rearrange("p a t -> p (a t)"), HF[:],
                                HH[:, ds(2 * m + e, 1), :].rearrange("p a t -> p (a t)")
                                .bitcast(F32), ALU.subtract).then_inc(h_lo, 1)
                            dve.wait_ge(h_lo, 8 * t + 2 * m + (e + 1))
                    with dve.Fori(0, 2) as m:
                        for j in range(4):
                            split_ahead_lo(c, dve, j, t, m, 16)
                            dve.wait_ge(c.unit_done,
                                        PER * t + 4 * m + (U_FFN + 16 + j + 1 - U_RET))
                            r = c.R[:, ds(4 * m + j, 1), :].rearrange(
                                "p a (h t) -> p (a h) t", h=2)
                            dve.tensor_tensor(r, r, banks2(c, 2 * j),
                                              ALU.add).then_inc(freed, 1)


def split_ahead_hi(c, act, j, t, m, off):
    u = U_FFN + off + j + 2
    act.wait_ge(c.raw[(u // 2) % 2], 96 * t + 16 * m + 16 * (u // 4 + 1))
    act.wait_ge(c.unit_done, 24 * t + 4 * m + (u - U_RET - 1))
    act.activation(c.WH[:, u % 2, :], raw_unit(c, u), ACT.Copy).then_inc(c.w_hi, 1)


def split_ahead_lo(c, dve, j, t, m, off):
    u = U_FFN + off + j + 2
    dve.wait_ge(c.w_hi, 24 * t + 4 * m + (u + 1))
    dve.tensor_tensor(c.WL[:, u % 2, :], raw_unit(c, u), c.WH[:, u % 2, :].bitcast(F32),
                      ALU.subtract).then_inc(c.w_lo, 1)


def decoder_layer(nc, c):
    with ExitStack() as ctx:
        sb = lambda n, shape, dt=F32: ctx.enter_context(nc.sbuf_tensor(n, shape, dt))
        sem = lambda n: ctx.enter_context(nc.semaphore(n))
        c.PS = ctx.enter_context(nc.psum_tensor("PS", [P, 8, 512], F32))
        c.RAW = sb("RAW", [P, 2, 2 * UNIT])
        c.WH, c.WL = sb("WH", [P, 2, UNIT], F32R), sb("WL", [P, 2, UNIT], F32R)
        c.COS, c.SIN = sb("COS", [P, T]), sb("SIN", [P, T])
        c.ID = sb("ID", [P, P])
        c.CMASK = sb("CMASK", [T, SELF_P + T])
        c.NW = sb("NW", [P, 2 * (QH_N + KV_N)])
        c.ONES_D, c.ONES_DV, c.ONES_HD = (sb(n, [P, P]) for n in ("ONES_D", "ONES_DV", "ONES_HD"))
        c.ONES = sb("ONES", [P, P])
        c.EPS5, c.EPS6 = sb("EPS5", [P, 1]), sb("EPS6", [P, 1])
        c.raw = [sem("raw0"), sem("raw1")]
        c.w_hi, c.w_lo, c.unit_done = sem("w_hi"), sem("w_lo"), sem("unit_done")
        c.const_in = sem("const_in")
        phase_constants(c, nc)
        phase_context(c, nc)
        c.R = sb("R", [P, KT, NT])
        c.XH, c.XL = sb("XH", [P, KT, NT], F32R), sb("XL", [P, KT, NT], F32R)
        phase_retention(c, nc)
        phase_layernorm(c, nc, "n1_")
        with ExitStack() as attention:
            c.QX = attention.enter_context(nc.sbuf_tensor("QX", [P, (QH_N + KV_N) * NT], F32))
            phase_heads(c, nc)
            phase_self_kv(c, nc)
            phase_attention(c, nc)
            phase_attention_out(c, nc)
        phase_layernorm(c, nc, "n2_")
        phase_ffn(c, nc)
        phase_layernorm(c, nc, "n3_", c.out)


def _tables():
    inv = np.float32(1.0) / np.float32(10000.0) ** (np.arange(0, HD, 2, dtype=np.float32)
                                                    / np.float32(HD))
    angle = np.arange(T, dtype=np.float32)[:, None] * inv[None, :]
    cos, sin = np.cos(angle).T, np.sin(angle).T
    gamma = np.float32(1.0) - np.exp2(-5.0 - np.arange(RH, dtype=np.float32)).astype(np.float32)
    diff = np.arange(T)[None, :] - np.arange(T)[:, None]
    power = np.exp2(np.log2(gamma.astype(np.float64))[None, :, None]
                    * np.maximum(diff, 0)[:, None, :])
    decay = np.where(diff[:, None, :] >= 0, power * float(HD) ** -0.5, 0.0)
    future = np.arange(T)[None, :] > np.arange(T)[:, None]
    f = lambda a: np.ascontiguousarray(a, dtype=np.float32)
    return {"cos": f(np.concatenate([cos, cos])), "sin": f(np.concatenate([-sin, sin])),
            "decay": f(decay), "cmask": f(np.pad(np.where(future, -1e30, 0.0), ((0, 0), (SELF_P, 0)))), "ident": f(np.eye(P))}


def _unit(w, n0):
    return w[:, n0:n0 + P].reshape(KT, P, P).transpose(1, 0, 2).reshape(P, UNIT)


def _values(w, n0, n):
    return w[:, n0:n0 + n].reshape(KT, P, n).transpose(1, 0, 2).reshape(P, KT * n)


def _pack_weights(a):
    out = np.empty((PAIRS, P, 2 * UNIT), np.float32)
    at = [0]

    def put(*parts):
        for x in parts:
            for m in range(0, x.shape[1], UNIT):
                out[at[0] // 2, :, (at[0] % 2) * UNIT:(at[0] % 2 + 1) * UNIT] = x[:, m:m + UNIT]
                at[0] += 1

    put(*(_unit(a["L0_xattn_wk_ctx"], v * HD) for v in range(KV_N)))
    put(_values(a["L0_xattn_wv_ctx"], 0, KV_N * HD))
    for h in range(RH):
        put(_unit(a["L0_attn_Wq"], h * P), _unit(a["L0_attn_Wk"], h * P))
        put(_values(a["L0_attn_Wv"], h * RDV, RDV))
        put(_unit(a["L0_attn_Wg"], h * RDV), _unit(a["L0_attn_Wg"], h * RDV + P))
        put(a["L0_attn_Wo"][h * RDV:(h + 1) * RDV].reshape(2, P, KT, P).transpose(1, 2, 0, 3)
            .reshape(P, 2 * UNIT))
    put(*(_unit(a["L0_xattn_wq"], h * HD) for h in range(QH_N)))
    put(*(_unit(a["L0_xattn_wk"], v * HD) for v in range(KV_N)))
    put(*(_values(a["L0_xattn_wv"], m * 2 * HD, 2 * HD) for m in range(2)))
    for g in range(2):
        put(*(_unit(a["L0_xattn_wo"][g * D:(g + 1) * D], n * P) for n in range(KT)))
    gate, up, down = (a[f"L0_ffn_w_{n}"].T for n in ("gate", "up", "down"))
    for t in range(CHUNKS):
        for k in range(KT):
            put(_unit(gate, t * D + k * P), _unit(up, t * D + k * P))
        put(*(_unit(down[t * D:(t + 1) * D], n * P) for n in range(KT)))
    return out


def kernel(**inputs):
    import concourse.bacc as bacc
    from concourse.bass_utils import run_bass_kernel_spmd

    a = {k: np.asarray(v) for k, v in inputs.items()}
    qw, kw = a["L0_xattn_q_norm_w"], a["L0_xattn_k_norm_w"]
    turn = lambda w: np.concatenate([w[HD // 2:], w[:HD // 2]])
    arrays = {
        "weights": _pack_weights(a),
        "x": np.ascontiguousarray(a["x"].reshape(NT, KT, P).transpose(2, 1, 0)),
        "context": np.ascontiguousarray(
            a["ctx_2048"].reshape(B, CTX, KT, P).transpose(0, 3, 2, 1)),
        "gnw": np.ascontiguousarray(a["L0_attn_g_norm_weight"].reshape(2, P).T),
        "nw": np.stack([qw] * QH_N + [kw] * KV_N + [turn(qw)] * QH_N + [turn(kw)] * KV_N, 1),
        **_tables(),
    }
    nc = bacc.Bacc("TRN2", target_bir_lowering=False, num_devices=1)
    c = Core()
    for name, array in arrays.items():
        handle = nc.dram_tensor(name + "_dram", array.shape, F32, kind="ExternalInput")
        c.__dict__[name] = handle.ap()
    c.out = nc.dram_tensor("out_dram", (P, KT, NT), F32, kind="ExternalOutput").ap()
    c.kscr = nc.dram_tensor("keys_scratch", (B, KV_N, P, KEYS), F32, kind="Internal").ap()
    c.vscr = nc.dram_tensor("values_scratch", (B, KV_N, P, KC, HD), F32, kind="Internal").ap()
    decoder_layer(nc, c)
    r = run_bass_kernel_spmd(nc, [{k + "_dram": v for k, v in arrays.items()}], core_ids=[0])
    return r.results[0]["out_dram"].transpose(2, 1, 0).reshape(B, T, D)
```

```python
from contextlib import ExitStack

import numpy as np

import concourse.bass as bass
from concourse import mybir

F32 = mybir.dt.float32
F32R = mybir.dt.float32r
ALU = mybir.AluOpType
ACT = mybir.ActivationFunctionType
AX = mybir.AxisListType
ds = bass.ds

P = 128
B, T, D = 8, 100, 1024
NT = B * T
HALF = NT // 2
KT = D // P
RH, RDV = 8, 256
QH_N, KV_N, HD = 16, 4, 128
GRP = QH_N // KV_N
CTX = 722
KEYS = CTX + T
CA = 384
CB = CTX - CA
FF = 4096
CHUNKS = FF // D
UNIT = KT * P
KEY_A = 412
X_EARLY = 4
RING = 4
KC = -(-KEYS // P)
LASTC = KEYS - (KC - 1) * P
SELF_C = CTX // P
SELF_P = CTX % P

U_CTX, U_RET = 0, 8
U_QK = U_RET + 8 * RH
U_V = U_QK + QH_N + KV_N
U_WO = U_V + 4
U_FFN = U_WO + 16
U_END = U_FFN + 24 * CHUNKS
PAIRS = U_END // 2


class Core:
    pass


def weight_stream(c, sp, first_pair, n):
    with sp.Fori(0, n) as i:
        for s in range(2):
            sp.wait_ge(c.w_lo, 4 * i + (2 * (first_pair + s) - 2))
            sp.dma_start(c.RAW[:, s, :], c.weights[ds(2 * i + (first_pair + s), 1)]
                         .rearrange("a p w -> (a p) w")).then_inc(c.raw[s], 16)


def raw_unit(c, u):
    return c.RAW[:, (u // 2) % 2, (u % 2) * UNIT:(u % 2 + 1) * UNIT]


def split_hi(c, act, u, loop=0, per4=0):
    act.wait_ge(c.raw[(u // 2) % 2], 16 * per4 * loop + 16 * (u // 4 + 1))
    if u >= U_RET + 2:
        act.wait_ge(c.unit_done, 4 * per4 * loop + (u - U_RET - 1))
    act.activation(c.WH[:, u % 2, :], raw_unit(c, u), ACT.Copy).then_inc(c.w_hi, 1)


def split_lo(c, dve, u, loop=0, per4=0):
    dve.wait_ge(c.w_hi, 4 * per4 * loop + (u + 1))
    dve.tensor_tensor(c.WL[:, u % 2, :], raw_unit(c, u), c.WH[:, u % 2, :].bitcast(F32),
                      ALU.subtract).then_inc(c.w_lo, 1)


def halves(ap):
    return ap.rearrange("p (h t) -> p h t", h=2)


def banks2(c, bank, p0=0, p1=P):
    return c.PS[p0:p1, bank:bank + 2, 0:HALF]


def unit_matmuls(c, pe, slot, bank, xh, xl, before=None, k_first=False):
    halves_first = [(h, k) for h in range(2) for k in range(KT)]
    for h, k in sorted(halves_first, key=lambda hk: hk[1]) if k_first else halves_first:
        cols = slice(h * HALF, (h + 1) * HALF)
        if before is not None:
            before(h, k)
        wh = c.WH[:, slot, k * P:(k + 1) * P]
        wl = c.WL[:, slot, k * P:(k + 1) * P]
        out = c.PS[:, bank + h, 0:HALF]
        pe.matmul(out, wh, xh[:, k, cols], start=(k == 0), stop=False)
        pe.matmul(out, wh, xl[:, k, cols], start=False, stop=False)
        mm = pe.matmul(out, wl, xh[:, k, cols], start=False, stop=(k == KT - 1))
    mm.then_inc(c.unit_done, 1)


def value_matmuls(c, pe, sweep, bank):
    wh = c.WH[:, sweep, :].rearrange("p (k n) -> p k n", n=256)
    wl = c.WL[:, sweep, :].rearrange("p (k n) -> p k n", n=256)
    for b in range(B):
        out = c.PS[0:T, bank + b // 2, (b % 2) * 256:(b % 2 + 1) * 256]
        for k in range(4):
            xh = c.XH[:, 4 * sweep + k, b * T:(b + 1) * T]
            xl = c.XL[:, 4 * sweep + k, b * T:(b + 1) * T]
            first = sweep == 0 and k == 0 and b % 2 == 0
            pe.matmul(out, xh, wh[:, k, :], start=first, stop=False, skip_group_check=True)
            pe.matmul(out, xl, wh[:, k, :], start=False, stop=False, skip_group_check=True)
            mm = pe.matmul(out, xh, wl[:, k, :], start=False, stop=(sweep == 1 and k == 3),
                           skip_group_check=True)
    mm.then_inc(c.unit_done, 1)


def rsqrt_from(c, act, out, stat, eps, ln_done, ln_count):
    act.activation(out, stat, ACT.Ln, bias=eps, scale=1.0).then_inc(ln_done, 1)
    act.wait_ge(ln_done, ln_count)
    return act.activation(out, out, ACT.Exp, scale=-0.5)


def phase_constants(c, nc):
    with nc.Block() as block:
        @block.sync
        def _(sp):
            for s in range(2):
                sp.dma_start(c.RAW[:, s, :], c.weights[s]).then_inc(c.raw[s], 16)

        @block.gpsimd
        def _(pool):
            pool.memset(c.ONES[:], 1.0)
            pool.memset(c.ONES_D[:], 1.0 / D)
            pool.memset(c.ONES_DV[:], 1.0 / RDV)
            pool.memset(c.ONES_HD[:], 1.0 / HD)
            pool.memset(c.EPS5[:], 1e-5)
            pool.memset(c.EPS6[:], 1e-6)


def phase_context(c, nc):
    with ExitStack() as ctx:
        sb = lambda name, shape, dt=F32: ctx.enter_context(nc.sbuf_tensor(name, shape, dt))
        sem = lambda name: ctx.enter_context(nc.semaphore(name))
        CWH = sb("CWH", [P, 8, UNIT], F32R)
        CWL = sb("CWL", [P, 8, UNIT], F32R)
        room = c.R[:].rearrange("p k t -> p (k t)")
        CR = room[:, 0:KT * CA].rearrange("p (k t) -> p k t", k=KT)
        at = X_EARLY * NT
        KS = room[:, at:at + 2 * KV_N * CA].rearrange("p (e v t) -> p e v t", e=2, v=KV_N)
        CH = sb("CH", [P, 2, KT, CA], F32R)
        CL = sb("CL", [P, 2, KT, CA], F32R)
        SQ = sb("CSQ", [P, 2, CA])
        SQH, SQL = sb("CSQH", [P, 2, CA], F32R), sb("CSQL", [P, 2, CA], F32R)
        ONE = sb("CONE", [P, P], F32R)
        RS = sb("CRS", [P, 2, CA])
        VS = sb("VS", [P, 3, KV_N * HD])
        chunk_in, chunk_hi, chunk_lo = sem("chunk_in"), sem("chunk_hi"), sem("chunk_lo")
        k_raw, k_sq, k_sq_hi, k_sq_lo, k_var, k_ln, k_rs, k_out = (sem(n) for n in (
            "k_raw", "k_sq", "k_sq_hi", "k_sq_lo", "k_var", "k_ln", "k_rs", "k_out"))
        v_raw, v_out, v_stored = sem("v_raw"), sem("v_out"), sem("v_stored")
        k_stored = [sem("k_stored0"), sem("k_stored1")]
        width, offset = (CA, CB), (0, CA)
        vwh = CWH[:, 4:8, :].rearrange("p u w -> p (u w)").rearrange("p (k n) -> p k n", n=512)
        vwl = CWL[:, 4:8, :].rearrange("p u w -> p (u w)").rearrange("p (k n) -> p k n", n=512)

        with nc.Block() as block:
            @block.gpsimd
            def _(pool):
                pool.sem_inc(k_out, 4)
                pool.sem_inc(k_ln, 2)
                pool.sem_inc(k_sq_lo, 2)
                pool.sem_inc(k_var, 2)
                pool.sem_inc(v_out, 2)
                pool.sem_inc(chunk_lo, 1)
                pool.sem_inc(k_stored[0], 16)
                pool.sem_inc(k_stored[1], 16)

            @block.sync
            def _(sp):
                def load(b, e):
                    sp.wait_ge(chunk_lo, 2 * b + e + 1)
                    w = width[e]
                    sp.dma_start(CR[:, :, 0:w], c.context[ds(b, 1), :, :, offset[e]:offset[e] + w]
                                 .rearrange("a p k t -> (a p) k t")).then_inc(chunk_in, 16)

                def store(b, e):
                    w = width[e]
                    sp.wait_ge(k_out, 4 * (2 * b + e) + 4 + 4)
                    dst = c.kscr[ds(b, 1), :, :, offset[e]:offset[e] + w]
                    sp.dma_start(dst.rearrange("a v p t -> p (a v) t"),
                                 KS[:, e, :, 0:w]).then_inc(k_stored[e], 16)
                    sp.wait_ge(v_out, 6 * b + 3 * e + 3 + 2)
                    for t in range(3):
                        rows = min(P, w - t * P)
                        dst = c.vscr[ds(b, 1), :, 0:rows, 3 * e + t, :]
                        sp.dma_start(dst.rearrange("a v p d -> p (a v) d"),
                                     VS[0:rows, t, :].rearrange("p (v d) -> p v d", v=KV_N)
                                     ).then_inc(v_stored, 16)

                load(0, 0)
                for s in range(2):
                    sp.wait_ge(c.w_lo, 2 * (2 + s) - 2)
                    sp.dma_start(c.RAW[:, s, :], c.weights[2 + s]).then_inc(c.raw[s], 16)
                for tile, src in ((c.NW, c.nw), (c.COS, c.cos), (c.SIN, c.sin), (c.ID, c.ident),
                                  (c.CMASK, c.cmask)):
                    sp.dma_start(tile[:], src).then_inc(c.const_in, 16)
                load(0, 1)
                for s in range(2):
                    sp.wait_ge(c.w_lo, 2 * (4 + s) - 2)
                    sp.dma_start(c.RAW[:, s, :], c.weights[4 + s]).then_inc(c.raw[s], 16)
                with sp.Fori(0, B - 1) as b:
                    load(b + 1, 0)
                    store(b, 0)
                    load(b + 1, 1)
                    store(b, 1)
                sp.wait_ge(chunk_lo, 2 * B + 1)
                for k in range(X_EARLY):
                    sp.dma_start(c.R[:, k, :], c.x[:, k, :]).then_inc(c.x_in[k], 16)
                store(B - 1, 0)
                store(B - 1, 1)
                sp.wait_ge(k_stored[0], 16 * B + 16)
                sp.wait_ge(k_stored[1], 16 * B + 16)
                sp.wait_ge(v_stored, 16 * 6 * B)

            @block.scalar
            def _(act):
                def resident_hi(u):
                    act.wait_ge(c.raw[(u // 2) % 2], 16 * (u // 4 + 1))
                    act.activation(CWH[:, u, :], raw_unit(c, u), ACT.Copy).then_inc(c.w_hi, 1)

                def chunk_split(b, e):
                    w = width[e]
                    act.wait_ge(chunk_in, 32 * b + 16 * (e + 1))
                    act.activation(CH[:, e, :, 0:w], CR[:, :, 0:w], ACT.Copy).then_inc(chunk_hi, 1)

                def body(b, last):
                    for e in range(2):
                        w, n0 = width[e], 4 * e
                        for h in range(KV_N):
                            act.wait_ge(k_raw, 8 * b + (n0 + h + 1))
                            act.wait_ge(k_sq_lo, 8 * b + (n0 + h + 1))
                            act.activation(SQ[:, h % 2, 0:w], c.PS[:, h, 0:w],
                                           ACT.Square).then_inc(k_sq, 1)
                            act.wait_ge(k_sq, 8 * b + (n0 + h + 1))
                            act.wait_ge(k_var, 8 * b + (n0 + h + 1))
                            act.activation(SQH[:, h % 2, 0:w], SQ[:, h % 2, 0:w],
                                           ACT.Copy).then_inc(k_sq_hi, 1)
                        if e == 0:
                            chunk_split(b, 1)
                        elif not last:
                            chunk_split(b + 1, 0)
                        for h in range(KV_N):
                            act.wait_ge(k_var, 8 * b + (n0 + h + 3))
                            act.wait_ge(k_out, 8 * b + (n0 + h + 3))
                            rsqrt_from(c, act, RS[:, h % 2, 0:w], c.PS[:, 6 + h % 2, 0:w],
                                       c.EPS6[:], k_ln, 8 * b + (n0 + h + 3)).then_inc(k_rs, 1)

                act.preload_act_table_set("natural_log_exp_and_others")
                act.activation(ONE[:], c.ONES_HD[:], ACT.Copy)
                for u in range(2):
                    resident_hi(u)
                chunk_split(0, 0)
                for u in range(2, 8):
                    resident_hi(u)
                split_hi(c, act, 8)
                split_hi(c, act, 9)
                with act.Fori(0, B - 1) as b:
                    body(b, False)
                body(B - 1, True)

            @block.vector
            def _(dve):
                def resident_lo(u):
                    dve.wait_ge(c.w_hi, u + 1)
                    dve.tensor_tensor(CWL[:, u, :], raw_unit(c, u), CWH[:, u, :].bitcast(F32),
                                      ALU.subtract).then_inc(c.w_lo, 1)

                def chunk_split(b, e):
                    w = width[e]
                    dve.wait_ge(chunk_hi, 2 * b + (e + 1))
                    dve.tensor_tensor(CL[:, e, :, 0:w], CR[:, :, 0:w],
                                      CH[:, e, :, 0:w].bitcast(F32),
                                      ALU.subtract).then_inc(chunk_lo, 1)

                def body(b, last):
                    for e in range(2):
                        w = width[e]

                        def square_lo(h):
                            dve.wait_ge(k_sq_hi, 8 * b + (4 * e + h + 1))
                            dve.tensor_tensor(SQL[:, h % 2, 0:w], SQ[:, h % 2, 0:w],
                                              SQH[:, h % 2, 0:w].bitcast(F32),
                                              ALU.subtract).then_inc(k_sq_lo, 1)

                        def value_out(t):
                            rows = min(P, w - t * P)
                            n = 3 * e + t
                            dve.wait_ge(v_raw, 6 * b + (n + 1))
                            if t == 0 and not (e == 0 and isinstance(b, int) and b == 0):
                                dve.wait_ge(v_stored, 96 * b + 48 * e)
                            dve.tensor_copy(VS[0:rows, t, :],
                                            c.PS[0:rows, 4 + n % 2, :]).then_inc(v_out, 1)

                        def key_out(h):
                            dve.wait_ge(k_rs, 8 * b + (4 * e + h + 1))
                            if h == 0:
                                dve.wait_ge(k_stored[e], 16 * b + 16)
                            dve.scalar_tensor_tensor(
                                out=KS[:, e, h, 0:w], in0=c.PS[:, h, 0:w],
                                scalar=c.NW[:, QH_N:QH_N + 1], in1=RS[:, h % 2, 0:w],
                                op0=ALU.mult, op1=ALU.mult).then_inc(k_out, 1)

                        square_lo(0)
                        square_lo(1)
                        value_out(0)
                        square_lo(2)
                        square_lo(3)
                        if e == 0:
                            chunk_split(b, 1)
                        elif not last:
                            chunk_split(b + 1, 0)
                        key_out(0)
                        key_out(1)
                        value_out(1)
                        key_out(2)
                        key_out(3)
                        value_out(2)

                for u in range(2):
                    resident_lo(u)
                chunk_split(0, 0)
                for u in range(2, 8):
                    resident_lo(u)
                split_lo(c, dve, 8)
                split_lo(c, dve, 9)
                dve.wait_ge(c.const_in, 80)
                body(0, False)
                with dve.Fori(1, B - 1) as b:
                    body(b, False)
                body(B - 1, True)

            @block.tensor
            def _(pe):
                def keys(b, e, h):
                    w = width[e]
                    pe.wait_ge(k_out, 8 * b + (4 * e + h + 1))
                    pe.wait_ge(c.w_lo, h + 1)
                    out = c.PS[:, h, 0:w]
                    for k in range(KT):
                        wh, wl = CWH[:, h, k * P:(k + 1) * P], CWL[:, h, k * P:(k + 1) * P]
                        pe.matmul(out, wh, CH[:, e, k, 0:w], start=(k == 0), stop=False)
                        pe.matmul(out, wh, CL[:, e, k, 0:w], start=False, stop=False)
                        mm = pe.matmul(out, wl, CH[:, e, k, 0:w], start=False, stop=(k == KT - 1))
                    mm.then_inc(k_raw, 1)

                def key_variance(b, e, h):
                    pe.wait_ge(k_sq_lo, 8 * b + (4 * e + h + 3))
                    pe.wait_ge(k_ln, 8 * b + (4 * e + h + 1))
                    out = c.PS[:, 6 + h % 2, 0:width[e]]
                    pe.matmul(out, ONE[:], SQH[:, h % 2, 0:width[e]], start=True, stop=False)
                    pe.matmul(out, ONE[:], SQL[:, h % 2, 0:width[e]], start=False,
                              stop=True).then_inc(k_var, 1)

                def values(b, e, t):
                    rows = min(P, width[e] - t * P)
                    n = 3 * e + t
                    pe.wait_ge(v_out, 6 * b + (n + 1))
                    pe.wait_ge(c.w_lo, 8)
                    out = c.PS[0:rows, 4 + n % 2, :]
                    for k in range(KT):
                        ch = CH[:, e, k, t * P:t * P + rows]
                        cl = CL[:, e, k, t * P:t * P + rows]
                        pe.matmul(out, ch, vwh[:, k, :], start=(k == 0), stop=False)
                        pe.matmul(out, cl, vwh[:, k, :], start=False, stop=False)
                        mm = pe.matmul(out, ch, vwl[:, k, :], start=False, stop=(k == KT - 1))
                    mm.then_inc(v_raw, 1)

                with pe.Fori(0, B) as b:
                    for e in range(2):
                        pe.wait_ge(chunk_lo, 2 * b + (e + 2))
                        for h in range(KV_N):
                            keys(b, e, h)
                        values(b, e, 0)
                        key_variance(b, e, 0)
                        key_variance(b, e, 1)
                        values(b, e, 1)
                        key_variance(b, e, 2)
                        key_variance(b, e, 3)
                        values(b, e, 2)


def phase_retention(c, nc):
    with ExitStack() as ctx:
        sb = lambda name, shape, dt=F32: ctx.enter_context(nc.sbuf_tensor(name, shape, dt))
        sem = lambda name: ctx.enter_context(nc.semaphore(name))
        DECAY = sb("DECAY", [T, RH, T])
        GNW = sb("GNW", [P, 2])
        T1, T2 = sb("T1", [P, NT]), sb("T2", [P, NT])
        QK = [[sb(f"{n}{part}", [P, NT], F32R) for part in "HL"] for n in "QK"]
        VH, VL = sb("VH", [T, B, RDV], F32R), sb("VL", [T, B, RDV], F32R)
        G = sb("G", [P, 2, NT])
        SM = sb("SM", [T, NT])
        SH, SL = sb("SH", [T, NT], F32R), sb("SL", [T, NT], F32R)
        SQ = sb("SQ", [P, 2, NT])
        RS = sb("RS", [P, NT])
        OR = sb("OR", [P, 2, NT])
        OH, OL = sb("OH", [P, 2, NT], F32R), sb("OL", [P, 2, NT], F32R)
        names = ("x_hi", "x_lo", "turned", "roped", "qk_hi", "qk_lo", "v_hi", "v_lo",
                 "s_raw", "s_masked", "s_hi", "s_lo", "gated", "o_raw", "o_sq", "o_sq_sum", "o_var", "o_ln",
                 "o_rs", "o_gated", "o_normed", "o_hi", "o_lo", "wo_raw", "r_added",
                 "r_summed", "mean")
        (x_hi, x_lo, turned, roped, qk_hi, qk_lo, v_hi, v_lo, s_raw, s_masked, s_hi, s_lo,
         gated, o_raw, o_sq, o_sq_sum, o_var, o_ln, o_rs, o_gated, o_normed, o_hi, o_lo, wo_raw,
         r_added, r_summed, mean) = (sem("r_" + n) for n in names)
        R, XH, XL = c.R, c.XH, c.XL
        WO, WV, WG = 2, 4, 6
        WO_BANKS = [(4, 6, 0)[n % 3] for n in range(KT)]

        def unit_no(unit, i, first):
            if first:
                return U_RET + (unit - 2 if unit >= WV else unit), 0
            return U_RET + 6 + unit, i - 1


        def in_order(first, scores, values):
            for step in (values, scores) if first else (scores, values):
                step()

        batches = lambda ap: ap.rearrange("p (b t) -> p b t", t=T)
        bank_tokens = lambda p0, p1: c.PS[p0:p1, 0:2, 0:HALF].rearrange(
            "p h (b t) -> p h b t", t=T)

        with nc.Block() as block:
            @block.sync
            def _(sp):
                for k in range(X_EARLY, KT):
                    sp.dma_start(R[:, k, :], c.x[:, k, :]).then_inc(c.x_in[k], 16)
                sp.dma_start(DECAY[:], c.decay).then_inc(c.const_in, 16)
                sp.dma_start(GNW[:], c.gnw).then_inc(c.const_in, 16)
                weight_stream(c, sp, U_RET // 2 + 2, 2 * RH)

            @block.scalar
            def _(act):
                for k in range(KT):
                    act.wait_ge(c.x_in[k], 16)
                    act.activation(XH[:, k, :], R[:, k, :], ACT.Copy).then_inc(x_hi, 1)

                def weights_ahead(unit, i, first):
                    u, loop = unit_no(unit, i, first)
                    split_hi(c, act, u + 2, loop, 2)

                def head(i, first):
                    for n in range(2):
                        weights_ahead(n, i, first)
                        act.wait_ge(roped, 2 * i + (n + 1))
                        act.activation(QK[n][0][:], T1[:], ACT.Copy).then_inc(qk_hi, 1)
                    if not first:
                        weights_ahead(WO, i, first)
                        weights_ahead(WO + 1, i, first)
                    def scores():
                        act.wait_ge(s_masked, i + 1)
                        act.activation(SH[:], SM[:], ACT.Copy).then_inc(s_hi, 1)

                    def values():
                        weights_ahead(WV, i, first)
                        weights_ahead(WV + 1, i, first)
                        act.activation(VH[:].rearrange("p (g b) n -> p g (b n)", b=2),
                                       c.PS[0:T, 4:8, :], ACT.Copy).then_inc(v_hi, 1)

                    in_order(first, scores, values)
                    weights_ahead(WG, i, first)
                    act.activation(halves(G[:, 0, :]), banks2(c, 2), ACT.Silu).then_inc(gated, 1)
                    act.wait_ge(o_raw, i + 1)
                    act.activation(SQ[:].rearrange("p t (h n) -> p (t h) n", h=2),
                                   c.PS[:, 4:8, 0:HALF], ACT.Square).then_inc(o_sq, 1)
                    weights_ahead(WG + 1, i, first)
                    act.activation(halves(G[:, 1, :]), banks2(c, 0), ACT.Silu).then_inc(gated, 1)
                    act.preload_act_table_set("natural_log_exp_and_others")
                    act.wait_ge(o_var, i + 1)
                    rsqrt_from(c, act, halves(RS[:]), banks2(c, 2), c.EPS5[:], o_ln,
                               i + 1).then_inc(o_rs, 1)
                    for t in range(2):
                        act.wait_ge(o_normed, 2 * i + (t + 1))
                        act.activation(OH[:, t, :], OR[:, t, :], ACT.Copy).then_inc(o_hi, 1)

                head(0, True)
                with act.Fori(1, RH) as i:
                    head(i, False)
                split_hi(c, act, U_QK)
                split_hi(c, act, U_QK + 1)

            @block.vector
            def _(dve):
                for k in range(KT):
                    dve.wait_ge(x_hi, k + 1)
                    dve.tensor_tensor(XL[:, k, :], R[:, k, :], XH[:, k, :].bitcast(F32),
                                      ALU.subtract).then_inc(x_lo, 1)
                dve.wait_ge(c.const_in, 112)
                cos = c.COS[:].unsqueeze(1).broadcast_to([P, 4, T])

                def rope(n, i, first, between):
                    dve.wait_ge(c.unit_done, n + 1 if first else 8 * i + (n - 1))
                    for h in range(2):
                        bank = c.PS[:, 2 * n + h, 0:HALF].rearrange("p (b t) -> p b t", t=T)
                        cols = slice(h * HALF, (h + 1) * HALF)
                        t1, t2 = batches(T1[:, cols]), batches(T2[:, cols])
                        dve.tensor_tensor(t1, bank, cos, ALU.mult)
                        for lo in (0, 64):
                            hi = 64 - lo
                            ins = dve.tensor_tensor(
                                t2[lo:lo + 64], bank[hi:hi + 64],
                                c.SIN[lo:lo + 64].unsqueeze(1).broadcast_to([64, 4, T]), ALU.mult)
                    ins.then_inc(turned, 1)
                    dve.wait_ge(turned, 2 * i + (n + 1))
                    dve.tensor_tensor(T1[:], T1[:], T2[:], ALU.add).then_inc(roped, 1)
                    between()
                    dve.wait_ge(qk_hi, 2 * i + (n + 1))
                    dve.tensor_tensor(QK[n][1][:], T1[:], QK[n][0][:].bitcast(F32),
                                      ALU.subtract).then_inc(qk_lo, 1)
                    dve.wait_ge(qk_lo, 2 * i + (n + 1))

                def weights_ahead(unit, i, first):
                    u, loop = unit_no(unit, i, first)
                    split_lo(c, dve, u + 2, loop, 2)

                def add_output(n, i, last=False):
                    if n % 4 == 3:
                        dve.wait_ge(c.unit_done, 8 * i + (n // 4 + 1 - (2 if last else 0)))
                    else:
                        dve.wait_ge(wo_raw, 6 * i + (n + 1 - n // 4 - 6))
                    dve.tensor_tensor(halves(R[:, n, :]), halves(R[:, n, :]),
                                      banks2(c, WO_BANKS[n]), ALU.add).then_inc(r_added, 1)

                def head(i, first):
                    rope(0, i, first, lambda: weights_ahead(0, i, first))

                    def while_k_is_split():
                        if not first:
                            add_output(0, i)
                        weights_ahead(1, i, first)

                    rope(1, i, first, while_k_is_split)
                    if not first:
                        for n in range(1, KT):
                            add_output(n, i)
                            if n % 4 == 3:
                                weights_ahead(WO + n // 4, i, first)
                    def scores():
                        dve.wait_ge(s_raw, i + 1)
                        for h in range(2):
                            decay = DECAY[:, ds(i, 1), :].broadcast_to([T, 4, T])
                            ins = dve.tensor_tensor(
                                batches(SM[:, h * HALF:(h + 1) * HALF]),
                                c.PS[0:T, h, 0:HALF].rearrange("p (b t) -> p b t", t=T), decay,
                                ALU.mult)
                        ins.then_inc(s_masked, 1)
                        dve.wait_ge(s_hi, i + 1)
                        dve.tensor_tensor(SL[:], SM[:], SH[:].bitcast(F32),
                                          ALU.subtract).then_inc(s_lo, 1)

                    def values():
                        weights_ahead(WV, i, first)
                        weights_ahead(WV + 1, i, first)
                        dve.wait_ge(v_hi, i + 1)
                        dve.tensor_tensor(VL[:].rearrange("p (g b) n -> p g (b n)", b=2),
                                          c.PS[0:T, 4:8, :],
                                          VH[:].bitcast(F32).rearrange("p (g b) n -> p g (b n)", b=2),
                                          ALU.subtract).then_inc(v_lo, 1)

                    in_order(first, scores, values)
                    weights_ahead(WG, i, first)
                    dve.wait_ge(o_sq, i + 1)
                    dve.tensor_tensor(SQ[:, 0, :], SQ[:, 0, :], SQ[:, 1, :],
                                      ALU.add).then_inc(o_sq_sum, 1)
                    weights_ahead(WG + 1, i, first)
                    dve.wait_ge(gated, 2 * i + 2)
                    dve.tensor_tensor(OR[:].rearrange("p t (h n) -> p (t h) n", h=2),
                                      c.PS[:, 4:8, 0:HALF],
                                      G[:].rearrange("p t (h n) -> p (t h) n", h=2),
                                      ALU.mult).then_inc(o_gated, 1)
                    dve.wait_ge(o_gated, i + 1)
                    dve.wait_ge(o_rs, i + 1)
                    for t in range(2):
                        dve.scalar_tensor_tensor(out=OR[:, t, :], in0=OR[:, t, :],
                                                 scalar=GNW[:, t:t + 1], in1=RS[:], op0=ALU.mult,
                                                 op1=ALU.mult).then_inc(o_normed, 1)
                    for t in range(2):
                        dve.wait_ge(o_hi, 2 * i + (t + 1))
                        dve.tensor_tensor(OL[:, t, :], OR[:, t, :], OH[:, t, :].bitcast(F32),
                                          ALU.subtract).then_inc(o_lo, 1)

                head(0, True)
                with dve.Fori(1, RH) as i:
                    head(i, False)
                for n in range(KT):
                    add_output(n, RH, last=True)
                    if n > 0:
                        dve.wait_ge(r_added, 8 * RH - 8 + n + 1)
                        if n > 1:
                            dve.wait_ge(r_summed, n - 1)
                        dve.tensor_tensor(T1[:], R[:, 0, :] if n == 1 else T1[:], R[:, n, :],
                                          ALU.add).then_inc(r_summed, 1)
                    if n % 4 == 3:
                        split_lo(c, dve, U_QK + n // 4)

            @block.tensor
            def _(pe):
                def weights(unit, i, first):
                    if first:
                        pe.wait_ge(c.w_lo, unit_no(unit, i, first)[0] + 1)
                    else:
                        pe.wait_ge(c.w_lo, 8 * i + (U_RET - 2 + unit + 1))

                def project_output(i, last):
                    for n in range(KT):
                        if n % 4 == 0:
                            pe.wait_ge(c.w_lo, 8 * i + (U_RET + (n // 4 + 1) - (2 if last else 0)))
                        if n == 0:
                            pe.wait_ge(o_lo, 2 * i)
                        if n >= 3:
                            pe.wait_ge(r_added, 8 * i + (n - 2 - 8))
                        elif n == 2 and not last:
                            pe.wait_ge(roped, 2 * i + 1)
                        for h in range(2):
                            cols = slice(h * HALF, (h + 1) * HALF)
                            out = c.PS[:, WO_BANKS[n] + h, 0:HALF]
                            for t in range(2):
                                w = slice(((n % 4) * 2 + t) * P, ((n % 4) * 2 + t + 1) * P)
                                wh, wl = c.WH[:, n // 4, w], c.WL[:, n // 4, w]
                                pe.matmul(out, wh, OH[:, t, cols], start=(t == 0), stop=False)
                                pe.matmul(out, wh, OL[:, t, cols], start=False, stop=False)
                                mm = pe.matmul(out, wl, OH[:, t, cols], start=False,
                                               stop=(t == 1))
                        mm.then_inc(c.unit_done if n % 4 == 3 else wo_raw, 1)

                def head(i, first):
                    weights(0, i, first)
                    if not first:
                        pe.wait_ge(gated, 2 * i)
                    unit_matmuls(c, pe, 0, 0, XH, XL,
                                 (lambda h, k: pe.wait_ge(x_lo, k + 1)) if first else None,
                                 k_first=first)
                    weights(1, i, first)
                    if not first:
                        pe.wait_ge(o_ln, i)
                    unit_matmuls(c, pe, 1, 2, XH, XL)
                    if not first:
                        project_output(i, False)
                    def scores():
                        pe.wait_ge(qk_lo, 2 * i + 2)
                        if not first:
                            pe.wait_ge(r_added, 8 * i - 2)
                        for b in range(B):
                            out = c.PS[0:T, b // 4, (b % 4) * T:(b % 4 + 1) * T]
                            cols = slice(b * T, (b + 1) * T)
                            (qh, ql), (kh, kl) = QK
                            pe.matmul(out, kh[:, cols], qh[:, cols], start=True, stop=False)
                            pe.matmul(out, kh[:, cols], ql[:, cols], start=False, stop=False)
                            mm = pe.matmul(out, kl[:, cols], qh[:, cols], start=False, stop=True)
                        mm.then_inc(s_raw, 1)

                    def values():
                        if not first:
                            pe.wait_ge(r_added, 8 * i)
                        for s in range(2):
                            weights(WV + s, i, first)
                            value_matmuls(c, pe, s, 4)

                    in_order(first, scores, values)
                    weights(WG, i, first)
                    unit_matmuls(c, pe, 0, 2, XH, XL)
                    pe.wait_ge(v_lo, i + 1)
                    pe.wait_ge(s_lo, i + 1)

                    def weigh(n):
                        t, b = n // B, n % B
                        out = c.PS[:, 4 + 2 * t + b // 4, (b % 4) * T:(b % 4 + 1) * T]
                        cols = slice(b * T, (b + 1) * T)
                        vh, vl = VH[:, b, t * P:(t + 1) * P], VL[:, b, t * P:(t + 1) * P]
                        pe.matmul(out, vh, SH[:, cols], start=True, stop=False)
                        pe.matmul(out, vh, SL[:, cols], start=False, stop=False)
                        mm = pe.matmul(out, vl, SH[:, cols], start=False, stop=True)
                        if n == 2 * B - 1:
                            mm.then_inc(o_raw, 1)

                    def weigh_between(h, k):
                        if h == 0:
                            weigh(2 * k)
                            weigh(2 * k + 1)

                    weights(WG + 1, i, first)
                    unit_matmuls(c, pe, 1, 0, XH, XL, weigh_between)
                    pe.wait_ge(o_sq_sum, i + 1)
                    pe.wait_ge(gated, 2 * i + 1)
                    for h in range(2):
                        mm = pe.matmul(c.PS[:, 2 + h, 0:HALF], c.ONES_DV[:],
                                       SQ[:, 0, h * HALF:(h + 1) * HALF], start=True, stop=True)
                    mm.then_inc(o_var, 1)

                head(0, True)
                with pe.Fori(1, RH) as i:
                    head(i, False)
                project_output(RH, True)
                mean_of(c, pe, T1, r_summed, KT - 1, mean)


class LayerNorm:

    def __init__(self, c, nc, ctx, name, SQ, Y, Z):
        sem = lambda n: ctx.enter_context(nc.semaphore(name + n))
        self.c, self.SQ, self.Y, self.Z = c, SQ, Y, Z
        (self.centred, self.squared, self.sq_used, self.ln, self.rs, self.newton, self.normed,
         self.hi, self.lo) = (sem(n) for n in (
             "centred", "squared", "sq_used", "ln", "rs", "newton", "normed", "hi", "lo"))

    @staticmethod
    def half(ap, h):
        return ap[:, h * HALF:(h + 1) * HALF]

    def tile(self, x, k, h):
        return x[:, k, h * HALF:(h + 1) * HALF]

    def pool(self, pool):
        pool.sem_inc(self.sq_used, 4)

    def tensor(self, pe):
        c = self.c
        for h in range(2):
            for k in range(KT):
                pe.wait_ge(self.squared, KT * h + k + 1)
                pe.matmul(c.PS[:, 4 + h, 0:HALF], c.ONES_D[:], self.SQ[:, k % 4, :],
                          start=(k == 0), stop=(k == KT - 1)).then_inc(self.sq_used, 1)

    def wait_inputs(self, pe, h, k):
        pe.wait_ge(self.lo, KT * h + k + 1)

    def scalar(self, act, split=True):
        c = self.c

        def square(h, k):
            act.wait_ge(self.centred, KT * h + k + 1)
            act.wait_ge(self.sq_used, KT * h + k + 1)
            act.activation(self.SQ[:, k % 4, :], self.tile(c.R, k, h),
                           ACT.Square).then_inc(self.squared, 1)

        def root(h):
            act.wait_ge(self.sq_used, KT * h + KT + 4)
            rsqrt_from(c, act, self.half(self.Y, h), c.PS[:, 4 + h, 0:HALF], c.EPS5[:], self.ln,
                       h + 1).then_inc(self.rs, 1)

        act.preload_act_table_set("natural_log_exp_and_others")
        for k in range(KT):
            square(0, k)
        for k in range(4):
            square(1, k)
        root(0)
        for k in range(4, KT):
            square(1, k)
        for h in range(2):
            for k in range(KT if split else 0):
                if h == 0 and k == 4:
                    root(1)
                act.wait_ge(self.normed, KT * h + k + 1)
                act.activation(self.tile(c.XH, k, h), self.tile(c.R, k, h),
                               ACT.Copy).then_inc(self.hi, 1)
        if not split:
            root(1)

    def vector(self, dve, split=True):
        c = self.c
        for h in range(2):
            for k in range(KT):
                r = self.tile(c.R, k, h)
                dve.tensor_tensor(r, r, c.PS[:, 2 + h, 0:HALF],
                                  ALU.subtract).then_inc(self.centred, 1)

        def low(h, k):
            dve.wait_ge(self.hi, KT * h + k + 1)
            dve.tensor_tensor(self.tile(c.XL, k, h), self.tile(c.R, k, h),
                              self.tile(c.XH, k, h).bitcast(F32),
                              ALU.subtract).then_inc(self.lo, 1)

        for h in range(2):
            y, z, var = self.half(self.Y, h), self.half(self.Z, h), c.PS[:, 4 + h, 0:HALF]
            dve.wait_ge(self.rs, h + 1)
            dve.scalar_tensor_tensor(out=z, in0=var, scalar=c.EPS5[:], in1=y, op0=ALU.add,
                                     op1=ALU.mult).then_inc(self.newton, 1)
            dve.wait_ge(self.newton, 4 * h + 1)
            dve.tensor_tensor(z, z, y, ALU.mult).then_inc(self.newton, 1)
            dve.wait_ge(self.newton, 4 * h + 2)
            dve.tensor_scalar(z, z, -0.5, 1.5, ALU.mult, ALU.add).then_inc(self.newton, 1)
            dve.wait_ge(self.newton, 4 * h + 3)
            dve.tensor_tensor(y, y, z, ALU.mult).then_inc(self.newton, 1)
            dve.wait_ge(self.newton, 4 * h + 4)
            for k in range(KT):
                r = self.tile(c.R, k, h)
                dve.tensor_tensor(r, r, y, ALU.mult).then_inc(self.normed, 1)
                if split and k > 0:
                    low(h, k - 1)
            if split:
                low(h, KT - 1)


def mean_of(c, pe, total, ready, count, done):
    pe.wait_ge(ready, count)
    for h in range(2):
        mm = pe.matmul(c.PS[:, 2 + h, 0:HALF], c.ONES_D[:], LayerNorm.half(total, h), start=True,
                       stop=True)
    mm.then_inc(done, 1)


def phase_result(c, nc):
    with ExitStack() as ctx:
        sb = lambda n, shape, dt=F32: ctx.enter_context(nc.sbuf_tensor("e_" + n, shape, dt))
        norm = LayerNorm(c, nc, ctx, "e_", sb("SQ", [P, 4, HALF]), sb("Y", [P, NT])[:],
                         sb("Z", [P, NT])[:])
        stored = ctx.enter_context(nc.semaphore("e_stored"))
        with nc.Block() as block:
            @block.gpsimd
            def _(pool):
                norm.pool(pool)

            @block.tensor
            def _(pe):
                norm.tensor(pe)

            @block.scalar
            def _(act):
                norm.scalar(act, split=False)

            @block.vector
            def _(dve):
                norm.vector(dve, split=False)

            @block.sync
            def _(sp):
                for h in range(2):
                    for k in range(0, KT, 2):
                        sp.wait_ge(norm.normed, KT * h + k + 2)
                        cols = slice(h * HALF, (h + 1) * HALF)
                        sp.dma_start(c.out[:, k:k + 2, cols],
                                     c.R[:, k:k + 2, cols]).then_inc(stored, 16)
                sp.wait_ge(stored, 16 * KT)


def phase_heads(c, nc):
    HEADS = QH_N + KV_N
    TURNS = HEADS // 4
    with ExitStack() as ctx:
        sb = lambda n, shape, dt=F32: ctx.enter_context(nc.sbuf_tensor("h_" + n, shape, dt))
        sem = lambda n: ctx.enter_context(nc.semaphore("h_" + n))
        T1, T2 = sb("T1", [P, 2, NT]), sb("T2", [P, NT])
        SQ, RS = sb("SQ", [P, NT]), sb("RS", [P, 2, NT])
        SQH, SQL = sb("SQH", [P, NT], F32R), sb("SQL", [P, NT], F32R)
        ONE = sb("ONE", [P, P], F32R)
        squared, sq_hi, sq_lo, taken, var, ln, rs, roped, out = (sem(n) for n in (
            "squared", "sq_hi", "sq_lo", "taken", "var", "ln", "rs", "roped", "out"))
        norm = LayerNorm(c, nc, ctx, "hn_", T1[:].rearrange("p s (h t) -> p (s h) t", h=2),
                         RS[:, 0, :], RS[:, 1, :])
        with nc.Block() as block:
            @block.gpsimd
            def _(pool):
                norm.pool(pool)
                pool.sem_inc(taken, 2)
                pool.sem_inc(ln, 2)
                pool.sem_inc(out, 2)
                pool.sem_inc(sq_lo, 1)
                pool.sem_inc(var, 1)

            @block.sync
            def _(sp):
                weight_stream(c, sp, U_QK // 2 + 2, HEADS // 4)

            @block.tensor
            def _(pe):
                def variance(j, i):
                    pe.wait_ge(sq_lo, 4 * i + (j + 2))
                    pe.wait_ge(ln, 4 * i + (j + 1))
                    for h in range(2):
                        bank = c.PS[:, 4 + 2 * (j % 2) + h, 0:HALF]
                        cols = slice(h * HALF, (h + 1) * HALF)
                        pe.matmul(bank, ONE[:], SQH[:, cols], start=True, stop=False)
                        mm = pe.matmul(bank, ONE[:], SQL[:, cols], start=False, stop=True)
                    mm.then_inc(var, 1)

                norm.tensor(pe)
                def turn(i, first):
                    for j in range(4):
                        pe.wait_ge(taken, 4 * i + (j + 1))
                        pe.wait_ge(c.w_lo, 4 * i + (U_QK + j + 1))
                        unit_matmuls(c, pe, j % 2, 2 * (j % 2), c.XH, c.XL,
                                     (lambda h, k: norm.wait_inputs(pe, h, k))
                                     if j == 0 else None)
                        if not (first and j == 0):
                            variance((j - 1) % 4, i if j > 0 else i - 1)

                turn(0, True)
                with pe.Fori(1, TURNS) as i:
                    turn(i, False)
                variance(3, TURNS - 1)

            @block.scalar
            def _(act):
                def root(j, i):
                    act.wait_ge(var, 4 * i + (j + 2))
                    act.wait_ge(out, 4 * i + (j + 1))
                    rsqrt_from(c, act, halves(RS[:, j % 2, :]), banks2(c, 4 + 2 * (j % 2)),
                               c.EPS6[:], ln, 4 * i + (j + 3)).then_inc(rs, 1)

                act.activation(ONE[:], c.ONES_HD[:], ACT.Copy)
                norm.scalar(act)

                def turn(i, first):
                    for j in range(4):
                        split_hi(c, act, U_QK + j + 2, i, 1)
                        act.wait_ge(sq_lo, 4 * i + (j + 1))
                        act.activation(halves(SQ[:]), banks2(c, 2 * (j % 2)),
                                       ACT.Square).then_inc(squared, 1)
                        act.wait_ge(squared, 4 * i + (j + 1))
                        act.wait_ge(var, 4 * i + (j + 1))
                        act.activation(SQH[:], SQ[:], ACT.Copy).then_inc(sq_hi, 1)
                        if not (first and j == 0):
                            root((j - 1) % 4, i if j > 0 else i - 1)

                turn(0, True)
                with act.Fori(1, TURNS) as i:
                    turn(i, False)
                root(3, TURNS - 1)

            @block.vector
            def _(dve):
                def finish(j, i):
                    dve.wait_ge(roped, 4 * i + (j + 1))
                    dve.wait_ge(rs, 4 * i + (j + 1))
                    dve.tensor_tensor(c.QX[:, ds(4 * NT * i + j * NT, NT)], T1[:, j % 2, :],
                                      RS[:, j % 2, :], ALU.mult).then_inc(out, 1)

                norm.vector(dve)

                def turn(i, first):
                    for j in range(4):
                        split_lo(c, dve, U_QK + j + 2, i, 1)
                        dve.wait_ge(squared, 4 * i + (j + 1))
                        for h in range(2):
                            bank = c.PS[:, 2 * (j % 2) + h, 0:HALF].rearrange(
                                "p (b t) -> p b t", t=T)
                            cols = slice(h * HALF, (h + 1) * HALF)
                            t1 = T1[:, j % 2, cols].rearrange("p (b t) -> p b t", t=T)
                            t2 = T2[:, cols].rearrange("p (b t) -> p b t", t=T)
                            dve.scalar_tensor_tensor(
                                out=t1, in0=bank, scalar=c.NW[:, ds(4 * i + j, 1)],
                                in1=c.COS[:].unsqueeze(1).broadcast_to([P, 4, T]), op0=ALU.mult,
                                op1=ALU.mult)
                            for lo in (0, 64):
                                hi = 64 - lo
                                ins = dve.scalar_tensor_tensor(
                                    out=t2[lo:lo + 64], in0=bank[hi:hi + 64],
                                    scalar=c.NW[lo:lo + 64, ds(4 * i + (HEADS + j), 1)],
                                    in1=c.SIN[lo:lo + 64].unsqueeze(1).broadcast_to([64, 4, T]),
                                    op0=ALU.mult, op1=ALU.mult)
                        ins.then_inc(taken, 1)
                        dve.wait_ge(taken, 4 * i + (j + 3))
                        dve.tensor_tensor(T1[:, j % 2, :], T1[:, j % 2, :], T2[:],
                                          ALU.add).then_inc(roped, 1)
                        dve.wait_ge(sq_hi, 4 * i + (j + 1))
                        dve.tensor_tensor(SQL[:], SQ[:], SQH[:].bitcast(F32),
                                          ALU.subtract).then_inc(sq_lo, 1)
                        if first and j == 0:
                            dve.wait_ge(roped, 1)
                        else:
                            finish((j - 1) % 4, i if j > 0 else i - 1)
                            dve.wait_ge(out, 4 * i + (j + 2))

                turn(0, True)
                with dve.Fori(1, TURNS) as i:
                    turn(i, False)
                finish(3, TURNS - 1)


def phase_self_kv(c, nc):
    with ExitStack() as ctx:
        sem = lambda n: ctx.enter_context(nc.semaphore("s_" + n))
        VT = ctx.enter_context(nc.sbuf_tensor("VT", [T, 2, B, 2 * HD], F32))
        copied, stored = sem("copied"), c.kv_stored
        with nc.Block() as block:
            @block.sync
            def _(sp):
                for v in range(KV_N):
                    sp.dma_start(c.kscr[:, v, :, CTX:KEYS].rearrange("b p t -> p b t"),
                                 c.QX[:, (QH_N + v) * NT:(QH_N + v + 1) * NT]
                                 .rearrange("p (b t) -> p b t", t=T)).then_inc(stored, 16)
                sp.wait_ge(stored, 16 * KV_N)
                sp.dma_start(c.KRAW[:], c.kscr[0, 0]).then_inc(c.k_in, 16)
                weight_stream(c, sp, U_V // 2 + 2, 1)
                for m in range(2):
                    sp.wait_ge(copied, m + 1)
                    for v in range(2):
                        for lo, hi, chunk, row in ((0, P - SELF_P, SELF_C, SELF_P),
                                                   (P - SELF_P, T, SELF_C + 1, 0)):
                            sp.dma_start(
                                c.vscr[:, 2 * m + v, row:row + hi - lo, chunk, :]
                                .rearrange("b p d -> p b d"),
                                VT[lo:hi, m, :, v * HD:(v + 1) * HD]).then_inc(stored, 16)

            @block.tensor
            def _(pe):
                for m in range(2):
                    for s in range(2):
                        pe.wait_ge(c.w_lo, U_V + 2 * m + s + 1)
                        value_matmuls(c, pe, s, 4 * m)

            @block.scalar
            def _(act):
                for j in range(4):
                    split_hi(c, act, U_V + j + 2)

            @block.vector
            def _(dve):
                for m in range(2):
                    split_lo(c, dve, U_V + 2 * m + 2)
                    split_lo(c, dve, U_V + 2 * m + 3)
                    dve.wait_ge(c.unit_done, U_V + 2 * m + 2 - U_RET)
                    dve.tensor_copy(VT[:, m].rearrange("p (g b) n -> p g (b n)", b=2),
                                    c.PS[0:T, 4 * m:4 * m + 4, :]).then_inc(copied, 1)


def phase_attention(c, nc):
    with ExitStack() as ctx:
        sb = lambda n, shape, dt=F32: ctx.enter_context(nc.sbuf_tensor("a_" + n, shape, dt))
        sem = lambda n: ctx.enter_context(nc.semaphore("a_" + n))
        GT = GRP * T
        KRAW, VRAW, E = c.KRAW, sb("VRAW", [P, KC, HD]), sb("E", [P, RING, GT])
        IV, CV, DG = sb("IV", [P, GT]), sb("CV", [P, GT]), sb("DG", [T, 2, GT], F32R)
        at = [0]

        def room(*shape):
            n = int(np.prod(shape))
            dims = "abc"[:len(shape)]
            views = [x[:].rearrange("p k t -> p (k t)")[:, at[0]:at[0] + n].rearrange(
                f"p ({' '.join(dims)}) -> p {' '.join(dims)}",
                **dict(zip(dims, shape))) for x in (c.XH, c.XL)]
            at[0] += n
            return views

        KHL = room(2, KEYS)
        VHL = room(2, KC * HD)
        EHL = room(KC, GT)
        QHL = [sb("QH", [P, 2, GT], F32R), sb("QL", [P, 2, GT], F32R)]
        MX = sb("MX", [T, 2])
        MASK, ID4 = sb("MASK", [T, SELF_P + T], F32R), sb("ID4", [T, GT], F32R)
        NEG, ONE = sb("NEG", [T, P], F32R), sb("ONE", [P, P], F32R)
        k_in = c.k_in
        (v_in, tables, k_hi, k_lo, v_hi, v_lo, q_hi, q_lo, m_raw, maxed, diag, s_raw,
         exped, e_hi, e_lo, weighed, ln, inverted, newton, o_out, zeroed) = (sem(n) for n in (
             "v_in", "tables", "k_hi", "k_lo", "v_hi", "v_lo", "q_hi", "q_lo", "m_raw",
             "maxed", "diag", "s_raw", "exped", "e_hi", "e_lo", "weighed", "ln", "inverted",
             "newton", "o_out", "zeroed"))
        SCALE = float(HD) ** -0.5
        qx = c.QX[:].rearrange("p (h n) -> p h n", n=NT)
        rows = [P] * (KC - 1) + [LASTC]
        MAXIMA_AT = (1, 2, 4, 5)
        KEYS_AT, VALUES_AT = 0, 4
        OUTPUT_AT = 2

        def query_view(b, v):
            return qx[:, GRP * v:GRP * (v + 1), ds(b * T, T)]

        def heads(ap):
            return ap.rearrange("p (h t) -> p h t", h=GRP)

        def after(b, v, last):
            if v + 1 < KV_N:
                return b, v + 1
            return None if last else (b + 1, 0)

        def before(b, v, first):
            if v > 0:
                return b, v - 1
            return None if first else (b - 1, KV_N - 1)

        def chunk_no(b, v, k):
            return KV_N * KC * b, KC * v + k

        def every_batch(eng, body):
            body(0, True, False)
            with eng.Fori(1, B - 1) as b:
                body(b, False, False)
            body(B - 1, False, True)

        with nc.Block() as block:
            @block.gpsimd
            def _(pool):
                pool.wait_ge(c.kv_stored, 16 * (KV_N + 8))
                pool.memset(VRAW[:, KC - 1, :], 0.0).then_inc(zeroed, 1)
                pool.sem_inc(k_lo, 1)
                pool.sem_inc(v_lo, 1)
                pool.sem_inc(maxed, 2)
                pool.sem_inc(diag, 2)
                pool.sem_inc(exped, RING)
                pool.sem_inc(e_lo, RING)
                pool.sem_inc(weighed, KC)
                pool.sem_inc(o_out, 1)

                def values_lo(b, v):
                    pool.wait_ge(v_hi, 4 * b + (v + 1))
                    pool.tensor_tensor(VHL[1][:, v % 2, :], VRAW[:].rearrange("p k d -> p (k d)"),
                                       VHL[0][:, v % 2, :].bitcast(F32),
                                       ALU.subtract).then_inc(v_lo, 1)

                def diagonal(b, v, j):
                    pool.wait_ge(maxed, 16 * b + (4 * v + j + 3))
                    pool.tensor_tensor(DG[:, v % 2, j * T:(j + 1) * T], c.ID[0:T, 0:T],
                                       MX[:, j % 2:j % 2 + 1].broadcast_to([T, T]),
                                       ALU.mult).then_inc(diag, 1)

                def body(b, first, last):
                    for v in range(KV_N):
                        if (nxt := after(b, v, last)) is not None:
                            for j in range(GRP):
                                diagonal(*nxt, j)
                            values_lo(*nxt)

                for j in range(GRP):
                    diagonal(0, 0, j)
                values_lo(0, 0)
                every_batch(pool, body)

            @block.sync
            def _(sp):
                sp.wait_ge(zeroed, 1)
                sp.wait_ge(c.kv_stored, 16 * (KV_N + 8))

                def body(b, first, last):
                    for v in range(KV_N):
                        if not (first and v == 0):
                            sp.wait_ge(k_lo, 4 * b + (v + 1))
                            sp.dma_start(KRAW[:], c.kscr[ds(b, 1), v]
                                         .rearrange("a p t -> (a p) t")).then_inc(k_in, 16)
                        sp.wait_ge(v_lo, 4 * b + (v + 1))
                        sp.dma_start(VRAW[:, 0:KC - 1, :], c.vscr[ds(b, 1), v, :, 0:KC - 1, :]
                                     .rearrange("a p k d -> (a p) k d")).then_inc(v_in, 16)
                        sp.dma_start(VRAW[0:LASTC, KC - 1, :],
                                     c.vscr[ds(b, 1), v, 0:LASTC, KC - 1, :]
                                     .rearrange("a p d -> (a p) d")).then_inc(v_in, 16)

                every_batch(sp, body)

            @block.tensor
            def _(pe):
                def maxima_scores(b, v, j):
                    if j == 0:
                        pe.wait_ge(q_hi, 4 * b + (v + 1))
                    pe.wait_ge(maxed, 16 * b + (4 * v + j + 1))
                    q, s = QHL[0][:, v % 2, j * T:(j + 1) * T], 2 * (j % 2)
                    pe.matmul(c.PS[0:T, s, 0:KEY_A], q, KHL[0][:, v % 2, 0:KEY_A], start=True,
                              stop=True)
                    pe.matmul(c.PS[0:T, s + 1, 0:KEY_A], q, KHL[0][:, v % 2, KEYS - KEY_A:KEYS],
                              start=True, stop=False, skip_group_check=True)
                    pe.matmul(c.PS[0:T, s + 1, KEY_A - T:KEY_A], ID4[:, 0:T],
                              MASK[:, SELF_P:SELF_P + T], start=False, stop=True,
                              skip_group_check=True).then_inc(m_raw, 1)

                def scores(b, v, k):
                    n, at = chunk_no(b, v, k)
                    out = c.PS[0:rows[k], 4 + at % 2, 0:GT]
                    kh, kl = (x[:, v % 2, k * P:k * P + rows[k]] for x in KHL)
                    qh, ql = (x[:, v % 2, :] for x in QHL)
                    pe.wait_ge(exped, n + (at + 1 + RING - 2))
                    if k == 0:
                        pe.wait_ge(q_lo, 4 * b + (v + 1))
                    pe.matmul(out, kh, qh, start=True, stop=False)
                    pe.matmul(out, kh, ql, start=False, stop=False)
                    pe.matmul(out, kl, qh, start=False, stop=False)
                    if k >= SELF_C:
                        m0 = (k - SELF_C) * P
                        pe.matmul(out, MASK[:, m0:m0 + rows[k]], ID4[:], start=False, stop=False)
                    if k == 0:
                        pe.wait_ge(diag, 16 * b + (4 * v + 4 + 2))
                    pe.matmul(out, NEG[:, 0:rows[k]], DG[:, v % 2, :], start=False,
                              stop=True).then_inc(s_raw, 1)

                def weigh(b, v, k):
                    n, at = chunk_no(b, v, k)
                    pe.wait_ge(e_lo, n + (at + 1 + RING))
                    if k == 0:
                        pe.wait_ge(v_lo, 4 * b + (v + 2))
                        pe.wait_ge(o_out, 4 * b + (v + 1))
                    r = rows[k]
                    vh, vl = (x[0:r, v % 2, k * HD:(k + 1) * HD] for x in VHL)
                    eh, el = (x[0:r, k, :] for x in EHL)
                    out, total = c.PS[:, 6, 0:GT], c.PS[:, 7, 0:GT]
                    pe.matmul(out, vh, eh, start=(k == 0), stop=False)
                    pe.matmul(out, vh, el, start=False, stop=False)
                    pe.matmul(out, vl, eh, start=False, stop=(k == KC - 1))
                    pe.matmul(total, ONE[0:r, :], eh, start=(k == 0), stop=False)
                    pe.matmul(total, ONE[0:r, :], el, start=False,
                              stop=(k == KC - 1)).then_inc(weighed, 1)

                WEIGHED_OF_LAST = {0: (3, 4), 1: (5,), 2: (6,)}
                WEIGHED_OF_OWN = {5: (0, 1), 6: (2,)}

                def body(b, first, last):
                    for v in range(KV_N):
                        nxt, prev = after(b, v, last), before(b, v, first)
                        for k in range(KC):
                            scores(b, v, k)
                            for w in WEIGHED_OF_LAST.get(k, ()) if prev is not None else ():
                                weigh(*prev, w)
                            for w in WEIGHED_OF_OWN.get(k, ()):
                                weigh(b, v, w)
                            if k in MAXIMA_AT and nxt is not None:
                                maxima_scores(*nxt, MAXIMA_AT.index(k))

                pe.wait_ge(tables, 4)
                for j in range(GRP):
                    maxima_scores(0, 0, j)
                every_batch(pe, body)
                for k in range(3, KC):
                    weigh(B - 1, KV_N - 1, k)

            @block.scalar
            def _(act):
                def keys_hi(b, v):
                    act.wait_ge(k_in, 64 * b + 16 * (v + 1))
                    act.activation(KHL[0][:, v % 2, :], KRAW[:], ACT.Copy).then_inc(k_hi, 1)
                    act.activation(heads(QHL[0][:, v % 2, :]), query_view(b, v),
                                   ACT.Copy).then_inc(q_hi, 1)

                def values_hi(b, v):
                    act.wait_ge(v_in, 128 * b + 32 * (v + 1))
                    act.activation(VHL[0][:, v % 2, :], VRAW[:].rearrange("p k d -> p (k d)"),
                                   ACT.Copy).then_inc(v_hi, 1)

                def exponentials(b, v, k):
                    n, at = chunk_no(b, v, k)
                    r = rows[k]
                    act.wait_ge(s_raw, n + (at + 1))
                    act.wait_ge(e_lo, n + (at + 1))
                    act.activation(E[0:r, at % RING, :], c.PS[0:r, 4 + at % 2, 0:GT], ACT.Exp,
                                   scale=SCALE).then_inc(exped, 1)
                    act.wait_ge(exped, n + (at + 1 + RING))
                    act.wait_ge(weighed, n + (at + 1))
                    act.activation(EHL[0][0:r, k, :], E[0:r, at % RING, :],
                                   ACT.Copy).then_inc(e_hi, 1)

                def inverse(b, v):
                    act.wait_ge(weighed, 28 * b + (KC * v + 2 * KC))
                    act.wait_ge(o_out, 4 * b + (v + 1))
                    act.activation(IV[:], c.PS[:, 7, 0:GT], ACT.Ln).then_inc(ln, 1)
                    act.wait_ge(ln, 4 * b + (v + 1))
                    act.activation(IV[:], IV[:], ACT.Exp, scale=-1.0).then_inc(inverted, 1)

                def body(b, first, last):
                    for v in range(KV_N):
                        nxt, prev = after(b, v, last), before(b, v, first)
                        for k in range(KC):
                            if k == 0 and nxt is not None:
                                keys_hi(*nxt)
                            exponentials(b, v, k)
                            if k == 2 and prev is not None:
                                inverse(*prev)
                            if k == VALUES_AT and nxt is not None:
                                values_hi(*nxt)

                act.activation(MASK[:], c.CMASK[:], ACT.Copy).then_inc(tables, 1)
                act.activation(heads(ID4[:]), c.ID[0:T, 0:T].unsqueeze(1)
                               .broadcast_to([T, GRP, T]), ACT.Copy).then_inc(tables, 1)
                act.activation(NEG[:], c.ONES[0:T, :], ACT.Copy, scale=-1.0).then_inc(tables, 1)
                act.activation(ONE[:], c.ONES[:], ACT.Copy).then_inc(tables, 1)
                keys_hi(0, 0)
                values_hi(0, 0)
                every_batch(act, body)
                inverse(B - 1, KV_N - 1)

            @block.vector
            def _(dve):
                def keys_lo(b, v):
                    dve.wait_ge(k_hi, 4 * b + (v + 1))
                    dve.tensor_tensor(KHL[1][:, v % 2, :], KRAW[:],
                                      KHL[0][:, v % 2, :].bitcast(F32),
                                      ALU.subtract).then_inc(k_lo, 1)
                    dve.wait_ge(q_hi, 4 * b + (v + 1))
                    dve.tensor_tensor(heads(QHL[1][:, v % 2, :]), query_view(b, v),
                                      heads(QHL[0][:, v % 2, :].bitcast(F32)),
                                      ALU.subtract).then_inc(q_lo, 1)

                def maximum(b, v, j):
                    dve.wait_ge(m_raw, 16 * b + (4 * v + j + 1))
                    dve.wait_ge(diag, 16 * b + (4 * v + j + 1))
                    dve.tensor_reduce(MX[:, j % 2:j % 2 + 1], c.PS[0:T, 2 * (j % 2):2 * (j % 2) + 2, 0:KEY_A], AX.XY,
                                      ALU.max).then_inc(maxed, 1)

                def exponentials_lo(b, v, k):
                    n, at = chunk_no(b, v, k)
                    r = rows[k]
                    dve.wait_ge(e_hi, n + (at + 1))
                    dve.tensor_tensor(EHL[1][0:r, k, :], E[0:r, at % RING, :],
                                      EHL[0][0:r, k, :].bitcast(F32),
                                      ALU.subtract).then_inc(e_lo, 1)

                def output(b, v):
                    dve.wait_ge(inverted, 4 * b + (v + 1))
                    dve.tensor_tensor(CV[:], c.PS[:, 7, 0:GT], IV[:], ALU.mult).then_inc(newton, 1)
                    dve.wait_ge(newton, 8 * b + (2 * v + 1))
                    dve.scalar_tensor_tensor(out=CV[:], in0=CV[:], scalar=2.0, in1=IV[:],
                                             op0=ALU.subtract, op1=ALU.mult).then_inc(newton, 1)
                    dve.wait_ge(newton, 8 * b + (2 * v + 2))
                    dve.scalar_tensor_tensor(out=query_view(b, v), in0=heads(c.PS[:, 6, 0:GT]),
                                             scalar=-1.0, in1=heads(CV[:]), op0=ALU.mult,
                                             op1=ALU.mult).then_inc(o_out, 1)

                def body(b, first, last):
                    for v in range(KV_N):
                        nxt, prev = after(b, v, last), before(b, v, first)
                        for k in range(KC):
                            if k in MAXIMA_AT and nxt is not None:
                                maximum(*nxt, MAXIMA_AT.index(k))
                            if k == OUTPUT_AT and prev is not None:
                                output(*prev)
                            exponentials_lo(b, v, k)
                            if k == KEYS_AT and nxt is not None:
                                keys_lo(*nxt)

                keys_lo(0, 0)
                for j in range(GRP):
                    maximum(0, 0, j)
                every_batch(dve, body)
                output(B - 1, KV_N - 1)


def phase_attention_out(c, nc):
    with ExitStack() as ctx:
        sem = lambda n: ctx.enter_context(nc.semaphore("w_" + n))
        x_hi, x_lo, added, summed, mean = (sem(n) for n in (
            "x_hi", "x_lo", "added", "summed", "mean"))
        SUM = ctx.enter_context(nc.sbuf_tensor("w_SUM", [P, NT], F32))
        qx = c.QX[:].rearrange("p (h n) -> p h n", n=NT)
        with nc.Block() as block:
            @block.gpsimd
            def _(pool):
                pool.sem_inc(added, 4)
                pool.memset(SUM[:], 0.0).then_inc(summed, 1)

            @block.sync
            def _(sp):
                weight_stream(c, sp, U_WO // 2 + 2, 4)

            @block.tensor
            def _(pe):
                for g in range(2):
                    with pe.Fori(0, 2) as q:
                        for j in range(4):
                            pe.wait_ge(added, 4 * q + (8 * g + j + 1))
                            pe.wait_ge(c.w_lo, 4 * q + (U_WO + 8 * g + j + 1))
                            unit_matmuls(c, pe, j % 2, 2 * j, c.XH, c.XL,
                                         (lambda h, k: pe.wait_ge(x_lo, 8 * g + k + 1))
                                         if j == 0 else None, k_first=(j == 0))
                mean_of(c, pe, SUM, summed, KT + 1, mean)

            @block.scalar
            def _(act):
                for g in range(2):
                    if g == 1:
                        act.wait_ge(c.unit_done, U_WO + 8 - U_RET)
                    for k in range(KT):
                        act.activation(c.XH[:, k, :], qx[:, 8 * g + k, :],
                                       ACT.Copy).then_inc(x_hi, 1)
                    with act.Fori(0, 2) as q:
                        for j in range(4):
                            split_hi(c, act, U_WO + 8 * g + j + 2, q, 1)

            @block.vector
            def _(dve):
                for g in range(2):
                    for k in range(KT):
                        dve.wait_ge(x_hi, 8 * g + k + 1)
                        dve.tensor_tensor(c.XL[:, k, :], qx[:, 8 * g + k, :],
                                          c.XH[:, k, :].bitcast(F32),
                                          ALU.subtract).then_inc(x_lo, 1)
                    with dve.Fori(0, 2) as q:
                        for j in range(4):
                            split_lo(c, dve, U_WO + 8 * g + j + 2, q, 1)
                            dve.wait_ge(c.unit_done, 4 * q + (U_WO + 8 * g + j + 1 - U_RET))
                            r = c.R[:, ds(4 * q + j, 1), :].rearrange(
                                "p a (h t) -> p (a h) t", h=2)
                            dve.tensor_tensor(r, r, banks2(c, 2 * j),
                                              ALU.add).then_inc(added, 1)
                            if g == 1:
                                dve.wait_ge(added, 4 * q + (8 + j + 1 + 4))
                                dve.wait_ge(summed, 4 * q + (j + 1))
                                dve.tensor_tensor(
                                    SUM[:], SUM[:], c.R[:, ds(4 * q + j, 1), :]
                                    .rearrange("p a t -> p (a t)"), ALU.add).then_inc(summed, 1)


def phase_ffn(c, nc):
    PER = 24
    with ExitStack() as ctx:
        sb = lambda n, shape, dt=F32: ctx.enter_context(nc.sbuf_tensor("f_" + n, shape, dt))
        sem = lambda n: ctx.enter_context(nc.semaphore("f_" + n))
        HH, HL = sb("HH", [P, KT, NT], F32R), sb("HL", [P, KT, NT], F32R)
        G, HF = sb("G", [P, NT]), sb("HF", [P, NT])
        gated, freed, h_hi, h_lo, summed, mean = (sem(n) for n in (
            "gated", "freed", "h_hi", "h_lo", "summed", "mean"))
        SUM = sb("SUM", [P, NT])
        norm = LayerNorm(c, nc, ctx, "fn_", sb("SQ", [P, 4, HALF]), sb("Y", [P, NT])[:],
                         sb("Z", [P, NT])[:])
        with nc.Block() as block:
            @block.gpsimd
            def _(pool):
                norm.pool(pool)
                pool.memset(SUM[:], 0.0).then_inc(summed, 1)
                pool.sem_inc(freed, 4)

            @block.sync
            def _(sp):
                weight_stream(c, sp, U_FFN // 2 + 2, (PAIRS - U_FFN // 2 - 2) // 2)
                sp.wait_ge(c.w_lo, 2 * PAIRS - 2)
                sp.dma_start(c.RAW[:, 0, :], c.weights[PAIRS - 1]).then_inc(c.raw[0], 16)

            @block.tensor
            def _(pe):
                def unit(t, m, j, off, xh, xl, before=None, k_first=False):
                    pe.wait_ge(freed, PER * t + 4 * m + (off + j + 1))
                    pe.wait_ge(c.w_lo, PER * t + 4 * m + (U_FFN + off + j + 1))
                    unit_matmuls(c, pe, j % 2, 2 * j, xh, xl, before, k_first)

                norm.tensor(pe)
                with pe.Fori(0, CHUNKS) as t:
                    with pe.Fori(0, 4) as m:
                        for j in range(4):
                            unit(t, m, j, 0, c.XH, c.XL,
                                 (lambda h, k: norm.wait_inputs(pe, h, k)) if j == 0 else None)
                    with pe.Fori(0, 2) as m:
                        for j in range(4):
                            unit(t, m, j, 16, HH, HL,
                                 (lambda h, k: pe.wait_ge(h_lo, 8 * t + (k + 1)))
                                 if j == 0 else None, k_first=(j == 0))
                mean_of(c, pe, SUM, summed, KT + 1, mean)

            @block.scalar
            def _(act):
                norm.scalar(act)
                with act.Fori(0, CHUNKS) as t:
                    for m in range(4):
                        for e in range(2):
                            split_ahead_hi(c, act, 2 * e, t, m, 0)
                            act.activation(halves(G[:]), banks2(c, 4 * e),
                                           ACT.Silu).then_inc(gated, 1)
                            split_ahead_hi(c, act, 2 * e + 1, t, m, 0)
                            act.wait_ge(freed, PER * t + 4 * m + (2 * e + 2 + 4))
                            act.activation(HH[:, 2 * m + e, :], HF[:],
                                           ACT.Copy).then_inc(h_hi, 1)
                    with act.Fori(0, 2) as m:
                        for j in range(4):
                            split_ahead_hi(c, act, j, t, m, 16)

            @block.vector
            def _(dve):
                def turn(t, last):
                    with dve.Fori(0, 4) as m:
                        for e in range(2):
                            split_ahead_lo(c, dve, 2 * e, t, m, 0)
                            split_ahead_lo(c, dve, 2 * e + 1, t, m, 0)
                            dve.wait_ge(gated, 8 * t + 2 * m + (e + 1))
                            dve.wait_ge(c.unit_done,
                                        PER * t + 4 * m + (U_FFN + 2 * e + 2 - U_RET))
                            dve.tensor_tensor(halves(HF[:]), banks2(c, 4 * e + 2),
                                              halves(G[:]), ALU.mult).then_inc(freed, 2)
                            dve.wait_ge(h_hi, 8 * t + 2 * m + (e + 1))
                            dve.tensor_tensor(
                                HL[:, ds(2 * m + e, 1), :].rearrange("p a t -> p (a t)"), HF[:],
                                HH[:, ds(2 * m + e, 1), :].rearrange("p a t -> p (a t)")
                                .bitcast(F32), ALU.subtract).then_inc(h_lo, 1)
                            dve.wait_ge(h_lo, 8 * t + 2 * m + (e + 1))
                    with dve.Fori(0, 2) as m:
                        for j in range(4):
                            split_ahead_lo(c, dve, j, t, m, 16)
                            dve.wait_ge(c.unit_done,
                                        PER * t + 4 * m + (U_FFN + 16 + j + 1 - U_RET))
                            r = c.R[:, ds(4 * m + j, 1), :].rearrange(
                                "p a (h t) -> p (a h) t", h=2)
                            dve.tensor_tensor(r, r, banks2(c, 2 * j),
                                              ALU.add).then_inc(freed, 1)
                            if last:
                                dve.wait_ge(freed, PER * t + 4 * m + (16 + j + 1 + 4))
                                dve.wait_ge(summed, 4 * m + (j + 1))
                                dve.tensor_tensor(
                                    SUM[:], SUM[:], c.R[:, ds(4 * m + j, 1), :]
                                    .rearrange("p a t -> p (a t)"), ALU.add).then_inc(summed, 1)

                norm.vector(dve)
                with dve.Fori(0, CHUNKS - 1) as t:
                    turn(t, False)
                turn(CHUNKS - 1, True)


def split_ahead_hi(c, act, j, t, m, off):
    u = U_FFN + off + j + 2
    act.wait_ge(c.raw[(u // 2) % 2], 96 * t + 16 * m + 16 * (u // 4 + 1))
    act.wait_ge(c.unit_done, 24 * t + 4 * m + (u - U_RET - 1))
    act.activation(c.WH[:, u % 2, :], raw_unit(c, u), ACT.Copy).then_inc(c.w_hi, 1)


def split_ahead_lo(c, dve, j, t, m, off):
    u = U_FFN + off + j + 2
    dve.wait_ge(c.w_hi, 24 * t + 4 * m + (u + 1))
    dve.tensor_tensor(c.WL[:, u % 2, :], raw_unit(c, u), c.WH[:, u % 2, :].bitcast(F32),
                      ALU.subtract).then_inc(c.w_lo, 1)


def decoder_layer(nc, c):
    with ExitStack() as ctx:
        sb = lambda n, shape, dt=F32: ctx.enter_context(nc.sbuf_tensor(n, shape, dt))
        sem = lambda n: ctx.enter_context(nc.semaphore(n))
        c.PS = ctx.enter_context(nc.psum_tensor("PS", [P, 8, 512], F32))
        c.RAW = sb("RAW", [P, 2, 2 * UNIT])
        c.WH, c.WL = sb("WH", [P, 2, UNIT], F32R), sb("WL", [P, 2, UNIT], F32R)
        c.COS, c.SIN = sb("COS", [P, T]), sb("SIN", [P, T])
        c.ID = sb("ID", [P, P])
        c.CMASK = sb("CMASK", [T, SELF_P + T])
        c.NW = sb("NW", [P, 2 * (QH_N + KV_N)])
        c.ONES_D, c.ONES_DV, c.ONES_HD = (sb(n, [P, P]) for n in ("ONES_D", "ONES_DV", "ONES_HD"))
        c.ONES = sb("ONES", [P, P])
        c.EPS5, c.EPS6 = sb("EPS5", [P, 1]), sb("EPS6", [P, 1])
        c.raw = [sem("raw0"), sem("raw1")]
        c.w_hi, c.w_lo, c.unit_done = sem("w_hi"), sem("w_lo"), sem("unit_done")
        c.const_in = sem("const_in")
        c.x_in = [sem(f"x_in{k}") for k in range(KT)]
        c.R = sb("R", [P, KT, NT])
        phase_constants(c, nc)
        phase_context(c, nc)
        c.XH, c.XL = sb("XH", [P, KT, NT], F32R), sb("XL", [P, KT, NT], F32R)
        phase_retention(c, nc)
        with ExitStack() as attention:
            c.QX = attention.enter_context(nc.sbuf_tensor("QX", [P, (QH_N + KV_N) * NT], F32))
            phase_heads(c, nc)
            c.KRAW = attention.enter_context(nc.sbuf_tensor("a_KRAW", [P, KEYS], F32))
            c.k_in = attention.enter_context(nc.semaphore("a_k_in"))
            c.kv_stored = attention.enter_context(nc.semaphore("kv_stored"))
            phase_self_kv(c, nc)
            phase_attention(c, nc)
            phase_attention_out(c, nc)
        phase_ffn(c, nc)
        phase_result(c, nc)


def _tables():
    inv = np.float32(1.0) / np.float32(10000.0) ** (np.arange(0, HD, 2, dtype=np.float32)
                                                    / np.float32(HD))
    angle = np.arange(T, dtype=np.float32)[:, None] * inv[None, :]
    cos, sin = np.cos(angle).T, np.sin(angle).T
    gamma = np.float32(1.0) - np.exp2(-5.0 - np.arange(RH, dtype=np.float32)).astype(np.float32)
    diff = np.arange(T)[None, :] - np.arange(T)[:, None]
    power = np.exp2(np.log2(gamma.astype(np.float64))[None, :, None]
                    * np.maximum(diff, 0)[:, None, :])
    decay = np.where(diff[:, None, :] >= 0, power * float(HD) ** -0.5, 0.0)
    future = np.arange(T)[None, :] > np.arange(T)[:, None]
    f = lambda a: np.ascontiguousarray(a, dtype=np.float32)
    return {"cos": f(np.concatenate([cos, cos])), "sin": f(np.concatenate([-sin, sin])),
            "decay": f(decay), "cmask": f(np.pad(np.where(future, -1e30, 0.0), ((0, 0), (SELF_P, 0)))), "ident": f(np.eye(P))}


def _unit(w, n0):
    return w[:, n0:n0 + P].reshape(KT, P, P).transpose(1, 0, 2).reshape(P, UNIT)


def _values(w, n0, n):
    return w[:, n0:n0 + n].reshape(KT, P, n).transpose(1, 0, 2).reshape(P, KT * n)


def _pack_weights(a):
    out = np.empty((PAIRS, P, 2 * UNIT), np.float32)
    at = [0]

    def put(*parts):
        for x in parts:
            for m in range(0, x.shape[1], UNIT):
                out[at[0] // 2, :, (at[0] % 2) * UNIT:(at[0] % 2 + 1) * UNIT] = x[:, m:m + UNIT]
                at[0] += 1

    put(*(_unit(a["L0_xattn_wk_ctx"], v * HD) for v in range(KV_N)))
    put(_values(a["L0_xattn_wv_ctx"], 0, KV_N * HD))
    for h in range(RH + 1):
        if h < RH:
            put(_unit(a["L0_attn_Wq"], h * P), _unit(a["L0_attn_Wk"], h * P))
        if h > 0:
            put(a["L0_attn_Wo"][(h - 1) * RDV:h * RDV].reshape(2, P, KT, P).transpose(1, 2, 0, 3)
                .reshape(P, 2 * UNIT))
        if h < RH:
            put(_values(a["L0_attn_Wv"], h * RDV, RDV))
            put(_unit(a["L0_attn_Wg"], h * RDV), _unit(a["L0_attn_Wg"], h * RDV + P))
    put(*(_unit(a["L0_xattn_wq"], h * HD) for h in range(QH_N)))
    put(*(_unit(a["L0_xattn_wk"], v * HD) for v in range(KV_N)))
    put(*(_values(a["L0_xattn_wv"], m * 2 * HD, 2 * HD) for m in range(2)))
    for g in range(2):
        put(*(_unit(a["L0_xattn_wo"][g * D:(g + 1) * D], n * P) for n in range(KT)))
    gate, up, down = (a[f"L0_ffn_w_{n}"].T for n in ("gate", "up", "down"))
    for t in range(CHUNKS):
        for k in range(KT):
            put(_unit(gate, t * D + k * P), _unit(up, t * D + k * P))
        put(*(_unit(down[t * D:(t + 1) * D], n * P) for n in range(KT)))
    return out


def kernel(**inputs):
    import concourse.bacc as bacc
    from concourse.bass_utils import run_bass_kernel_spmd

    a = {k: np.asarray(v) for k, v in inputs.items()}
    qw, kw = a["L0_xattn_q_norm_w"], a["L0_xattn_k_norm_w"]
    turn = lambda w: np.concatenate([w[HD // 2:], w[:HD // 2]])
    arrays = {
        "weights": _pack_weights(a),
        "x": np.ascontiguousarray(a["x"].reshape(NT, KT, P).transpose(2, 1, 0)),
        "context": np.ascontiguousarray(
            a["ctx_2048"].reshape(B, CTX, KT, P).transpose(0, 3, 2, 1)),
        "gnw": np.ascontiguousarray(a["L0_attn_g_norm_weight"].reshape(2, P).T),
        "nw": np.stack([qw] * QH_N + [kw] * KV_N + [turn(qw)] * QH_N + [turn(kw)] * KV_N, 1),
        **_tables(),
    }
    nc = bacc.Bacc("TRN2", target_bir_lowering=False, num_devices=1)
    c = Core()
    for name, array in arrays.items():
        handle = nc.dram_tensor(name + "_dram", array.shape, F32, kind="ExternalInput")
        c.__dict__[name] = handle.ap()
    c.out = nc.dram_tensor("out_dram", (P, KT, NT), F32, kind="ExternalOutput").ap()
    c.kscr = nc.dram_tensor("keys_scratch", (B, KV_N, P, KEYS), F32, kind="Internal").ap()
    c.vscr = nc.dram_tensor("values_scratch", (B, KV_N, P, KC, HD), F32, kind="Internal").ap()
    decoder_layer(nc, c)
    r = run_bass_kernel_spmd(nc, [{k + "_dram": v for k, v in arrays.items()}], core_ids=[0])
    return r.results[0]["out_dram"].transpose(2, 1, 0).reshape(B, T, D)
```
